# Optimizing a Trainium2 kernel written in Bass

```python
import numpy as np
import jax
import jax.numpy as jnp

def _softmax(x, axis=-1):
    return jax.nn.softmax(x, axis=axis)

def _gelu(x):
    return jax.nn.gelu(x, approximate=True)

def _silu(x):
    return jax.nn.silu(x)

def _sigmoid(x):
    return jax.nn.sigmoid(x)

def _layernorm(x, axis=-1, eps=1e-05):
    m = jnp.mean(x, axis=axis, keepdims=True)
    v = jnp.var(x, axis=axis, keepdims=True)
    return (x - m) / jnp.sqrt(v + eps)

def _scatter_add(tgt, idx, src, axis=0):
    return tgt.at[idx].add(src)

def _segment_sum(src, seg, n):
    return jax.ops.segment_sum(src, seg, n)
kernel_name = 'mk_prb_d1_jaxref_r8_d39e0a'

def setup_inputs(seed: int=0):
    np.random.seed(seed)
    _w = jnp.asarray

    def _L0_attn_setup():
        import jax, jax.numpy as jnp
        import numpy as np
        NUM_BUCKETS = 63

        def _rp_bucket(N):
            rel = jnp.arange(N)[None, :] - jnp.arange(N)[:, None]
            half = NUM_BUCKETS // 2
            return (jnp.clip(rel, -half, half) + half).astype(jnp.int32)
        key = jax.random.key(seed)
        ks = jax.random.split(key, 7)
        B, N, C, H = (4, 128, 128, 16)
        hd = C // H
        g = lambda k, shp, sc: jax.random.normal(k, shp, jnp.float32) * sc
        return {'x': g(ks[0], (B, N, C), 1.0), 'w_qkv': g(ks[1], (3 * C, C), C ** (-0.5)), 'w_proj': g(ks[2], (C, C), C ** (-0.5)), 'b_proj': jnp.zeros((C,), jnp.float32), 'rpe_q_table': g(ks[3], (H, hd, NUM_BUCKETS), 0.02), 'rpe_k_table': g(ks[4], (H, hd, NUM_BUCKETS), 0.02), 'rpe_v_table': g(ks[5], (H, NUM_BUCKETS, hd), 0.02)}
    _L0_attn_in = _L0_attn_setup()

    def _L0_ffn_setup():
        import jax, jax.numpy as jnp
        import numpy as np
        E = 64
        K = 6
        CAP = 64
        ROUTE_SCALE = 1.0
        key = jax.random.key(seed)
        ks = jax.random.split(key, 9)
        B, S, D, I = (2, 128, 128, 88)
        SI = 2 * I
        s = 0.02
        return {'x': jax.random.normal(ks[0], (B, S, D), jnp.float32), 'gate_w': jax.random.normal(ks[1], (E, D), jnp.float32) * s, 'gate_b': jnp.zeros((E,), jnp.float32), 'w1': jax.random.normal(ks[2], (E, I, D), jnp.float32) * s, 'w2': jax.random.normal(ks[3], (E, D, I), jnp.float32) * s, 'w3': jax.random.normal(ks[4], (E, I, D), jnp.float32) * s, 'ws1': jax.random.normal(ks[5], (SI, D), jnp.float32) * s, 'ws2': jax.random.normal(ks[6], (D, SI), jnp.float32) * s, 'ws3': jax.random.normal(ks[7], (SI, D), jnp.float32) * s}
    _L0_ffn_in = _L0_ffn_setup()
    _d = {'L0_attn_x': _L0_attn_in['x'], 'L0_attn_w_qkv': _L0_attn_in['w_qkv'], 'L0_attn_w_proj': _L0_attn_in['w_proj'], 'L0_attn_b_proj': _L0_attn_in['b_proj'], 'L0_attn_rpe_q_table': _L0_attn_in['rpe_q_table'], 'L0_attn_rpe_k_table': _L0_attn_in['rpe_k_table'], 'L0_attn_rpe_v_table': _L0_attn_in['rpe_v_table'], 'L0_ffn_gate_w': _L0_ffn_in['gate_w'], 'L0_ffn_gate_b': _L0_ffn_in['gate_b'], 'L0_ffn_w1': _L0_ffn_in['w1'], 'L0_ffn_w2': _L0_ffn_in['w2'], 'L0_ffn_w3': _L0_ffn_in['w3'], 'L0_ffn_ws1': _L0_ffn_in['ws1'], 'L0_ffn_ws2': _L0_ffn_in['ws2'], 'L0_ffn_ws3': _L0_ffn_in['ws3']}
    _x0 = _d['L0_attn_x']
    _d['L0_attn_x'] = jax.random.normal(jax.random.fold_in(jax.random.key(seed), 1), (4, 1024, 128), dtype=_x0.dtype)
    del _x0
    return _d

def reference(L0_attn_x, L0_attn_w_qkv, L0_attn_w_proj, L0_attn_b_proj, L0_attn_rpe_q_table, L0_attn_rpe_k_table, L0_attn_rpe_v_table, L0_ffn_gate_w, L0_ffn_gate_b, L0_ffn_w1, L0_ffn_w2, L0_ffn_w3, L0_ffn_ws1, L0_ffn_ws2, L0_ffn_ws3):

    def _L0_attn_ref(x, w_qkv, w_proj, b_proj, rpe_q_table, rpe_k_table, rpe_v_table):
        import jax, jax.numpy as jnp
        import numpy as np
        NUM_BUCKETS = 63

        def _rp_bucket(N):
            rel = jnp.arange(N)[None, :] - jnp.arange(N)[:, None]
            half = NUM_BUCKETS // 2
            return (jnp.clip(rel, -half, half) + half).astype(jnp.int32)
        B, N, C = x.shape
        H = rpe_k_table.shape[0]
        hd = C // H
        scale = hd ** (-0.5)
        qkv = (x @ w_qkv.T).reshape(B, N, 3, H, hd).transpose(2, 0, 3, 1, 4)
        q, k, v = (qkv[0] * scale, qkv[1], qkv[2])
        attn = jnp.einsum('bhid,bhjd->bhij', q, k)
        rp = _rp_bucket(N)
        idx = rp[None, None]
        qL = jnp.einsum('bhid,hdm->bhim', q, rpe_k_table)
        attn = attn + jnp.take_along_axis(qL, idx, axis=-1)
        kL = jnp.einsum('bhjd,hdm->bhjm', k * scale, rpe_q_table)
        attn = attn + jnp.swapaxes(jnp.take_along_axis(kL, idx, axis=-1), 2, 3)
        attn = jax.nn.softmax(attn, axis=-1)
        out = jnp.einsum('bhij,bhjd->bhid', attn, v)
        a_t = attn.transpose(2, 3, 0, 1)
        S = jax.vmap(lambda a, seg: jax.ops.segment_sum(a, seg, num_segments=NUM_BUCKETS))(a_t, rp)
        out = out + jnp.einsum('inbh,hnd->bhid', S, rpe_v_table)
        x_out = out.transpose(0, 2, 1, 3).reshape(B, N, C)
        return x_out @ w_proj.T + b_proj

    def _L0_ffn_ref(x, gate_w, gate_b, w1, w2, w3, ws1, ws2, ws3):
        import jax, jax.numpy as jnp
        import numpy as np
        E = 64
        K = 6
        CAP = 64
        ROUTE_SCALE = 1.0
        shape = x.shape
        D = shape[-1]
        xf = x.reshape(-1, D)
        T = xf.shape[0]
        scores = jax.nn.softmax(xf @ gate_w.T, axis=-1)
        _, idx = jax.lax.top_k(scores + gate_b, K)
        weights = jnp.take_along_axis(scores, idx, axis=1) * ROUTE_SCALE
        flat_e = idx.reshape(-1)
        order = jnp.argsort(flat_e)
        se = flat_e[order]
        counts = jnp.bincount(flat_e, length=E)
        starts = jnp.cumsum(counts) - counts
        pos = jnp.arange(T * K) - starts[se]
        tok = order // K
        xb = jnp.zeros((E, CAP, D), xf.dtype).at[se, pos].set(xf[tok], mode='drop')
        h = jax.nn.silu(jnp.einsum('ecd,eid->eci', xb, w1)) * jnp.einsum('ecd,eid->eci', xb, w3)
        yb = jnp.einsum('eci,edi->ecd', h, w2)
        valid = (pos < CAP).astype(xf.dtype)
        contrib = yb[se, jnp.minimum(pos, CAP - 1)]
        wf = weights.reshape(-1)[order] * valid
        y = jnp.zeros_like(xf).at[tok].add(contrib * wf[:, None])
        z = jax.nn.silu(xf @ ws1.T) * (xf @ ws3.T) @ ws2.T
        return (y + z).reshape(shape)
    x = L0_attn_x
    xn = _layernorm(x, axis=-1)
    x = x + _L0_attn_ref(xn, L0_attn_w_qkv, L0_attn_w_proj, L0_attn_b_proj, L0_attn_rpe_q_table, L0_attn_rpe_k_table, L0_attn_rpe_v_table) + _L0_ffn_ref(xn, L0_ffn_gate_w, L0_ffn_gate_b, L0_ffn_w1, L0_ffn_w2, L0_ffn_w3, L0_ffn_ws1, L0_ffn_ws2, L0_ffn_ws3)
    return x

_drawn_inputs = setup_inputs


def setup_inputs(seed=0):
    import zlib

    import numpy as np

    out = dict(_drawn_inputs(seed))
    spreads = {'L0_attn_b_proj': (0.0, 0.367), 'L0_ffn_gate_b': (0.0, 0.8)}
    factors = {'L0_attn_rpe_q_table': 39.96,
     'L0_attn_rpe_k_table': 64.0,
     'L0_attn_rpe_v_table': 16.493,
     'L0_ffn_gate_w': 8.0,
     'L0_ffn_w1': 8.0,
     'L0_ffn_w2': 8.0,
     'L0_ffn_w3': 8.0,
     'L0_ffn_ws1': 8.0,
     'L0_ffn_ws2': 8.0,
     'L0_ffn_ws3': 8.0}
    for name, (base, spread) in spreads.items():
        noise = np.random.default_rng([zlib.crc32(name.encode()), seed]).standard_normal(out[name].shape)
        drawn = base * np.exp(spread * noise) if base else spread * noise
        out[name] = jnp.asarray(drawn.astype(out[name].dtype))
    for name, factor in factors.items():
        out[name] = (out[name] * factor).astype(out[name].dtype)
    return out
```

```python
from contextlib import ExitStack

import concourse.bass as bass
from concourse import mybir

F32 = mybir.dt.float32
BF16 = mybir.dt.bfloat16
I32 = mybir.dt.int32
ALU = mybir.AluOpType
ACT = mybir.ActivationFunctionType
AX = mybir.AxisListType

P = 128
COMBOS = 6
K_PART = [0, 0, 1, 1, 0, 2]
Q_PART = [0, 1, 0, 1, 2, 0]
TILE = 32
WIN = 3 * TILE
DIST = 4 * TILE - 1
ROW_M = 64
ROW_C = 67
ROW_K = 73
ROWS = 76
DROW = 1024 + 128
SLOTS = 16
LAG = 4
BIG = 1.0e30


def wait(eng, sem, value):
    if not isinstance(value, int) or value > 0:
        eng.wait_ge(sem, value)


def span(lo, hi, half):
    lo, hi = max(lo, 512 * half), min(hi, 512 * half + 512)
    return (lo, hi) if lo < hi else None


def value_variant(ti, J):
    r = ti - 4 * J
    return 1 if r <= -2 else 2 if r == -1 else 4 + r if r <= 3 else 3 if r == 4 else 0


def value_kind(variant, s):
    if variant == 0:
        return 0
    if variant == 1:
        return 1
    r = {2: -1, 3: 4}.get(variant, variant - 4)
    return None if abs(s - r) <= 1 else (0 if s < r else 1)


def program(nc, x, wqkvg, w_proj, b_proj, rk_far, rq_far, rk_rows, rq_rows, rv_rows, rv_far,
            gate_b, w1, w3, w2, ws1, ws3, ws2, ident_c, tri_c, part_c, kconst_c, vmask_c, slot_c, out):
    B, N, C = x.shape
    T = B * N
    NB = T // P
    G = T // 512
    H = 16
    HD = C // H
    HEADS = B * H
    NJ = N // P
    E = gate_b.shape[1]
    I = w1.shape[2]
    SC = float(HD) ** -0.5
    TOPK, CAP = 6, 64
    HALF_LOOPS = (HEADS - 4) // 8
    LOOPS = (HEADS - 4) // 4

    ctx = ExitStack()
    with ctx:
        def sb(name, shape, dt=F32):
            return ctx.enter_context(nc.sbuf_tensor(name, shape, dt))

        def sem(name):
            return ctx.enter_context(nc.semaphore(name))

        def dram(name, shape, dt=F32):
            return nc.dram_tensor(name, shape, dt, kind="Internal").ap()

        q_stack = dram("q_stack", [H * HD, COMBOS, T], BF16)
        k_stack = dram("k_stack", [H * HD, COMBOS, T], BF16)
        q_far = dram("q_far", [H, 9, T], BF16)
        k_far = dram("k_far", [H, 6, T], BF16)
        tab_stack = dram("tab_stack", [48, H, 2, P], BF16)
        dq_d = dram("dq_d", [DIST, DROW])
        aj_d = dram("aj_d", [N, P])
        pa_d = dram("pa_d", [N, P])
        dp_d = dram("dp_d", [DIST, DROW])
        xb_d = dram("xb_d", [E * CAP, C])
        yb_d = dram("yb_d", [E * CAP, C])

        X = sb("X", [P, NB, C])
        XNA = sb("XNA", [P, NB, C])
        VR = sb("VR", [P, B, H, NJ, HD])
        ON = sb("ON", [P, NB, C])
        TV = sb("TV", [P, H, 8, HD])
        PT = sb("PT", [P, TILE + NJ * N + TILE])
        accm = sb("accm", [P, 2, N])
        Qs = sb("Qs", [ROWS, 4, N], BF16)
        Ks = sb("Ks", [ROWS, 4, 2, N], BF16)
        Ksf = Ks[:, :, :, :].rearrange("p a b c -> p (a b c)")
        Qsf = Qs[:, :, :].rearrange("p a b -> p (a b)")
        tab = sb("tab", [ROWS, 4, 2, P], BF16)
        WT = sb("WT", [P, 4, NJ, WIN])
        Vst = sb("Vst", [P, 2, NJ, 8, 9])
        dq_e = sb("dq_e", [P, N])
        dq_s = sb("dq_s", [P, N])
        aj_e = sb("aj_e", [P, NJ, P])
        pa_s = sb("pa_s", [P, NJ, P])
        dp_e = sb("dp_e", [P, N])
        dp_s = sb("dp_s", [P, N])
        Oev = sb("Oev", [P, 2, 256])
        mx = sb("mx", [P, 4, NJ])
        mparts = sb("mparts", [P, NJ, 3], BF16)
        rden = sb("rden", [P, NJ])
        ident = sb("ident", [P, P])
        zcol = sb("zcol", [P, 1])
        identb = sb("identb", [P, P], BF16)
        RV = sb("RV", [P, H, HD])
        wp = sb("wp", [P, C])
        yg = sb("yg", [P, TOPK, C])
        idx = sb("idx", [P, NB, 8], I32)
        wts = sb("wts", [P, TOPK, NB])
        ew = sb("ew", [P, 2, 2 * 2 * I])
        ew2 = sb("ew2", [P, 2, 2 * C])
        exb = sb("exb", [P, 2, C])

        def cut(t, at, shape, dt=F32):
            n = 1
            for s in shape[1:]:
                n *= s
            w = n if dt == F32 else n // 2
            a = t[:, at:at + w]
            if dt != F32:
                a = a.bitcast(dt)
            names = " ".join("abcd"[:len(shape) - 1])
            kw = {"abcd"[k]: shape[k + 1] for k in range(len(shape) - 1)}
            return (a.rearrange(f"p ({names}) -> p {names}", **kw) if len(shape) > 2 else a), at + w

        at = 0
        LG, at = cut(PT, at, [P, NB, E])
        RB, at = cut(PT, at, [P, NB, E])
        RC, at = cut(PT, at, [P, NB, E])
        RD, at = cut(PT, at, [P, NB, E])
        ONf = ON[:, :, :].rearrange("p a b -> p (a b)")
        at = 0
        RV66, at = cut(ONf, at, [P, NB, E + 2])
        maskb, at = cut(ONf, at, [P, NB, E], BF16)
        assert at <= NB * C
        accf = accm[:, :, :].rearrange("p a b -> p (a b)")
        prevb, at = cut(accf, 0, [P, NB, E], BF16)
        at = 0
        XN, at = cut(accf, at, [P, 4, C])
        XT, at = cut(accf, at, [P, 512])
        QF, at = cut(accf, at, [P, 512])
        KF, at = cut(accf, at, [P, 512])
        at = 0
        CF, at = cut(dq_e, at, [P, 512])
        QR, at = cut(dq_e, at, [P, 512])
        at = 0
        KR, at = cut(dp_e, at, [P, 512])
        CR, at = cut(dp_e, at, [P, 512])
        at = 0
        QP, at = cut(dq_s, at, [P, 3, 512], BF16)
        at = 0
        KP, at = cut(dp_s, at, [P, 3, 512], BF16)
        pas = pa_s[:, :, :].rearrange("p a b -> p (a b)")
        CP, at = cut(pas, 0, [P, 3, 512], BF16)
        aje = aj_e[:, :, :].rearrange("p a b -> p (a b)")
        EX, at = cut(aje, 0, [P, 2, 512])
        WTf = WT[:, :, :, :].rearrange("p a b c -> p (a b c)")
        at = 0
        HG, at = cut(WTf, at, [P, 2, 512])
        wq_s, at = cut(WTf, at, [P, 3 * C + E])
        ws1_s, at = cut(WTf, at, [P, 2 * I])
        ws3_s, at = cut(WTf, at, [P, 2 * I])
        ws2_s, at = cut(WTf, at, [P, 2, C])
        bp_s, at = cut(WTf, at, [P, C])
        cqk, at = cut(WTf, at, [P, 2, 2 * H])
        st6, at = cut(WTf, at, [P, NB, 6])
        mean, at = cut(WTf, at, [P, NB])
        rstd, at = cut(WTf, at, [P, NB])
        tmpn, at = cut(WTf, at, [P, 2, NB])
        assert at <= 3072
        Vf = Vst[:, :, :, :, :].rearrange("p a b c d -> p (a b c d)")
        at = 0
        gb_s, at = cut(Vf, at, [P, E])
        slot_s, at = cut(Vf, at, [P, E])
        trib, at = cut(Vf, at, [P, P], BF16)
        oneb, at = cut(Vf, at, [P, P], BF16)
        rmax, at = cut(Vf, at, [P, NB])
        rsum, at = cut(Vf, at, [P, NB])
        top8, at = cut(Vf, at, [P, NB, 8])
        assert at <= 1152
        vm_s = dp_s[0:2, 0:8 * P]
        ewf = ew[:, :, :].rearrange("p a b -> p (a b)")
        rvf_s = ewf[0:2, 0:C]
        part_s = sb("part_s", [48, 2, 3])

        PS = ctx.enter_context(nc.psum_tensor("PS", [P, 8, 512], F32))
        MISC = PS[:, 6:8, :].rearrange("p a b -> p (a b)")

        w_in, x_in, c_in, tabs_in = sem("w_in"), sem("x_in"), sem("c_in"), sem("tabs_in")
        zero_set, one_set, zeros_out = sem("zero_set"), sem("one_set"), sem("zeros_out")
        psum_zeroed, pads_set, kconst_in = sem("psum_zeroed"), sem("pads_set"), sem("kconst_in")
        dve_step, pool_step, cut_step = sem("dve_step"), sem("pool_step"), sem("cut_step")
        bn_done, max_step, rden_ready = sem("bn_done"), sem("max_step"), sem("rden_ready")
        stats_ready, rstd_ready = sem("stats_ready"), sem("rstd_ready")
        xn_ready, xna_copied = sem("xn_ready"), sem("xna_copied")
        xt_psum, xt_ready, qk_psum, qf_ready, kf_ready = (
            sem("xt_psum"), sem("xt_ready"), sem("qk_psum"), sem("qf_ready"), sem("kf_ready"))
        vg_psum, vg_copied = sem("vg_psum"), sem("vg_copied")
        sh_psum, sh_exp, sh_ready, z_psum, z_added = (
            sem("sh_psum"), sem("sh_exp"), sem("sh_ready"), sem("z_psum"), sem("z_added"))
        c_psum, cf_ready, cqk_scaled = sem("c_psum"), sem("cf_ready"), sem("cqk_scaled")
        q_cut, k_cut, c_cut, stacks_out = sem("q_cut"), sem("k_cut"), sem("c_cut"), sem("stacks_out")
        tv_psum, tv_ready, tabs_cut, tabs_out = (
            sem("tv_psum"), sem("tv_ready"), sem("tabs_cut"), sem("tabs_out"))
        route_max, route_exp, mask_ready, pos_psum, pos_read, idx_ready, wts_ready = (
            sem("route_max"), sem("route_exp"), sem("mask_ready"), sem("pos_psum"), sem("pos_read"),
            sem("idx_ready"), sem("wts_ready"))
        stack_in = [sem(f"stack_in{r}") for r in range(4)]
        wt_in = [sem(f"wt_in{r}") for r in range(4)]
        s1_ready, s1_read, s2_ready, s2_read = (
            sem("s1_ready"), sem("s1_read"), sem("s2_ready"), sem("s2_read"))
        accT_psum, mparts_ready, mrow_psum, mrow_ready = (
            sem("accT_psum"), sem("mparts_ready"), sem("mrow_psum"), sem("mrow_ready"))
        dq_psum, dq_copied, dq_out, dq_in = sem("dq_psum"), sem("dq_copied"), sem("dq_out"), sem("dq_in")
        aj_psum, aj_copied, aj_out = sem("aj_psum"), sem("aj_copied"), sem("aj_out")
        pa_out = [sem("pa_out0"), sem("pa_out1")]
        pa_in = sem("pa_in")
        dp_psum, dp_copied, dp_out, dp_in = sem("dp_psum"), sem("dp_copied"), sem("dp_out"), sem("dp_in")
        v_ready, pv_done, o_copied, fin_psum, on_ready = (
            sem("v_ready"), sem("pv_done"), sem("o_copied"), sem("fin_psum"), sem("on_ready"))
        scattered, ew_in, ex_T, ex_Tc, ex_h, ex_e, ex_g, ex_y, ex_yc, ex_out = (
            sem("scattered"), [sem("ew_in0"), sem("ew_in1")], sem("ex_T"), sem("ex_Tc"), sem("ex_h"),
            sem("ex_e"), sem("ex_g"), sem("ex_y"), sem("ex_yc"), sem("ex_out"))
        ex_step = sem("ex_step")
        gathered, y_added = sem("gathered"), sem("y_added")
        on_st, pj_T, pj_Tc, pj_y, pj_add, stored = (
            sem("on_st"), sem("pj_T"), sem("pj_Tc"), sem("pj_y"), sem("pj_add"), sem("stored"))

        def live(h, c):
            return c is None or 0 <= h < HEADS

        def iterations(eng, body):
            for h in range(-2, 2):
                body(0, h, True)
            with eng.Fori(0, HALF_LOOPS) as i:
                for r in range(4):
                    body(i, 2 + r, False)
            yield
            with eng.Fori(HALF_LOOPS, LOOPS) as i:
                for r in range(4):
                    body(i, 2 + r, False)
            for h in range(HEADS - 2, HEADS + 2):
                body(0, h, True)

        def batch_of(h):
            b = h // H
            return b if isinstance(h, int) else nc.s_assert_within(
                b, 0, B - 1, skip_runtime_bounds_check_because="the loops' heads are below HEADS")

        def rows(t, offset, pattern):
            return bass.AP(t.tensor, offset, pattern)

        ZEROS = 16 * (5 + E * CAP // 1024 + 3 * (T // 1024))

        block = ctx.enter_context(nc.Block())

        @block.sync
        def _(sp):
            for dst, src in ((wq_s, wqkvg), (ws1_s, ws1), (ws3_s, ws3), (wp[:, :], w_proj),
                             (ident[:, :], ident_c), (cqk[:, 0, :], rk_far), (cqk[:, 1, :], rq_far)):
                sp.dma_start(dst, src).then_inc(w_in, 16)
            sp.dma_start(ws2_s[0:I], ws2.rearrange("c i d -> i c d")).then_inc(w_in, 16)
            sp.dma_start(RV[0:DIST, :, :], rv_rows).then_inc(w_in, 16)
            sp.dma_start(bp_s, b_proj.partition_broadcast(P)).then_inc(w_in, 16)
            sp.dma_start(gb_s, gate_b.partition_broadcast(P)).then_inc(w_in, 16)
            sp.dma_start(slot_s, slot_c.partition_broadcast(P)).then_inc(w_in, 16)
            sp.dma_start(vm_s, vmask_c).then_inc(w_in, 16)
            sp.dma_start(rvf_s, rv_far).then_inc(w_in, 16)
            xv = x.rearrange("b (j p) c -> p (b j) c", p=P)
            for g in range(4):
                n = NB // 4
                sp.dma_start(X[:, n * g:n * g + n, :], xv[:, n * g:n * g + n, :]).then_inc(x_in, 16)
            sp.wait_ge(zero_set, 1)
            Z = dp_e
            sp.dma_start(dq_d[:, 0:N], Z[0:DIST, :]).then_inc(zeros_out, 16)
            sp.dma_start(dq_d[:, N:DROW], Z[0:DIST, 0:P]).then_inc(zeros_out, 16)
            sp.dma_start(dp_d[:, 0:N], Z[0:DIST, :]).then_inc(zeros_out, 16)
            sp.dma_start(dp_d[:, N:DROW], Z[0:DIST, 0:P]).then_inc(zeros_out, 16)
            sp.dma_start(pa_d.rearrange("(a p) n -> p a n", p=P), Z[:, :].rearrange("p (a n) -> p a n", n=P)).then_inc(zeros_out, 16)
            for n in range(E * CAP // 1024):
                sp.dma_start(xb_d[n * 1024:(n + 1) * 1024, :].rearrange("(p a) n -> p (a n)", p=P),
                             Z[:, :]).then_inc(zeros_out, 16)
            Zb = Z[0:H, :].bitcast(BF16)
            for n in range(3):
                for m in range(T // 1024):
                    sp.dma_start(q_far[:, n, m * 1024:(m + 1) * 1024], Zb[:, 0:1024]).then_inc(zeros_out, 16)
            sp.wait_ge(zeros_out, ZEROS)
            with sp.Fori(0, G) as g:
                tok = bass.ds(g * 512, 512)
                sp.wait_ge(q_cut, g + 1)
                for n, part in enumerate(Q_PART):
                    sp.dma_start(q_stack[:, n, tok], QP[:, part, :]).then_inc(stacks_out, 16)
                sp.wait_ge(k_cut, g + 1)
                for n, part in enumerate(K_PART):
                    sp.dma_start(k_stack[:, n, tok], KP[:, part, :]).then_inc(stacks_out, 16)
                sp.wait_ge(c_cut, g + 1)
                for n in range(3):
                    for m in range(2):
                        sp.dma_start(q_far[:, 3 + 3 * m + n, tok],
                                     CP[16 * m:16 * m + 16, n, :]).then_inc(stacks_out, 16)
                        sp.dma_start(k_far[:, 3 * m + n, tok],
                                     CP[32 + 16 * m:48 + 16 * m, n, :]).then_inc(stacks_out, 16)
            sp.wait_ge(stacks_out, 24 * 16 * G)

            sp.wait_ge(tabs_cut, 2)
            for n, t in ((0, Ksf), (1, Qsf)):
                sp.dma_start(tab_stack[:, :, n, :],
                             t[0:48, 0:H * P].rearrange("p (h n) -> p h n", h=H)).then_inc(tabs_out, 16)
            sp.wait_ge(tabs_out, 32)
            sp.wait_ge(pads_set, 1)
            sp.wait_ge(kconst_in, 64)
            sp.wait_ge(wts_ready, 1)

            def load_stacks(i, c):
                h, r = (4 * i + c) % HEADS, c % 4
                b, hh = batch_of(h), h % H
                tok = bass.ds(b * N, N)
                qs = q_stack.rearrange("(h d) n t -> h (d n) t", h=H)[bass.ds(hh, 1), :, tok].rearrange("a n t -> (a n) t")
                sp.dma_start(Qs[0:48, r, :], qs).then_inc(stack_in[r], 16)
                sp.dma_start(Qs[ROW_M:ROW_M + 9, r, :], q_far[bass.ds(hh, 1), :, tok].rearrange("a n t -> (a n) t")
                             ).then_inc(stack_in[r], 16)
                ks = k_stack.rearrange("(h d) n t -> h (d n) t", h=H)[bass.ds(hh, 1), :, tok].rearrange("a n t -> (a n) t")
                kf = k_far[bass.ds(hh, 1), :, tok].rearrange("a (v n) t -> n (a v) t", v=2)
                for v in range(2):
                    sp.dma_start(Ks[0:48, r, v, :], ks).then_inc(stack_in[r], 16)
                sp.dma_start(Ks[ROW_K:ROWS, r, :, :], kf).then_inc(stack_in[r], 16)
                sp.dma_start(tab[0:48, r, :, :],
                             tab_stack[:, bass.ds(hh, 1), :, :].rearrange("p a v n -> p (a v) n")).then_inc(stack_in[r], 16)

            def shear(s, J0, J1, t):
                return rows(t, (P * J0 + TILE * s) * P + TILE - 1,
                            [[P - 1, TILE], [P * P, J1 - J0], [1, WIN]])

            def window_out(c, i, part):
                h = 4 * i + c
                sp.wait_ge(s2_read, SLOTS * h + 8 * part + 8)
                wait(sp, pa_in, 16 * h)
                for s in range(4):
                    src = rows(PT[:, :], 0, PT[TILE * s:TILE * s + TILE, 0:1].ap)
                    base = PT[TILE * s:TILE * s + TILE, TILE * s + 4 * part * (N + P):TILE * s + 4 * part * (N + P) + WIN]
                    src = rows(base, base.offset, [list(base.ap[0]), [N + P, 4], [1, WIN]])
                    sp.dma_start(shear(s, 4 * part, 4 * part + 4, pa_d), src).then_inc(pa_out[part], 16)

            def iteration(i, c, peeled):
                h = 4 * i + c
                on = lambda n: (not peeled) or 0 <= c + n < HEADS
                if on(-1):
                    window_out(c - 1, i, 1)
                if on(3):
                    wait(sp, s2_ready, SLOTS * h)
                    load_stacks(i, c + 3)
                if on(-1):
                    sp.wait_ge(pa_out[0], 64 * h)
                    sp.wait_ge(pa_out[1], 64 * h)
                    wait(sp, dp_psum, h - 1)
                    sp.dma_start(pa_s[:, :, :], pa_d.rearrange("(a p) n -> p a n", p=P)).then_inc(pa_in, 16)
                if on(2):
                    sp.wait_ge(dq_copied, h + 3)
                    wait(sp, dq_in, 16 * (h + 2))
                    sp.dma_start(dq_d[:, 64:64 + N], dq_e[0:DIST, :]).then_inc(dq_out, 16)
                    sp.wait_ge(dq_out, 16 * (h + 3))
                    wait(sp, aj_psum, h + 2)
                    sp.dma_start(dq_s[0:DIST, :], rows(dq_d, 1, [[DROW + 1, DIST], [1, N]])).then_inc(dq_in, 16)
                    sp.wait_ge(aj_copied, h + 3)
                    if not peeled or c + 1 >= 0:
                        sp.wait_ge(wt_in[(c + 1) % 4], 64 * (i + (c + 1) // 4 + 1))
                    sp.dma_start(aj_d.rearrange("(a p) n -> p a n", p=P), aj_e[:, :, :]).then_inc(aj_out, 16)
                    sp.wait_ge(aj_out, 16 * (h + 3))
                    wait(sp, s2_ready, SLOTS * (h - 1))
                    for s in range(4):
                        sp.dma_start(WT[TILE * s:TILE * s + TILE, (c + 2) % 4, :, :],
                                     shear(s, 0, NJ, aj_d)).then_inc(wt_in[(c + 2) % 4], 16)
                if on(0):
                    window_out(c, i, 0)
                if on(-1):
                    sp.wait_ge(dp_copied, h)
                    wait(sp, dp_in, 16 * (h - 1))
                    sp.dma_start(dp_d[:, 64:64 + N], dp_e[0:DIST, :]).then_inc(dp_out, 16)
                    sp.wait_ge(dp_out, 16 * h)
                    wait(sp, fin_psum, h - 1)
                    sp.dma_start(dp_s[0:DIST, :], rows(dp_d, DIST, [[DROW - 1, DIST], [1, N]])).then_inc(dp_in, 16)

            load_stacks(0, 0)
            steps = iterations(sp, iteration)
            next(steps)
            sp.wait_ge(scattered, 16 * NB * TOPK)

            def load_pair(p, e):
                sp.dma_start(exb[:, p, :], xb_d[bass.ds(e * 2 * CAP, 2 * CAP), :]).then_inc(ew_in[p], 16)
                sp.dma_start(ew[:, p, 0:2 * I].rearrange("p (a i) -> p a i", a=2), w1[:, bass.ds(e * 2, 2), :]).then_inc(ew_in[p], 16)
                sp.dma_start(ew[:, p, 2 * I:4 * I].rearrange("p (a i) -> p a i", a=2), w3[:, bass.ds(e * 2, 2), :]).then_inc(ew_in[p], 16)
                sp.dma_start(ew2[0:I, p, :].rearrange("p (a i) -> p a i", a=2), w2[:, bass.ds(e * 2, 2), :]).then_inc(ew_in[p], 16)

            load_pair(0, 0)
            load_pair(1, 1)
            with sp.Fori(0, E // 4) as k:
                for p in range(2):
                    e = 2 * k + p
                    sp.wait_ge(ex_yc, e + 1)
                    for m in range(2):
                        sp.dma_start(yb_d[bass.ds((2 * e + m) * CAP, CAP), :],
                                     aj_e[0:CAP, 2 * p + m, :]).then_inc(ex_out, 16)
                    nxt = 2 * ((k + 1) % (E // 4)) + p
                    load_pair(p, nxt)
            sp.wait_ge(ex_out, 32 * (E // 2))
            for p in range(2):
                sp.wait_ge(ew_in[p], 64 * (E // 4 + 1))
            for _ in steps:
                pass
            sp.wait_ge(stack_in[0], 96 * (HEADS // 4 + 1))
            ov = out.rearrange("b (j p) c -> p (b j) c", p=P)
            with sp.Fori(0, G) as g:
                sp.wait_ge(pj_add, g + 1)
                sp.dma_start(ov[:, bass.ds(g * 4, 4), :], X[:, bass.ds(g * 4, 4), :]).then_inc(stored, 16)
            sp.wait_ge(stored, 16 * G)

        @block.gpsimd
        def _(pool):
            n = [0]

            def step(ins):
                n[0] += 1
                ins.then_inc(pool_step, 1)
                pool.wait_ge(pool_step, n[0])

            pool.memset(dp_e[:, :], 0.0).then_inc(zero_set, 1)
            pool.dma_start(trib, tri_c).then_inc(c_in, 16)
            pool.dma_start(part_s[:, :, :], part_c).then_inc(c_in, 16)
            pool.memset(oneb, 1.0).then_inc(one_set, 1)
            pool.wait_ge(c_in, 32)
            pool.wait_ge(zeros_out, ZEROS)
            zero_row = zcol[:, :].broadcast_to([P, 512])
            step(pool.memset(zcol[:, :], 0.0))
            with pool.Fori(0, G) as g:
                pool.wait_ge(xn_ready, g + 1)
                pool.tensor_copy(XNA[:, bass.ds(g * 4, 4), :], XN).then_inc(xna_copied, 1)
                for m, (F, R, Pt, rdy, done, np_) in enumerate(
                        ((KF, KR, KP, kf_ready, k_cut, P), (CF, CR, CP, cf_ready, c_cut, 64))):
                    def gstep(ins, k):
                        ins.then_inc(cut_step, 1)
                        pool.wait_ge(cut_step, g * 8 + (4 * m + k))

                    pool.wait_ge(rdy, g + 1)
                    pool.wait_ge(stacks_out, 24 * 16 * g)
                    gstep(pool.tensor_tensor(Pt[0:np_, 0, :], F[0:np_, :], zero_row[0:np_, :], ALU.add), 1)
                    gstep(pool.tensor_tensor(R[0:np_, :], F[0:np_, :], Pt[0:np_, 0, :], ALU.subtract), 2)
                    gstep(pool.tensor_tensor(Pt[0:np_, 1, :], R[0:np_, :], zero_row[0:np_, :], ALU.add), 3)
                    gstep(pool.tensor_tensor(R[0:np_, :], R[0:np_, :], Pt[0:np_, 1, :], ALU.subtract), 4)
                    pool.tensor_tensor(Pt[0:np_, 2, :], R[0:np_, :], zero_row[0:np_, :], ALU.add).then_inc(done, 1)
            res = Ksf[0:48, 4 * N:8 * N].bitcast(F32)
            prt = Ksf[0:48, 2 * N:4 * N]
            mul = Qsf[0:48, 2 * N:4 * N]
            for m, (src, dst) in enumerate(((rk_rows, Ksf), (rq_rows, Qsf))):
                part = dst[0:48, 0:H * P]
                pool.dma_start(res, src).then_inc(tabs_in, 16)
                pool.wait_ge(tabs_in, 16 * (m + 1))
                if m == 1:
                    step(pool.tensor_scalar(res, res, SC, None, ALU.mult))
                step(pool.tensor_copy(prt, res))
                step(pool.tensor_tensor(res, res, prt, ALU.subtract))
                step(pool.tensor_scalar(part, prt, part_s[:, m, 0:1], None, ALU.mult))
                for k in (1, 2):
                    step(pool.tensor_copy(prt, res))
                    if k == 1:
                        step(pool.tensor_tensor(res, res, prt, ALU.subtract))
                    step(pool.tensor_scalar(mul, prt, part_s[:, m, k:k + 1], None, ALU.mult))
                    ins = pool.tensor_tensor(part, part, mul, ALU.add)
                    if k == 1:
                        step(ins)
                ins.then_inc(tabs_cut, 1)
                pool.wait_ge(tabs_cut, m + 1)
            pool.wait_ge(tabs_out, 32)
            pool.wait_ge(wts_ready, 1)
            pool.memset(Qs[:, :, :], 1.0)
            pool.memset(tab[:, :, :, :], 0.0)
            for J in range(2):
                pool.memset(Vst[:, J, :, :, :], 1.0)
            pool.memset(PT[:, 0:TILE], 0.0)
            pool.memset(PT[:, TILE + NJ * N:], 0.0)
            pool.memset(Ks[:, :, :, :], 0.0).then_inc(pads_set, 1)
            pool.wait_ge(pads_set, 1)
            for r in range(4):
                pool.dma_start(Ks[ROW_M:ROW_K, r, :, :], kconst_c).then_inc(kconst_in, 16)
            pool.wait_ge(idx_ready, 1)
            pool.wait_ge(xna_copied, G)
            for blk in range(NB):
                for k in range(TOPK):
                    pool.indirect_dma_start(
                        out=xb_d, out_offset=bass.IndirectOffsetOnAxis(ap=idx[:, blk, k:k + 1], axis=0),
                        in_=XNA[:, blk, :], in_offset=None, bounds_check=E * CAP - 1, oob_is_err=False,
                    ).then_inc(scattered, 16)
            pool.wait_ge(ex_out, 32 * (E // 2))
            pool.memset(yg[:, :, :], 0.0).then_inc(y_added, 1)
            for blk in range(NB):
                def ystep(m, *a):
                    pool.tensor_tensor(*a).then_inc(y_added, 1)
                    pool.wait_ge(y_added, 5 * blk + m + 1)

                pool.wait_ge(y_added, 5 * blk + 1)
                for k in range(TOPK):
                    pool.indirect_dma_start(
                        out=yg[:, k, :], out_offset=None, in_=yb_d,
                        in_offset=bass.IndirectOffsetOnAxis(ap=idx[:, blk, k:k + 1], axis=0),
                        bounds_check=E * CAP - 1, oob_is_err=False,
                    ).then_inc(gathered, 16)
                pool.wait_ge(gathered, 16 * TOPK * (blk + 1))
                ystep(1, yg[:, :, :], yg[:, :, :], wts[:, :, blk:blk + 1].broadcast_to([P, TOPK, C]), ALU.mult)
                ystep(2, yg[:, 0:3, :], yg[:, 0:3, :], yg[:, 3:6, :], ALU.add)
                ystep(3, yg[:, 0, :], yg[:, 0, :], yg[:, 1, :], ALU.add)
                ystep(4, yg[:, 0, :], yg[:, 0, :], yg[:, 2, :], ALU.add)
                ystep(5, X[:, blk, :], X[:, blk, :], yg[:, 0, :], ALU.add)

        @block.tensor
        def _(pe):
            def mm(o, l, r, start=True, stop=True):
                return pe.matmul(o, l, r, start=start, stop=stop, skip_group_check=True)

            pe.wait_ge(w_in, 16 * 14)
            for v in range(8):
                ins = mm(PS[:, v // 4, (v % 4) * P:(v % 4 + 1) * P], vm_s[:, v * P:(v + 1) * P], rvf_s,
                         start=v % 4 == 0)
            ins.then_inc(tv_psum, 1)
            pe.wait_ge(tv_ready, 1)
            pe.wait_ge(cqk_scaled, 1)
            with pe.Fori(0, G) as g:
                pe.wait_ge(xn_ready, g + 1)
                pe.wait_ge(z_added, g)
                for q in range(4):
                    ins = pe.transpose(PS[:, 0, q * P:(q + 1) * P], XN[:, q, :], ident[:, :])
                ins.then_inc(xt_psum, 1)
                pe.wait_ge(xt_ready, g + 1)
                pe.wait_ge(cf_ready, g)
                mm(PS[:, 1, :], wq_s[:, 0:C], XT).then_inc(qk_psum, 1)
                pe.wait_ge(sh_ready, 2 * g)
                mm(PS[:, 2, :], wq_s[:, C:2 * C], XT).then_inc(qk_psum, 1)
                pe.wait_ge(vg_copied, g)
                for q in range(4):
                    ins = mm(PS[:, 3 + q // 2, (q % 2) * 192:(q % 2) * 192 + 192], XT[:, q * P:(q + 1) * P],
                             wq_s[:, 2 * C:3 * C + E], start=q % 2 == 0)
                ins.then_inc(vg_psum, 1)
                mm(PS[0:I, 5, :], ws1_s[:, 0:I], XT)
                mm(PS[0:I, 6, :], ws3_s[:, 0:I], XT).then_inc(sh_psum, 1)
                mm(PS[0:I, 7, :], ws1_s[:, I:2 * I], XT)
                pe.wait_ge(kf_ready, g + 1)
                mm(PS[0:I, 2, :], ws3_s[:, I:2 * I], XT).then_inc(sh_psum, 1)
                pe.wait_ge(qf_ready, g + 1)
                mm(PS[0:32, 1, :], cqk[:, 0, :], QF)
                mm(PS[32:64, 1, :], cqk[:, 1, :], KF).then_inc(c_psum, 1)
                pe.wait_ge(sh_ready, 2 * g + 2)
                for q in range(4):
                    for a in range(2):
                        ins = mm(PS[:, 0, q * P:(q + 1) * P], HG[0:I, a, q * P:(q + 1) * P], ws2_s[0:I, a, :],
                                 start=q == 0 and a == 0, stop=a == 1)
                ins.then_inc(z_psum, 1)
            pe.wait_ge(mask_ready, 1)
            pe.wait_ge(z_added, G)
            for m in range(NB // 8):
                mm(PS[:, m, :], trib, maskb[:, 8 * m:8 * m + 8, :].rearrange("p a e -> p (a e)"), stop=False)
                mm(PS[:, m, :], oneb, prevb[:, 8 * m:8 * m + 8, :].rearrange("p a e -> p (a e)"),
                   start=False).then_inc(pos_psum, 1)
            pe.wait_ge(pos_read, 1)
            pe.wait_ge(psum_zeroed, 1)

            def bias(bank, half, J, r):
                ins = None
                for s in range(4):
                    t = 4 * J + s
                    w = span(TILE * (t - 1), TILE * (t + 2), half)
                    w = w and (max(w[0], 0), min(w[1], N))
                    if w and w[0] < w[1]:
                        a = w[0] - TILE * (t - 1)
                        ins = mm(PS[TILE * s:TILE * s + TILE, bank, w[0] - 512 * half:w[1] - 512 * half],
                                 ident[:, TILE * s:TILE * s + TILE], WT[:, r, J, a:a + w[1] - w[0]], start=False)
                return ins

            def scores(bank, half, J, r):
                pieces = []
                for s in range(4):
                    t = 4 * J + s
                    own = []
                    for kind, lo, hi in (("U", 0, TILE * (t - 1)), ("W", max(0, TILE * (t - 1)), min(N, TILE * (t + 2))),
                                         ("L", TILE * (t + 2), N)):
                        w = span(lo, hi, half)
                        if w:
                            own.append((s, kind, w, not own))
                    pieces.append(own)
                for n in range(3):
                    for own in pieces:
                        if n < len(own):
                            s, kind, w, first = own[n]
                            k = ROWS if kind != "W" else ROW_C
                            ins = mm(
                               PS[TILE * s:TILE * s + TILE, bank, w[0] - 512 * half:w[1] - 512 * half],
                               Ks[0:k, r, 1 if kind == "U" else 0, P * J + TILE * s:P * J + TILE * s + TILE],
                               Qs[0:k, r, w[0]:w[1]], start=first)
                return bias(bank, half, J, r) or ins

            def unit(i, c, u, which):
                h, r = 4 * i + c, c % 4
                ready, read, bank = ((s1_ready, s1_read, 0), (s2_ready, s2_read, 2))[which]
                if which == 0 and u == 0:
                    pe.wait_ge(stack_in[r], 96 * (i + c // 4 + 1))
                    pe.wait_ge(wt_in[r], 64 * (i + c // 4 + 1))
                if which == 1 and u == 0:
                    pe.wait_ge(mrow_ready, h + 1)
                wait(pe, read, SLOTS * h + u - 1)
                J, half = u // 2, u % 2
                scores(bank + u % 2, half, J, r).then_inc(ready, 1)

            def values(i, c, J):
                h, p = 4 * i + c, c % 2
                pe.wait_ge(s2_read, SLOTS * h + 2 * J + 2)
                if J == 0:
                    pe.wait_ge(v_ready, h + 1)
                    wait(pe, o_copied, h - 1)
                own = []
                for q in range(4):
                    mine, t = [], 8 * q
                    while t < 8 * q + 8:
                        v, e = value_variant(t, J), t
                        while e < 8 * q + 8 and value_variant(e, J) == v:
                            e += 1
                        mine.append((q, v, t, e))
                        t = e
                    own.append(mine)
                for n in range(max(map(len, own))):
                    for mine in own:
                        if n < len(mine):
                            q, v, t, e = mine[n]
                            ins = mm(PS[TILE * q:TILE * q + 9, 4 + p, TILE * (t - 8 * q):TILE * (e - 8 * q)],
                                     Vst[:, p, J, v, :], PT[:, TILE + N * J + TILE * t:TILE + N * J + TILE * e],
                                     start=J == 0 and n == 0, stop=J == NJ - 1)
                ins.then_inc(pv_done, 1)

            def misc_free(h, *which):
                for s, v in which:
                    wait(pe, s, v if not isinstance(v, int) else min(v, HEADS))

            def iteration(i, c, peeled):
                h = 4 * i + c
                on = lambda n: (not peeled) or 0 <= c + n < HEADS
                for s in range(SLOTS):
                    if on(1):
                        unit(i, c + 1, s, 0)
                    if s == 0 and on(0):
                        pe.wait_ge(s1_read, SLOTS * h + SLOTS)
                        misc_free(h, (dp_copied, h - 1), (aj_copied, h + 2))
                        for I_ in range(NJ):
                            ins = pe.transpose(MISC[:, I_ * P:(I_ + 1) * P], accm[:, c % 2, I_ * P:(I_ + 1) * P], ident[:, :])
                        ins.then_inc(accT_psum, 1)
                    if s == 2 and on(0):
                        pe.wait_ge(mparts_ready, h + 1)
                        for I_ in range(NJ):
                            ins = mm(MISC[0:3, I_ * P:(I_ + 1) * P], mparts[:, I_, :], identb[:, :], start=I_ % 4 == 0)
                        ins.then_inc(mrow_psum, 1)
                    if s == 3 and on(2):
                        r = (c + 2) % 4
                        pe.wait_ge(stack_in[r], 96 * (i + (c + 2) // 4 + 1))
                        misc_free(h, (mrow_ready, h + 1), (aj_copied, h + 2))
                        for a in range(2):
                            ins = mm(MISC[:, 512 * a:512 * a + 512], tab[:, r, 0, :], Qs[:, r, 512 * a:512 * a + 512])
                        ins.then_inc(dq_psum, 1)
                    if s >= LAG and on(0):
                        unit(i, c, s - LAG, 1)
                    if s < LAG and on(-1):
                        unit(i, c - 1, s + SLOTS - LAG, 1)
                    if s == 6 and on(-2):
                        misc_free(h, (dq_copied, h + 3), (dp_copied, h - 1))
                        pe.wait_ge(o_copied, h - 1)
                        pe.wait_ge(dp_in, 16 * (h - 1))
                        for I_ in range(NJ):
                            q, a = I_ // 2, (I_ % 2) * P
                            mm(MISC[:, 16 * I_:16 * I_ + 9], Oev[:, c % 2, a:a + P], ident[:, TILE * q:TILE * q + 9],
                               start=I_ == 0, stop=False)
                        g_ = (h - 2) % H
                        for I_ in range(NJ):
                            ins = mm(MISC[:, 16 * I_:16 * I_ + HD], dp_s[0:DIST, I_ * P:(I_ + 1) * P],
                                     RV[0:DIST, bass.ds(g_, 1), :].rearrange("p a d -> p (a d)"), start=False)
                        ins.then_inc(fin_psum, 1)
                    if s == 9 and on(2):
                        r = (c + 2) % 4
                        misc_free(h, (on_ready, h - 1), (dq_copied, h + 3))
                        pe.wait_ge(dq_in, 16 * (h + 3))
                        for J in range(NJ):
                            mm(MISC[:, J * P:(J + 1) * P], Ks[:, r, 0, J * P:(J + 1) * P], tab[:, r, 1, :],
                               start=J % 4 == 0, stop=False)
                            ins = mm(MISC[:, J * P:J * P + DIST], dq_s[0:DIST, J * P:(J + 1) * P],
                                     ident[0:DIST, 0:DIST], start=False)
                        ins.then_inc(aj_psum, 1)
                    if s == 12 and on(-1):
                        misc_free(h, (aj_copied, h + 3), (on_ready, h - 1))
                        pe.wait_ge(pa_in, 16 * h)
                        for J in range(NJ):
                            ins = pe.transpose(MISC[:, J * P:(J + 1) * P], pa_s[:, J, :], ident[:, :])
                        ins.then_inc(dp_psum, 1)
                    if s % 2 and s >= LAG + 3 and on(0):
                        values(i, c, (s - LAG - 3) // 2)
                    if s % 2 and s < LAG + 3 and on(-1):
                        values(i, c - 1, (s - LAG - 3 + SLOTS) // 2)

            steps = iterations(pe, iteration)
            next(steps)
            hm = 2 + 4 * HALF_LOOPS
            pe.wait_ge(dp_copied, hm - 1)
            with pe.Fori(0, E // 4) as k:
                for p in range(2):
                    e = 2 * k + p
                    pe.wait_ge(ew_in[p], 64 * (k + 1))
                    pe.wait_ge(ex_yc, e)
                    pe.transpose(PS[:, 6, 0:P], exb[:, p, :], ident[:, :]).then_inc(ex_T, 1)
                    pe.wait_ge(ex_Tc, e + 1)
                    for m in range(2):
                        for w in range(2):
                            ins = mm(PS[0:I, 7, (2 * w + m) * CAP:(2 * w + m + 1) * CAP],
                                     ew[:, p, (2 * w + m) * I:(2 * w + m + 1) * I], dp_e[:, p * P + m * CAP:p * P + (m + 1) * CAP],
                                     start=m == 0 and w == 0)
                    ins.then_inc(ex_h, 1)
                    pe.wait_ge(ex_g, e + 1)
                    for m in range(2):
                        ins = mm(PS[0:CAP, 6, (1 + m) * P:(2 + m) * P], dq_e[0:I, p * P + m * CAP:p * P + (m + 1) * CAP],
                                 ew2[0:I, p, m * C:(m + 1) * C], start=m == 0)
                    ins.then_inc(ex_y, 1)
            pe.wait_ge(ex_yc, E // 2)
            for _ in steps:
                pass
            with pe.Fori(0, G) as g:
                pe.wait_ge(on_st, g + 1)
                for q in range(4):
                    ins = pe.transpose(PS[:, 0, q * P:(q + 1) * P], accm[:, 0, q * P:(q + 1) * P], ident[:, :])
                ins.then_inc(pj_T, 1)
                pe.wait_ge(pj_Tc, g + 1)
                pe.wait_ge(pj_add, g)
                for q in range(4):
                    ins = mm(PS[:, 1, q * P:(q + 1) * P], accm[:, 1, q * P:(q + 1) * P], wp[:, :], start=q == 0)
                ins.then_inc(pj_y, 1)

        @block.scalar
        def _(act):
            act.wait_ge(stats_ready, 1)
            act.activation(rstd, rstd, ACT.Sqrt).then_inc(rstd_ready, 1)
            with act.Fori(0, G) as g:
                act.wait_ge(xt_psum, g + 1)
                act.wait_ge(sh_psum, 2 * g)
                act.activation(XT, PS[:, 0, :], ACT.Copy).then_inc(xt_ready, 1)
                act.wait_ge(qk_psum, 2 * g + 1)
                act.wait_ge(q_cut, g)
                act.wait_ge(c_psum, g)
                act.activation(QF, PS[:, 1, :], ACT.Copy, scale=SC).then_inc(qf_ready, 1)
                act.wait_ge(qk_psum, 2 * g + 2)
                act.wait_ge(k_cut, g)
                act.activation(KF, PS[:, 2, :], ACT.Copy).then_inc(kf_ready, 1)
                act.wait_ge(sh_ready, 2 * g)
                for a in range(2):
                    act.wait_ge(sh_psum, 2 * g + a + 1)
                    act.activation(EX[0:I, a, :], PS[0:I, 5 + 2 * a, :], ACT.Exp, scale=-1.0).then_inc(sh_exp, 1)
                act.wait_ge(c_psum, g + 1)
                act.wait_ge(c_cut, g)
                act.activation(CF[0:64, :], PS[0:64, 1, :], ACT.Copy).then_inc(cf_ready, 1)
            act.wait_ge(route_max, 1)
            act.activation(RB[:, :, :].rearrange("p a e -> p (a e)"), RB[:, :, :].rearrange("p a e -> p (a e)"),
                           ACT.Exp).then_inc(route_exp, 1)
            act.wait_ge(wts_ready, 1)
            act.wait_ge(pads_set, 1)

            def exps(i, c, u):
                h = 4 * i + c
                act.wait_ge(s2_ready, SLOTS * h + u + 1)
                J, half = u // 2, u % 2
                if half == 0:
                    wait(act, pv_done, NJ * (h - 1) + J + 1)
                    wait(act, pa_out[J // 4], 64 * h)
                act.activation(PT[:, TILE + N * J + 512 * half:TILE + N * J + 512 * half + 512],
                               PS[:, 2 + u % 2, :], ACT.Exp).then_inc(s2_read, 1)

            def iteration(i, c, peeled):
                h = 4 * i + c
                on = lambda n: (not peeled) or 0 <= c + n < HEADS
                for s in range(SLOTS):
                    if s == 2 and on(0):
                        act.wait_ge(mrow_psum, h + 1)
                        act.wait_ge(s1_ready, SLOTS * h + SLOTS)
                        act.activation(Qs[ROW_M:ROW_M + 3, c % 4, :], MISC[0:3, :], ACT.Copy).then_inc(mrow_ready, 1)
                    if s == 3 and on(2):
                        act.wait_ge(dq_psum, h + 3)
                        wait(act, dq_out, 16 * (h + 2))
                        act.activation(dq_e[:, :], MISC, ACT.Copy).then_inc(dq_copied, 1)
                    if s >= LAG and on(0):
                        exps(i, c, s - LAG)
                    if s < LAG and on(-1):
                        exps(i, c - 1, s + SLOTS - LAG)
                    if s == 5 and on(-1):
                        act.wait_ge(pv_done, NJ * h)
                        wait(act, fin_psum, h - 2)
                        act.activation(Oev[:, (c - 1) % 2, :], PS[:, 4 + (c - 1) % 2, 0:256], ACT.Copy).then_inc(o_copied, 1)

            steps = iterations(act, iteration)
            next(steps)
            hm = 2 + 4 * HALF_LOOPS
            act.wait_ge(dp_out, 16 * (hm - 1))
            act.wait_ge(dq_out, 16 * (hm + 2))
            with act.Fori(0, E // 4) as k:
                for p in range(2):
                    e = 2 * k + p
                    act.wait_ge(ex_T, e + 1)
                    act.activation(dp_e[:, p * P:p * P + P], PS[:, 6, 0:P], ACT.Copy).then_inc(ex_Tc, 1)
                    act.wait_ge(ex_h, e + 1)
                    act.activation(dq_e[0:I, 256 + p * P:256 + p * P + P], PS[0:I, 7, 0:P], ACT.Exp, scale=-1.0).then_inc(ex_e, 1)
            for _ in steps:
                pass
            with act.Fori(0, G) as g:
                act.wait_ge(pj_T, g + 1)
                act.wait_ge(pj_y, g)
                act.activation(accm[:, 1, 0:512], PS[:, 0, :], ACT.Copy).then_inc(pj_Tc, 1)

        @block.vector
        def _(dve):
            n = [0]

            def step(ins):
                n[0] += 1
                ins.then_inc(dve_step, 1)
                dve.wait_ge(dve_step, n[0])

            dve.wait_ge(w_in, 16 * 14)
            dve.tensor_copy(identb[:, :], ident[:, :])
            dve.tensor_scalar(cqk[:, 1, :], cqk[:, 1, :], SC, None, ALU.mult).then_inc(cqk_scaled, 1)
            dve.wait_ge(tv_psum, 1)
            for a in range(2):
                ins = dve.tensor_copy(TV[:, :, 4 * a:4 * a + 4, :].rearrange("p h v d -> p v h d"),
                                      PS[:, a, :].rearrange("p (v h d) -> p v h d", v=4, h=H))
            ins.then_inc(tv_ready, 1)
            dve.wait_ge(x_in, 64)
            with dve.Fori(0, NB) as k:
                dve.bn_stats(st6[:, bass.ds(k, 1), :].rearrange("p a s -> p (a s)"),
                             X[:, bass.ds(k, 1), :].rearrange("p a c -> p (a c)")).then_inc(bn_done, 1)
            dve.wait_ge(bn_done, NB)
            step(dve.tensor_copy(tmpn[:, 0, :], st6[:, :, 1]))
            step(dve.tensor_tensor(mean, tmpn[:, 0, :], st6[:, :, 4], ALU.add))
            step(dve.tensor_tensor(tmpn[:, 0, :], tmpn[:, 0, :], st6[:, :, 4], ALU.subtract))
            step(dve.tensor_tensor(tmpn[:, 1, :], tmpn[:, 0, :], tmpn[:, 0, :], ALU.mult))
            step(dve.tensor_tensor(rstd, st6[:, :, 2], st6[:, :, 5], ALU.add))
            step(dve.tensor_scalar(rstd, rstd, 1.0 / C, None, ALU.mult))
            step(dve.scalar_tensor_tensor(out=rstd, in0=tmpn[:, 1, :], scalar=0.25, in1=rstd, op0=ALU.mult, op1=ALU.add))
            step(dve.tensor_scalar(mean, mean, 0.5, None, ALU.mult))
            step(dve.tensor_scalar(rstd, rstd, 1e-5, None, ALU.add))
            dve.sem_inc(stats_ready, 1)
            dve.wait_ge(rstd_ready, 1)
            step(dve.reciprocal(rstd, rstd))
            base = n[0]
            PER = 10
            with dve.Fori(0, G) as g:
                k = [0]

                def gstep(ins):
                    k[0] += 1
                    ins.then_inc(dve_step, 1)
                    dve.wait_ge(dve_step, g * PER + (base + k[0]))

                dve.wait_ge(xt_psum, g)
                dve.wait_ge(xna_copied, g)
                for q in range(4):
                    ins = dve.tensor_scalar(XN[:, q, :], X[:, bass.ds(g * 4 + q, 1), :].rearrange("p a c -> p (a c)"),
                                            mean[:, bass.ds(g * 4 + q, 1)], rstd[:, bass.ds(g * 4 + q, 1)],
                                            ALU.subtract, ALU.mult)
                ins.then_inc(xn_ready, 1)
                dve.wait_ge(xn_ready, g + 1)
                dve.tensor_tensor(X[:, bass.ds(g * 4, 4), :], X[:, bass.ds(g * 4, 4), :],
                                  bp_s[:, :].unsqueeze(1).broadcast_to([P, 4, C]), ALU.add)
                dve.wait_ge(qf_ready, g + 1)
                dve.wait_ge(stacks_out, 24 * 16 * g)
                gstep(dve.tensor_copy(QP[:, 0, :], QF))
                gstep(dve.tensor_tensor(QR, QF, QP[:, 0, :], ALU.subtract))
                gstep(dve.tensor_copy(QP[:, 1, :], QR))
                gstep(dve.tensor_tensor(QR, QR, QP[:, 1, :], ALU.subtract))
                dve.tensor_copy(QP[:, 2, :], QR).then_inc(q_cut, 1)
                dve.wait_ge(vg_psum, g + 1)
                VRf = VR[:, :, :, :, :].rearrange("p b h j d -> p b j h d")
                for a in range(2):
                    src = PS[:, 3 + a, 0:384].rearrange("p (q n) -> p q n", q=2)
                    for q in range(2):
                        dve.tensor_copy(
                            VRf[:, bass.ds(g // 2, 1), bass.ds((g % 2) * 4 + 2 * a + q, 1), :, :].rearrange("p b j h d -> p (b j h) d"),
                            src[:, q, 0:C].rearrange("p (h d) -> p h d", h=H))
                    ins = dve.tensor_copy(LG[:, bass.ds(g * 4 + 2 * a, 2), :], src[:, :, C:C + E])
                ins.then_inc(vg_copied, 1)
                for a in range(2):
                    dve.wait_ge(sh_exp, 2 * g + a + 1)
                    gstep(dve.tensor_scalar(EX[0:I, a, :], EX[0:I, a, :], 1.0, None, ALU.add))
                    gstep(dve.reciprocal(EX[0:I, a, :], EX[0:I, a, :]))
                    if a == 0:
                        dve.wait_ge(z_psum, g)
                    gstep(dve.tensor_tensor(EX[0:I, a, :], PS[0:I, 5 + 2 * a, :], EX[0:I, a, :], ALU.mult))
                    dve.tensor_tensor(HG[0:I, a, :], PS[0:I, 6 if a == 0 else 2, :], EX[0:I, a, :], ALU.mult).then_inc(sh_ready, 1)
                dve.wait_ge(z_psum, g + 1)
                dve.tensor_tensor(X[:, bass.ds(g * 4, 4), :], X[:, bass.ds(g * 4, 4), :],
                                  PS[:, 0, :].rearrange("p (q c) -> p q c", q=4), ALU.add).then_inc(z_added, 1)
            assert k[0] == PER
            n[0] = base + PER * G

            def over_e(a):
                return a.unsqueeze(2).broadcast_to([P, NB, E])

            dve.wait_ge(z_added, G)
            dve.wait_ge(vg_copied, G)
            step(dve.tensor_reduce(rmax, LG, AX.X, ALU.max))
            step(dve.tensor_tensor(RB, LG, over_e(rmax), ALU.subtract))
            dve.sem_inc(route_max, 1)
            dve.wait_ge(route_exp, 1)
            step(dve.tensor_reduce(rsum, RB, AX.X, ALU.add))
            step(dve.reciprocal(rsum, rsum))
            step(dve.tensor_tensor(LG, RB, over_e(rsum), ALU.mult))
            dve.memset(RV66[:, :, E:E + 2], BIG)
            step(dve.tensor_tensor(RV66[:, :, 0:E], LG, gb_s[:, :].unsqueeze(1).broadcast_to([P, NB, E]), ALU.add))
            for blk in range(NB):
                ins = dve.max(top8[:, blk, :], RV66[:, blk, :])
            step(ins)
            for blk in range(NB):
                ins = dve.match_replace(RV66[:, blk, :], top8[:, blk, :], RV66[:, blk, :], -BIG)
            step(ins)
            step(dve.tensor_scalar(maskb, RV66[:, :, 0:E], -BIG, None, ALU.is_equal))
            dve.wait_ge(xna_copied, G)
            step(dve.memset(prevb[:, 0, :], 0.0))
            for blk in range(1, NB):
                ins = dve.tensor_tensor(prevb[:, blk, :], prevb[:, blk - 1, :], maskb[:, blk - 1, :], ALU.add)
                step(ins)
            dve.sem_inc(mask_ready, 1)
            dve.wait_ge(one_set, 1)
            for m in range(NB // 8):
                dve.wait_ge(pos_psum, m + 1)
                pos = PS[:, m, :].rearrange("p (a e) -> p a e", e=E)
                b8 = slice(8 * m, 8 * m + 8)
                step(dve.scalar_tensor_tensor(out=RD[:, b8, :], in0=pos, scalar=float(CAP), in1=maskb[:, b8, :],
                                              op0=ALU.is_lt, op1=ALU.mult))
                step(dve.tensor_tensor(RC[:, b8, :], pos, slot_s[:, :].unsqueeze(1).broadcast_to([P, 8, E]), ALU.add))
                step(dve.tensor_tensor(RC[:, b8, :], RC[:, b8, :], RD[:, b8, :], ALU.mult))
            dve.sem_inc(pos_read, 1)
            for blk in range(NB):
                ins = dve.max(top8[:, blk, :], RC[:, blk, :])
            step(ins)
            step(dve.tensor_scalar(RV66[:, :, 0:8], top8, 0.5, 2.0 * E * CAP, ALU.is_lt, ALU.mult))
            step(dve.tensor_tensor(RV66[:, :, 0:8], RV66[:, :, 0:8], top8, ALU.add))
            step(dve.tensor_scalar(RV66[:, :, 0:8], RV66[:, :, 0:8], -1.0, None, ALU.add))
            dve.tensor_copy(idx[:, :, :], RV66[:, :, 0:8]).then_inc(idx_ready, 1)
            step(dve.tensor_tensor(RD, RD, LG, ALU.mult))
            for k6 in range(TOPK):
                step(dve.tensor_tensor(RB, RC, top8[:, :, k6:k6 + 1].broadcast_to([P, NB, E]), ALU.is_equal))
                step(dve.tensor_tensor(RB, RB, RD, ALU.mult))
                step(dve.tensor_reduce(wts[:, k6, :], RB, AX.X, ALU.add))
            dve.sem_inc(wts_ready, 1)
            dve.memset(PS[:, 4, 0:256], 0.0)
            step(dve.memset(PS[:, 5, 0:256], 0.0))
            dve.sem_inc(psum_zeroed, 1)
            dve.wait_ge(pads_set, 1)

            def iteration(i, c, peeled):
                h = 4 * i + c
                on = lambda m: (not peeled) or 0 <= c + m < HEADS
                for s in range(SLOTS):
                    if on(1):
                        dve.wait_ge(s1_ready, SLOTS * (h + 1) + s + 1)
                        dst = accm[:, (c + 1) % 2, 512 * (s % 2):512 * (s % 2) + 512]
                        if s < 2:
                            wait(dve, accT_psum, h)
                            dve.tensor_copy(dst, PS[:, s % 2, :]).then_inc(s1_read, 1)
                        else:
                            dve.wait_ge(s1_read, SLOTS * (h + 1) + s - 1)
                            dve.tensor_tensor(dst, PS[:, s % 2, :], dst, ALU.max).then_inc(s1_read, 1)
                    if s == 0 and on(0):
                        dve.wait_ge(accT_psum, h + 1)

                        def hstep(ins, m):
                            ins.then_inc(max_step, 1)
                            dve.wait_ge(max_step, 6 * h + m)
                        hstep(dve.tensor_reduce(mx[:, 0, :], MISC.rearrange("p (a b) -> p a b", a=NJ), AX.X, ALU.max), 1)
                        wait(dve, mrow_psum, h)
                        hstep(dve.tensor_scalar(mx[:, 1, :], mx[:, 0, :], -1.0, None, ALU.mult), 2)
                        hstep(dve.tensor_copy(mparts[:, :, 0], mx[:, 1, :]), 3)
                        hstep(dve.tensor_tensor(mx[:, 2, :], mx[:, 1, :], mparts[:, :, 0], ALU.subtract), 4)
                        hstep(dve.tensor_copy(mparts[:, :, 1], mx[:, 2, :]), 5)
                        hstep(dve.tensor_tensor(mx[:, 3, :], mx[:, 2, :], mparts[:, :, 1], ALU.subtract), 6)
                        dve.tensor_copy(mparts[:, :, 2], mx[:, 3, :]).then_inc(mparts_ready, 1)
                    if s == 4 and on(0):
                        wait(dve, pv_done, NJ * (h - 1))
                        v = VR[:, bass.ds(batch_of(h), 1), bass.ds(h % H, 1), :, :].rearrange("p b h j d -> p (b h j) d")
                        t = TV[:, bass.ds(h % H, 1), :, :].rearrange("p h v d -> p (h v) d")
                        dve.tensor_tensor(Vst[:, c % 2, :, :, 0:HD], v.unsqueeze(2).broadcast_to([P, NJ, 8, HD]),
                                          t.unsqueeze(1).broadcast_to([P, NJ, 8, HD]), ALU.add).then_inc(v_ready, 1)
                    if s == 6 and on(-2):
                        hh = h - 2
                        dve.wait_ge(fin_psum, h - 1)
                        o = MISC[:, 0:128].rearrange("p (a b) -> p a b", a=NJ)
                        dve.reciprocal(rden[:, :], o[:, :, HD]).then_inc(rden_ready, 1)
                        dve.wait_ge(rden_ready, h - 1)
                        dst = ON[:, :, :].rearrange("p (b j) (h d) -> p b h j d", b=B, h=H)[
                            :, bass.ds(batch_of(hh), 1), bass.ds(hh % H, 1), :, :].rearrange("p b h j d -> p (b h j) d")
                        dve.tensor_tensor(dst, o[:, :, 0:HD], rden[:, :].unsqueeze(2).broadcast_to([P, NJ, HD]),
                                          ALU.mult).then_inc(on_ready, 1)
                    if s == 9 and on(2):
                        dve.wait_ge(aj_psum, h + 3)
                        wait(dve, aj_out, 16 * (h + 2))
                        dve.tensor_copy(aj_e[:, :, :].rearrange("p a b -> p (a b)"), MISC).then_inc(aj_copied, 1)
                    if s == 12 and on(-1):
                        dve.wait_ge(dp_psum, h)
                        wait(dve, dp_out, 16 * (h - 1))
                        dve.tensor_copy(dp_e[:, :], MISC).then_inc(dp_copied, 1)

            steps = iterations(dve, iteration)
            next(steps)
            hm = 2 + 4 * HALF_LOOPS
            dve.wait_ge(aj_out, 16 * (hm + 2))
            with dve.Fori(0, E // 4) as k:
                for p in range(2):
                    e = 2 * k + p
                    g_, t_ = dq_e[0:I, p * P:p * P + P], dq_e[0:I, 256 + p * P:256 + p * P + P]

                    def estep(ins, m):
                        ins.then_inc(ex_step, 1)
                        dve.wait_ge(ex_step, 3 * e + m)
                    dve.wait_ge(ex_e, e + 1)
                    estep(dve.tensor_scalar(t_, t_, 1.0, None, ALU.add), 1)
                    estep(dve.reciprocal(t_, t_), 2)
                    estep(dve.tensor_tensor(t_, PS[0:I, 7, 0:P], t_, ALU.mult), 3)
                    dve.tensor_tensor(g_, PS[0:I, 7, P:2 * P], t_, ALU.mult).then_inc(ex_g, 1)
                    dve.wait_ge(ex_y, e + 1)
                    dve.wait_ge(ex_out, 64 * k)
                    dve.tensor_copy(aj_e[0:CAP, 2 * p:2 * p + 2, :],
                                    PS[0:CAP, 6, P:3 * P].rearrange("p (m c) -> p m c", m=2)).then_inc(ex_yc, 1)
            dve.wait_ge(ex_out, 32 * (E // 2))
            for _ in steps:
                pass
            dve.wait_ge(y_added, 5 * NB + 1)
            dve.wait_ge(on_ready, HEADS)
            with dve.Fori(0, G) as g:
                dve.wait_ge(pj_T, g)
                dve.tensor_copy(accm[:, 0, 0:512].rearrange("p (a c) -> p a c", a=4), ON[:, bass.ds(g * 4, 4), :]).then_inc(on_st, 1)
                dve.wait_ge(pj_y, g + 1)
                dve.tensor_tensor(X[:, bass.ds(g * 4, 4), :], X[:, bass.ds(g * 4, 4), :],
                                  PS[:, 1, :].rearrange("p (a c) -> p a c", a=4), ALU.add).then_inc(pj_add, 1)


def kernel(**inputs):
    import numpy as np
    import concourse.bacc as bacc
    from concourse.bass_utils import run_bass_kernel_spmd

    a = {k.replace("L0_", ""): np.asarray(v) for k, v in inputs.items()}
    H, HD, NBK = a["attn_rpe_q_table"].shape
    C = H * HD
    E, D = a["ffn_gate_w"].shape
    I = a["ffn_w1"].shape[1]
    f32 = np.float32

    def by_distance(table, sign):
        return table[..., np.clip(sign * (np.arange(P) - (DIST // 2)), -31, 31) + 31]

    def stack_rows(table, sign):
        t = by_distance(table, sign).transpose(1, 0, 2)
        return np.repeat(t, COMBOS, axis=0).reshape(COMBOS * HD, H * P)

    def far(table, lower, upper):
        t = np.zeros((H, HD, 2, H), f32)
        for h in range(H):
            t[h, :, 0, h] = table[h, :, lower]
            t[h, :, 1, h] = table[h, :, upper]
        return t.reshape(C, 2 * H)

    wqkv = a["attn_w_qkv"]
    part = np.zeros((COMBOS * HD, 2, 3), f32)
    for r in range(COMBOS * HD):
        part[r, 0, K_PART[r % COMBOS]] = 1
        part[r, 1, Q_PART[r % COMBOS]] = 1
    vmask = np.zeros((2, 8, P), f32)
    for v in range(8):
        for s in range(4):
            k = value_kind(v, s)
            if k is not None:
                vmask[k, v, TILE * s:TILE * s + TILE] = 1
    kc = np.zeros((9, 2, 1024), f32)
    kc[0:6, 0] = 1
    kc[0:3, 1] = 1
    kc[6:9, 1] = 1
    kc = kc[:ROW_K - ROW_M]
    arrays = {
        "x": a["attn_x"],
        "wqkvg": np.concatenate([wqkv.T, a["ffn_gate_w"].T], axis=1),
        "w_proj": a["attn_w_proj"].T,
        "b_proj": a["attn_b_proj"].reshape(1, C),
        "rk_far": far(a["attn_rpe_k_table"], 0, NBK - 1),
        "rq_far": far(a["attn_rpe_q_table"], NBK - 1, 0),
        "rk_rows": stack_rows(a["attn_rpe_k_table"], -1),
        "rq_rows": stack_rows(a["attn_rpe_q_table"], 1),
        "rv_rows": by_distance(a["attn_rpe_v_table"].transpose(0, 2, 1), -1).transpose(2, 0, 1)[:DIST],
        "rv_far": np.stack([a["attn_rpe_v_table"][:, 0].reshape(C), a["attn_rpe_v_table"][:, NBK - 1].reshape(C)]),
        "gate_b": a["ffn_gate_b"].reshape(1, E),
        "w1": a["ffn_w1"].transpose(2, 0, 1),
        "w3": a["ffn_w3"].transpose(2, 0, 1),
        "w2": a["ffn_w2"].transpose(2, 0, 1),
        "ws1": a["ffn_ws1"].T,
        "ws3": a["ffn_ws3"].T,
        "ws2": a["ffn_ws2"].T.reshape(2, I, D),
        "ident_c": np.eye(P, dtype=f32),
        "tri_c": np.triu(np.ones((P, P), f32), 1),
        "part_c": part,
        "kconst_c": kc,
        "vmask_c": vmask.reshape(2, 8 * P),
        "slot_c": (np.arange(E) * 64 + 1).astype(f32).reshape(1, E),
    }
    nc = bacc.Bacc("TRN2", target_bir_lowering=False, num_devices=1)
    args, feed = [], {}
    for name, v in arrays.items():
        v = np.ascontiguousarray(v)
        feed[f"in_{name}"] = v
        args.append(nc.dram_tensor(f"in_{name}", v.shape, mybir.dt.from_np(v.dtype), kind="ExternalInput").ap())
    out = nc.dram_tensor("out_0", a["attn_x"].shape, F32, kind="ExternalOutput").ap()
    program(nc, *args, out)
    r = run_bass_kernel_spmd(nc, [feed], core_ids=[0])
    return r.results[0]["out_0"]
```

```python
from contextlib import ExitStack

import concourse.bass as bass
from concourse import mybir

F32 = mybir.dt.float32
BF16 = mybir.dt.bfloat16
I32 = mybir.dt.int32
ALU = mybir.AluOpType
ACT = mybir.ActivationFunctionType
AX = mybir.AxisListType

P = 128
COMBOS = 6
K_PART = [0, 0, 1, 1, 0, 2]
Q_PART = [0, 1, 0, 1, 2, 0]
TILE = 32
WIN = 3 * TILE
DIST = 4 * TILE - 1
ROW_M = 64
ROW_C = 67
ROW_K = 73
ROWS = 76
DROW = 1024 + 128
SLOTS = 16
LAG = 4
BIG = 1.0e30


def wait(eng, sem, value):
    if not isinstance(value, int) or value > 0:
        eng.wait_ge(sem, value)


def span(lo, hi, half):
    lo, hi = max(lo, 512 * half), min(hi, 512 * half + 512)
    return (lo, hi) if lo < hi else None


def value_variant(ti, J):
    r = ti - 4 * J
    return 1 if r <= -2 else 2 if r == -1 else 4 + r if r <= 3 else 3 if r == 4 else 0


def value_kind(variant, s):
    if variant == 0:
        return 0
    if variant == 1:
        return 1
    r = {2: -1, 3: 4}.get(variant, variant - 4)
    return None if abs(s - r) <= 1 else (0 if s < r else 1)


def program(nc, x, wqkvg, w_proj, b_proj, rk_far, rq_far, rk_dist, rq_dist, rv_rows, rv_far,
            gate_b, w1, w3, w2, ws1, ws3, ws2, ident_c, tri_c, kconst_c, vmask_c, slot_c, out):
    B, N, C = x.shape
    T = B * N
    NB = T // P
    G = T // 512
    H = 16
    HD = C // H
    HEADS = B * H
    NJ = N // P
    E = gate_b.shape[1]
    I = w1.shape[2]
    SC = float(HD) ** -0.5
    TOPK, CAP = 6, 64
    HALF_LOOPS = (HEADS - 4) // 8
    LOOPS = (HEADS - 4) // 4

    ctx = ExitStack()
    with ctx:
        def sb(name, shape, dt=F32):
            return ctx.enter_context(nc.sbuf_tensor(name, shape, dt))

        def sem(name):
            return ctx.enter_context(nc.semaphore(name))

        def dram(name, shape, dt=F32):
            return nc.dram_tensor(name, shape, dt, kind="Internal").ap()

        q_stack = dram("q_stack", [H * HD, COMBOS, T], BF16)
        k_stack = dram("k_stack", [H * HD, COMBOS, T], BF16)
        q_far = dram("q_far", [H, 9, T], BF16)
        k_far = dram("k_far", [H, 6, T], BF16)
        tab_stack = dram("tab_stack", [H * HD, COMBOS, 2, P], BF16)
        dq_d = dram("dq_d", [DIST, DROW])
        aj_d = dram("aj_d", [N, P])
        pa_d = dram("pa_d", [N, P])
        dp_d = dram("dp_d", [DIST, DROW])
        xb_d = dram("xb_d", [E * CAP, C])
        yb_d = dram("yb_d", [E * CAP, C])

        X = sb("X", [P, NB, C])
        XNA = sb("XNA", [P, NB, C])
        VR = sb("VR", [P, B, H, NJ, HD])
        ON = sb("ON", [P, max(NB, 32), C])
        TV = sb("TV", [P, H, 8, HD])
        PT = sb("PT", [P, TILE + NJ * N + TILE])
        accm = sb("accm", [P, 2, N])
        Qs = sb("Qs", [ROWS, 4, N], BF16)
        Ks = sb("Ks", [ROWS, 4, 2, N], BF16)
        Ksf = Ks[:, :, :, :].rearrange("p a b c -> p (a b c)")
        Qsf = Qs[:, :, :].rearrange("p a b -> p (a b)")
        tab = sb("tab", [ROWS, 4, 2, P], BF16)
        WT = sb("WT", [P, 4, NJ, WIN])
        Vst = sb("Vst", [P, 2, NJ, 8, 9])
        dq_e = sb("dq_e", [P, N])
        dq_s = sb("dq_s", [P, N])
        aj_e = sb("aj_e", [P, NJ, P])
        pa_s = sb("pa_s", [P, NJ, P])
        dp_e = sb("dp_e", [P, N])
        dp_s = sb("dp_s", [P, N])
        Oev = sb("Oev", [P, 2, 256])
        mx = sb("mx", [P, 4, NJ])
        mparts = sb("mparts", [P, NJ, 3], BF16)
        rden = sb("rden", [P, 4, 2])
        RVc = sb("RVc", [P, 2, HD])
        ident = sb("ident", [P, P])
        zcol = sb("zcol", [P, 1])
        identb = sb("identb", [P, P], BF16)
        RV = sb("RV", [P, H, HD])
        wp = sb("wp", [P, C])
        yg = sb("yg", [P, TOPK, C])
        idx = sb("idx", [P, NB, 8], I32)
        wts = sb("wts", [P, TOPK, NB])
        ew = sb("ew", [P, 2, 2 * 2 * I])
        ew2 = sb("ew2", [P, 2, 2 * C])
        exb = sb("exb", [P, 2, C])

        def cut(t, at, shape, dt=F32):
            n = 1
            for s in shape[1:]:
                n *= s
            w = n if dt == F32 else n // 2
            a = t[:, at:at + w]
            if dt != F32:
                a = a.bitcast(dt)
            names = " ".join("abcd"[:len(shape) - 1])
            kw = {"abcd"[k]: shape[k + 1] for k in range(len(shape) - 1)}
            return (a.rearrange(f"p ({names}) -> p {names}", **kw) if len(shape) > 2 else a), at + w

        at = 0
        LG, at = cut(PT, at, [P, NB, E])
        RB, at = cut(PT, at, [P, NB, E])
        RC, at = cut(PT, at, [P, NB, E])
        RD, at = cut(PT, at, [P, NB, E])
        ONf = ON[:, :, :].rearrange("p a b -> p (a b)")
        at = 0
        RV66, at = cut(ONf, at, [P, NB, E + 2])
        maskb, at = cut(ONf, at, [P, NB, E], BF16)
        assert at <= NB * C
        accf = accm[:, :, :].rearrange("p a b -> p (a b)")
        prevb, at = cut(accf, 0, [P, NB, E], BF16)
        pas = pa_s[:, :, :].rearrange("p a b -> p (a b)")
        XN, at = cut(accf, 0, [P, 4, C])
        XT, at = cut(accf, at, [P, 2, 512])
        QF, at = cut(accf, at, [P, 512])
        CF, QR = dq_e[:, 0:512], dq_e[:, 512:N]
        KR, CR = dp_e[:, 0:512], dp_e[:, 512:N]
        QP = [cut(dq_s, 0, [P, 3, 512], BF16)[0]]
        KP = [cut(dp_s, 0, [P, 3, 512], BF16)[0]]
        CP = [cut(pas, 0, [P, 3, 512], BF16)[0]]
        fz = 0
        QP1, fz = cut(ONf, fz, [P, 3, 512], BF16)
        KP1, fz = cut(ONf, fz, [P, 3, 512], BF16)
        CP1, fz = cut(ONf, fz, [P, 3, 512], BF16)
        QP.append(QP1)
        KP.append(KP1)
        CP.append(CP1)
        KF, fz = cut(ONf, fz, [P, 512])
        Z, fz = cut(ONf, fz, [P, 1024])
        aje = aj_e[:, :, :].rearrange("p a b -> p (a b)")
        EX, at = cut(aje, 0, [P, 2, 512])
        WTf = WT[:, :, :, :].rearrange("p a b c -> p (a b c)")
        at = 0
        HG, at = cut(WTf, at, [P, 2, 512])
        wq_s, at = cut(WTf, at, [P, 3 * C + E])
        ws1_s, at = cut(WTf, at, [P, 2 * I])
        ws3_s, at = cut(WTf, at, [P, 2 * I])
        ws2_s, at = cut(WTf, at, [P, 2, C])
        bp_s, at = cut(WTf, at, [P, C])
        cqk, at = cut(WTf, at, [P, 2, 2 * H])
        st6, at = cut(WTf, at, [P, NB, 6])
        mean, at = cut(WTf, at, [P, NB])
        rstd, at = cut(WTf, at, [P, NB])
        tmpn, at = cut(WTf, at, [P, 2, NB])
        assert at <= 3072
        ygf = yg[:, :, :].rearrange("p a b -> p (a b)")
        at = 0
        gb_s, at = cut(ygf, at, [P, E])
        slot_s, at = cut(ygf, at, [P, E])
        trib, at = cut(ygf, at, [P, P], BF16)
        oneb, at = cut(ygf, at, [P, P], BF16)
        rmax, at = cut(ygf, at, [P, NB])
        rsum, at = cut(ygf, at, [P, NB])
        top8, at = cut(ygf, at, [P, NB, 8])
        assert at <= TOPK * C
        vm_s = dp_s[0:2, 0:8 * P]
        ewf = ew[:, :, :].rearrange("p a b -> p (a b)")
        rvf_s = ewf[0:2, 0:C]
        tres = exb
        tprt, _ = cut(ew2[:, :, :].rearrange("p a b -> p (a b)"), 0, [P, 3, 2, P], BF16)

        PS = ctx.enter_context(nc.psum_tensor("PS", [P, 8, 512], F32))
        MISC = PS[:, 6:8, :].rearrange("p a b -> p (a b)")

        w_in, x_in, c_in, tabs_in = sem("w_in"), sem("x_in"), sem("c_in"), sem("tabs_in")
        zero_set, one_set, zeros_out, zcol_set, k_zeroed = (
            sem("zero_set"), sem("one_set"), sem("zeros_out"), sem("zcol_set"), sem("k_zeroed"))
        psum_zeroed, pads_set, kconst_in = sem("psum_zeroed"), sem("pads_set"), sem("kconst_in")
        dve_step, cut_step, tab_step = sem("dve_step"), sem("cut_step"), sem("tab_step")
        bn_done, max_step, rden_ready = sem("bn_done"), sem("max_step"), sem("rden_ready")
        stats_ready, rstd_ready = sem("stats_ready"), sem("rstd_ready")
        xn_ready, xna_copied = sem("xn_ready"), sem("xna_copied")
        xt_psum, xt_ready, qk_psum, qf_ready, kf_ready = (
            sem("xt_psum"), sem("xt_ready"), sem("qk_psum"), sem("qf_ready"), sem("kf_ready"))
        vg_psum, vg_copied = sem("vg_psum"), sem("vg_copied")
        sh_psum, sh_exp, sh_ready, z_psum, z_added = (
            sem("sh_psum"), sem("sh_exp"), sem("sh_ready"), sem("z_psum"), sem("z_added"))
        c_psum, cf_ready, cqk_scaled = sem("c_psum"), sem("cf_ready"), sem("cqk_scaled")
        q_cut, k_cut, c_cut, stacks_out = sem("q_cut"), sem("k_cut"), sem("c_cut"), [sem("stacks_out0"), sem("stacks_out1")]
        tv_psum, tv_ready, tabs_cut, tabs_out = (
            sem("tv_psum"), sem("tv_ready"), sem("tabs_cut"), sem("tabs_out"))
        route_max, route_exp, mask_ready, pos_psum, pos_read, idx_ready, wts_ready = (
            sem("route_max"), sem("route_exp"), sem("mask_ready"), sem("pos_psum"), sem("pos_read"),
            sem("idx_ready"), sem("wts_ready"))
        stack_in = [sem(f"stack_in{r}") for r in range(4)]
        wt_in = [sem(f"wt_in{r}") for r in range(4)]
        s1_ready, s1_read, s2_ready, s2_read = (
            sem("s1_ready"), sem("s1_read"), sem("s2_ready"), sem("s2_read"))
        accT_psum, mparts_ready, mrow_psum, mrow_ready = (
            sem("accT_psum"), sem("mparts_ready"), sem("mrow_psum"), sem("mrow_ready"))
        dq_psum, dq_copied, dq_out, dq_in = sem("dq_psum"), sem("dq_copied"), sem("dq_out"), sem("dq_in")
        aj_psum, aj_copied, aj_out = sem("aj_psum"), sem("aj_copied"), sem("aj_out")
        pa_out = [sem("pa_out0"), sem("pa_out1")]
        pa_in = sem("pa_in")
        dp_psum, dp_copied, dp_out, dp_in = sem("dp_psum"), sem("dp_copied"), sem("dp_out"), sem("dp_in")
        v_ready, pv_done, o_copied, fin_psum, on_ready = (
            sem("v_ready"), sem("pv_done"), sem("o_copied"), sem("fin_psum"), sem("on_ready"))
        scattered, ew_in, ex_T, ex_Tc, ex_h, ex_e, ex_g, ex_y, ex_yc, ex_out = (
            sem("scattered"), [sem("ew_in0"), sem("ew_in1")], sem("ex_T"), sem("ex_Tc"), sem("ex_h"),
            sem("ex_e"), sem("ex_g"), sem("ex_y"), sem("ex_yc"), sem("ex_out"))
        ex_step = sem("ex_step")
        rel_done, rv_ready, ajk_psum, ajk_copied = sem("rel_done"), sem("rv_ready"), sem("ajk_psum"), sem("ajk_copied")
        gathered, y_added = sem("gathered"), sem("y_added")
        on_st, pj_T, pj_Tc, pj_y, pj_add, stored = (
            sem("on_st"), sem("pj_T"), sem("pj_Tc"), sem("pj_y"), sem("pj_add"), sem("stored"))

        def live(h, c):
            return c is None or 0 <= h < HEADS

        def iterations(eng, body):
            for h in range(-3, 2):
                body(0, h, True)
            with eng.Fori(0, HALF_LOOPS) as i:
                for r in range(4):
                    body(i, 2 + r, False)
            yield
            with eng.Fori(HALF_LOOPS, LOOPS) as i:
                for r in range(4):
                    body(i, 2 + r, False)
            for h in range(HEADS - 2, HEADS + 2):
                body(0, h, True)

        def groups(eng, body):
            for g in range(2):
                body(g, g % 2, 0)
            with eng.Fori(1, max(1, G // 2 - 1)) as k:
                for p in range(2):
                    body(2 * k + p, p, k)
            for g in range(max(2, G - 2), G):
                body(g, g % 2, g // 2)

        def after(g, n=1):
            return not isinstance(g, int) or g + n < G

        def batch_of(h):
            b = h // H
            return b if isinstance(h, int) else nc.s_assert_within(
                b, 0, B - 1, skip_runtime_bounds_check_because="the loops' heads are below HEADS")

        def rows(t, offset, pattern):
            return bass.AP(t.tensor, offset, pattern)

        STORES = 16 * (3 + 3 + 4)
        ZEROS = 16 * (5 + E * CAP // 1024 + 3 * (T // 1024))

        block = ctx.enter_context(nc.Block())

        @block.sync
        def _(sp):
            def parts_out(dst, src, part, sem_):
                for n in range(0, COMBOS, 2):
                    a, b = part[n], part[n + 1]
                    s = src[:, a:a + 1, :].ap
                    view = bass.AP(src.tensor, src[:, a:a + 1, :].offset,
                                   [list(s[0]), [(b - a) * src.ap[1][0], 2], list(s[-1])])
                    sp.dma_start(dst[:, n:n + 2, :], view).then_inc(sem_, 16)

            xv = x.rearrange("b (j p) c -> p (b j) c", p=P)
            for g in range(4):
                n = NB // 4
                sp.dma_start(X[:, n * g:n * g + n, :], xv[:, n * g:n * g + n, :]).then_inc(x_in, 16)
            for dst, src in ((tres[:, 0, :], rk_dist), (tres[:, 1, :], rq_dist), (ident[:, :], ident_c)):
                sp.dma_start(dst, src).then_inc(tabs_in, 16)
            for dst, src in ((wq_s, wqkvg), (ws1_s, ws1), (ws3_s, ws3), (wp[:, :], w_proj),
                             (cqk[:, 0, :], rk_far), (cqk[:, 1, :], rq_far)):
                sp.dma_start(dst, src).then_inc(w_in, 16)
            sp.dma_start(ws2_s[0:I], ws2.rearrange("c i d -> i c d")).then_inc(w_in, 16)
            sp.dma_start(RV[0:DIST, :, :], rv_rows).then_inc(w_in, 16)
            sp.dma_start(bp_s, b_proj.partition_broadcast(P)).then_inc(w_in, 16)
            sp.dma_start(gb_s, gate_b.partition_broadcast(P)).then_inc(w_in, 16)
            sp.dma_start(slot_s, slot_c.partition_broadcast(P)).then_inc(w_in, 16)
            sp.dma_start(vm_s, vmask_c).then_inc(w_in, 16)
            sp.dma_start(rvf_s, rv_far).then_inc(w_in, 16)
            sp.wait_ge(tabs_cut, 1)
            parts_out(tab_stack[:, :, 0, :], tprt[:, :, 0, :], K_PART, tabs_out)
            parts_out(tab_stack[:, :, 1, :], tprt[:, :, 1, :], Q_PART, tabs_out)
            sp.wait_ge(zero_set, 1)
            sp.dma_start(dq_d[:, 0:N], Z[0:DIST, :]).then_inc(zeros_out, 16)
            sp.dma_start(dq_d[:, N:DROW], Z[0:DIST, 0:P]).then_inc(zeros_out, 16)
            sp.dma_start(dp_d[:, 0:N], Z[0:DIST, :]).then_inc(zeros_out, 16)
            sp.dma_start(dp_d[:, N:DROW], Z[0:DIST, 0:P]).then_inc(zeros_out, 16)
            sp.dma_start(pa_d.rearrange("(a p) n -> p a n", p=P), Z[:, :].rearrange("p (a n) -> p a n", n=P)).then_inc(zeros_out, 16)
            for n in range(E * CAP // 1024):
                sp.dma_start(xb_d[n * 1024:(n + 1) * 1024, :].rearrange("(p a) n -> p (a n)", p=P),
                             Z[:, :]).then_inc(zeros_out, 16)
            Zb = Z[0:H, :].bitcast(BF16)
            for n in range(3):
                for m in range(T // 1024):
                    sp.dma_start(q_far[:, n, m * 1024:(m + 1) * 1024], Zb[:, 0:1024]).then_inc(zeros_out, 16)

            def stores(g, p, k2):
                tok = bass.ds(g * 512, 512)
                sp.wait_ge(q_cut, g + 1)
                parts_out(q_stack[:, :, tok], QP[p], Q_PART, stacks_out[p])
                sp.wait_ge(k_cut, g + 1)
                parts_out(k_stack[:, :, tok], KP[p], K_PART, stacks_out[p])
                sp.wait_ge(c_cut, g + 1)
                for m in range(2):
                    sp.dma_start(q_far[:, 3 + 3 * m:6 + 3 * m, tok], CP[p][16 * m:16 * m + 16, :, :]).then_inc(stacks_out[p], 16)
                    sp.dma_start(k_far[:, 3 * m:3 * m + 3, tok], CP[p][32 + 16 * m:48 + 16 * m, :, :]).then_inc(stacks_out[p], 16)

            groups(sp, stores)
            sp.wait_ge(zeros_out, ZEROS)
            for p in range(2):
                sp.wait_ge(stacks_out[p], STORES * (G // 2))
            sp.wait_ge(tabs_out, 96)
            sp.wait_ge(pads_set, 1)
            sp.wait_ge(kconst_in, 64)
            sp.wait_ge(wts_ready, 1)

            def load_stacks(i, c):
                h, r = (4 * i + c) % HEADS, c % 4
                b, hh = batch_of(h), h % H
                tok = bass.ds(b * N, N)
                qs = q_stack.rearrange("(h d) n t -> h (d n) t", h=H)[bass.ds(hh, 1), :, tok].rearrange("a n t -> (a n) t")
                sp.dma_start(Qs[0:48, r, :], qs).then_inc(stack_in[r], 16)
                sp.dma_start(Qs[ROW_M:ROW_M + 9, r, :], q_far[bass.ds(hh, 1), :, tok].rearrange("a n t -> (a n) t")
                             ).then_inc(stack_in[r], 16)
                ks = k_stack.rearrange("(h d) n t -> h (d n) t", h=H)[bass.ds(hh, 1), :, tok].rearrange("a n t -> (a n) t")
                kf = k_far[bass.ds(hh, 1), :, tok].rearrange("a (v n) t -> n (a v) t", v=2)
                for v in range(2):
                    sp.dma_start(Ks[0:48, r, v, :], ks).then_inc(stack_in[r], 16)
                sp.dma_start(Ks[ROW_K:ROWS, r, :, :], kf).then_inc(stack_in[r], 16)
                sp.dma_start(tab[0:48, r, :, :],
                             tab_stack.rearrange("(h d) n v p -> h (d n) v p", h=H)[bass.ds(hh, 1), :, :, :].rearrange(
                                 "a n v p -> (a n) v p")).then_inc(stack_in[r], 16)

            def shear(s, J0, J1, t):
                return rows(t, (P * J0 + TILE * s) * P + TILE - 1,
                            [[P - 1, TILE], [P * P, J1 - J0], [1, WIN]])

            def window_out(c, i, part):
                h = 4 * i + c
                sp.wait_ge(s2_read, SLOTS * h + 8 * part + 8)
                wait(sp, pa_in, 16 * h)
                for s in range(4):
                    src = rows(PT[:, :], 0, PT[TILE * s:TILE * s + TILE, 0:1].ap)
                    base = PT[TILE * s:TILE * s + TILE, TILE * s + 4 * part * (N + P):TILE * s + 4 * part * (N + P) + WIN]
                    src = rows(base, base.offset, [list(base.ap[0]), [N + P, 4], [1, WIN]])
                    sp.dma_start(shear(s, 4 * part, 4 * part + 4, pa_d), src).then_inc(pa_out[part], 16)

            def iteration(i, c, peeled):
                h = 4 * i + c
                on = lambda n: (not peeled) or 0 <= c + n < HEADS
                if on(-1):
                    window_out(c - 1, i, 1)
                if on(3):
                    wait(sp, s2_ready, SLOTS * h)
                    load_stacks(i, c + 3)
                if on(2):
                    sp.wait_ge(aj_copied, 2 * h + 6)
                    if not peeled or c + 1 >= 0:
                        sp.wait_ge(wt_in[(c + 1) % 4], 64 * (i + (c + 1) // 4 + 1))
                    sp.dma_start(aj_d.rearrange("(a p) n -> p a n", p=P), aj_e[:, :, :]).then_inc(aj_out, 16)
                if on(-1):
                    sp.wait_ge(pa_out[0], 64 * h)
                    sp.wait_ge(pa_out[1], 64 * h)
                    wait(sp, dp_psum, h - 1)
                    sp.dma_start(pa_s[:, :, :], pa_d.rearrange("(a p) n -> p a n", p=P)).then_inc(pa_in, 16)
                if on(2):
                    sp.wait_ge(aj_out, 16 * (h + 3))
                    wait(sp, s2_ready, SLOTS * (h - 1))
                    for s in range(4):
                        sp.dma_start(WT[TILE * s:TILE * s + TILE, (c + 2) % 4, :, :],
                                     shear(s, 0, NJ, aj_d)).then_inc(wt_in[(c + 2) % 4], 16)
                if on(0):
                    window_out(c, i, 0)
                if on(-1):
                    sp.wait_ge(dp_copied, h)
                    wait(sp, dp_in, 16 * (h - 1))
                    sp.dma_start(dp_d[:, 64:64 + N], dp_e[0:DIST, :]).then_inc(dp_out, 16)
                    sp.wait_ge(dp_out, 16 * h)
                    wait(sp, rel_done, h - 1)
                    sp.dma_start(dp_s[0:DIST, :], rows(dp_d, DIST, [[DROW - 1, DIST], [1, N]])).then_inc(dp_in, 16)
                if on(3):
                    sp.wait_ge(dq_copied, h + 4)
                    wait(sp, dq_in, 16 * (h + 3))
                    sp.dma_start(dq_d[:, 64:64 + N], dq_e[0:DIST, :]).then_inc(dq_out, 16)
                    sp.wait_ge(dq_out, 16 * (h + 4))
                    wait(sp, aj_psum, 2 * h + 6)
                    sp.dma_start(dq_s[0:DIST, :], rows(dq_d, 1, [[DROW + 1, DIST], [1, N]])).then_inc(dq_in, 16)

            steps = iterations(sp, iteration)
            next(steps)
            sp.wait_ge(scattered, 16 * NB * TOPK)

            def load_pair(p, e):
                sp.dma_start(exb[:, p, :], xb_d[bass.ds(e * 2 * CAP, 2 * CAP), :]).then_inc(ew_in[p], 16)
                sp.dma_start(ew[:, p, 0:2 * I].rearrange("p (a i) -> p a i", a=2), w1[:, bass.ds(e * 2, 2), :]).then_inc(ew_in[p], 16)
                sp.dma_start(ew[:, p, 2 * I:4 * I].rearrange("p (a i) -> p a i", a=2), w3[:, bass.ds(e * 2, 2), :]).then_inc(ew_in[p], 16)
                sp.dma_start(ew2[0:I, p, :].rearrange("p (a i) -> p a i", a=2), w2[:, bass.ds(e * 2, 2), :]).then_inc(ew_in[p], 16)

            load_pair(0, 0)
            load_pair(1, 1)
            with sp.Fori(0, E // 4) as k:
                for p in range(2):
                    e = 2 * k + p
                    sp.wait_ge(ex_yc, e + 1)
                    for m in range(2):
                        sp.dma_start(yb_d[bass.ds((2 * e + m) * CAP, CAP), :],
                                     aj_e[0:CAP, 2 * p + m, :]).then_inc(ex_out, 16)
                    nxt = 2 * ((k + 1) % (E // 4)) + p
                    load_pair(p, nxt)
            sp.wait_ge(ex_out, 32 * (E // 2))
            for p in range(2):
                sp.wait_ge(ew_in[p], 64 * (E // 4 + 1))
            for _ in steps:
                pass
            sp.wait_ge(stack_in[0], 96 * (HEADS // 4 + 1))
            sp.wait_ge(dq_in, 16 * (HEADS + 1))
            ov = out.rearrange("b (j p) c -> p (b j) c", p=P)
            with sp.Fori(0, G) as g:
                sp.wait_ge(pj_add, g + 1)
                sp.dma_start(ov[:, bass.ds(g * 4, 4), :], X[:, bass.ds(g * 4, 4), :]).then_inc(stored, 16)
            sp.wait_ge(stored, 16 * G)

        @block.gpsimd
        def _(pool):
            pool.memset(Z, 0.0).then_inc(zero_set, 1)
            pool.dma_start(trib, tri_c).then_inc(c_in, 16)
            pool.memset(oneb, 1.0).then_inc(one_set, 1)
            pool.memset(Ks[:, :, :, :], 0.0).then_inc(k_zeroed, 1)
            pool.wait_ge(k_zeroed, 1)
            for r in range(4):
                pool.dma_start(Ks[ROW_M:ROW_K, r, :, :], kconst_c).then_inc(kconst_in, 16)
            pool.memset(Qs[:, :, :], 1.0)
            pool.memset(tab[:, :, :, :], 0.0)
            for J in range(2):
                pool.memset(Vst[:, J, :, :, :], 1.0)
            pool.memset(zcol[:, :], 0.0).then_inc(zcol_set, 1)
            pool.wait_ge(zcol_set, 1)
            zero_row = zcol[:, :].broadcast_to([P, 512])
            pool.wait_ge(c_in, 16)

            def group(g, p, k2):
                pool.wait_ge(xn_ready, g + 1)
                pool.tensor_copy(XNA[:, bass.ds(g * 4, 4), :], XN).then_inc(xna_copied, 1)
                for m, (F, R, Pt, rdy, done, np_) in enumerate(
                        ((KF, KR, KP[p], kf_ready, k_cut, P), (CF, CR, CP[p], cf_ready, c_cut, 64))):
                    def gstep(ins, k):
                        ins.then_inc(cut_step, 1)
                        pool.wait_ge(cut_step, g * 6 + (3 * m + k))

                    pool.wait_ge(rdy, g + 1)
                    gstep(pool.tensor_tensor(R[0:np_, :], F[0:np_, :], Pt[0:np_, 0, :], ALU.subtract), 1)
                    gstep(pool.tensor_tensor(Pt[0:np_, 1, :], R[0:np_, :], zero_row[0:np_, :], ALU.add), 2)
                    gstep(pool.tensor_tensor(R[0:np_, :], R[0:np_, :], Pt[0:np_, 1, :], ALU.subtract), 3)
                    pool.tensor_tensor(Pt[0:np_, 2, :], R[0:np_, :], zero_row[0:np_, :], ALU.add).then_inc(done, 1)

            groups(pool, group)
            pool.wait_ge(wts_ready, 1)
            pool.memset(PT[:, 0:TILE], 0.0)
            pool.memset(PT[:, TILE + NJ * N:], 0.0).then_inc(pads_set, 1)
            pool.wait_ge(idx_ready, 1)
            pool.wait_ge(xna_copied, G)
            for blk in range(NB):
                for k in range(TOPK):
                    pool.indirect_dma_start(
                        out=xb_d, out_offset=bass.IndirectOffsetOnAxis(ap=idx[:, blk, k:k + 1], axis=0),
                        in_=XNA[:, blk, :], in_offset=None, bounds_check=E * CAP - 1, oob_is_err=False,
                    ).then_inc(scattered, 16)
            pool.wait_ge(ex_out, 32 * (E // 2))
            pool.memset(yg[:, :, :], 0.0).then_inc(y_added, 1)
            for blk in range(NB):
                def ystep(m, *a):
                    pool.tensor_tensor(*a).then_inc(y_added, 1)
                    pool.wait_ge(y_added, 5 * blk + m + 1)

                pool.wait_ge(y_added, 5 * blk + 1)
                for k in range(TOPK):
                    pool.indirect_dma_start(
                        out=yg[:, k, :], out_offset=None, in_=yb_d,
                        in_offset=bass.IndirectOffsetOnAxis(ap=idx[:, blk, k:k + 1], axis=0),
                        bounds_check=E * CAP - 1, oob_is_err=False,
                    ).then_inc(gathered, 16)
                pool.wait_ge(gathered, 16 * TOPK * (blk + 1))
                ystep(1, yg[:, :, :], yg[:, :, :], wts[:, :, blk:blk + 1].broadcast_to([P, TOPK, C]), ALU.mult)
                ystep(2, yg[:, 0:3, :], yg[:, 0:3, :], yg[:, 3:6, :], ALU.add)
                ystep(3, yg[:, 0, :], yg[:, 0, :], yg[:, 1, :], ALU.add)
                ystep(4, yg[:, 0, :], yg[:, 0, :], yg[:, 2, :], ALU.add)
                ystep(5, X[:, blk, :], X[:, blk, :], yg[:, 0, :], ALU.add)

        @block.tensor
        def _(pe):
            def mm(o, l, r, start=True, stop=True):
                return pe.matmul(o, l, r, start=start, stop=stop, skip_group_check=True)

            pe.sem_inc(fin_psum, 1)
            pe.wait_ge(w_in, 16 * 13)
            pe.wait_ge(tabs_in, 48)
            for v in range(8):
                ins = mm(PS[:, v // 4, (v % 4) * P:(v % 4 + 1) * P], vm_s[:, v * P:(v + 1) * P], rvf_s,
                         start=v % 4 == 0)
            ins.then_inc(tv_psum, 1)
            pe.wait_ge(tv_ready, 1)
            pe.wait_ge(cqk_scaled, 1)

            def transposes(g):
                pe.wait_ge(xn_ready, g + 1)
                wait(pe, z_added, g - 1)
                for q in range(4):
                    ins = pe.transpose(PS[:, 0, q * P:(q + 1) * P], XN[:, q, :], ident[:, :])
                ins.then_inc(xt_psum, 1)

            def shared_out(g):
                pe.wait_ge(sh_ready, 2 * g + 2)
                for q in range(4):
                    for a in range(2):
                        ins = mm(PS[:, 0, q * P:(q + 1) * P], HG[0:I, a, q * P:(q + 1) * P], ws2_s[0:I, a, :],
                                 start=q == 0 and a == 0, stop=a == 1)
                ins.then_inc(z_psum, 1)

            def group(g, p, k2):
                XTp = XT[:, p, :]
                pe.wait_ge(xt_ready, g + 1)
                wait(pe, cf_ready, g)
                mm(PS[:, 1, :], wq_s[:, 0:C], XTp).then_inc(qk_psum, 1)
                wait(pe, vg_copied, g)
                for q in range(4):
                    ins = mm(PS[:, 3 + q // 2, (q % 2) * 192:(q % 2) * 192 + 192], XT[:, p, q * P:(q + 1) * P],
                             wq_s[:, 2 * C:3 * C + E], start=q % 2 == 0)
                ins.then_inc(vg_psum, 1)
                if not isinstance(g, int) or g > 0:
                    shared_out(g - 1)
                mm(PS[:, 2, :], wq_s[:, C:2 * C], XTp).then_inc(qk_psum, 1)
                mm(PS[0:I, 5, :], ws1_s[:, 0:I], XTp)
                mm(PS[0:I, 6, :], ws3_s[:, 0:I], XTp).then_inc(sh_psum, 1)
                mm(PS[0:I, 7, :], ws1_s[:, I:2 * I], XTp)
                pe.wait_ge(kf_ready, g + 1)
                mm(PS[0:I, 2, :], ws3_s[:, I:2 * I], XTp).then_inc(sh_psum, 1)
                if after(g):
                    transposes(g + 1)
                pe.wait_ge(qf_ready, g + 1)
                mm(PS[0:32, 1, :], cqk[:, 0, :], QF)
                mm(PS[32:64, 1, :], cqk[:, 1, :], KF).then_inc(c_psum, 1)

            transposes(0)
            groups(pe, group)
            shared_out(G - 1)
            pe.wait_ge(mask_ready, 1)
            pe.wait_ge(z_added, G)
            for m in range(NB // 8):
                mm(PS[:, m, :], trib, maskb[:, 8 * m:8 * m + 8, :].rearrange("p a e -> p (a e)"), stop=False)
                mm(PS[:, m, :], oneb, prevb[:, 8 * m:8 * m + 8, :].rearrange("p a e -> p (a e)"),
                   start=False).then_inc(pos_psum, 1)
            pe.wait_ge(pos_read, 1)
            pe.wait_ge(psum_zeroed, 1)

            def bias(bank, half, J, r):
                ins = None
                for s in range(4):
                    t = 4 * J + s
                    w = span(TILE * (t - 1), TILE * (t + 2), half)
                    w = w and (max(w[0], 0), min(w[1], N))
                    if w and w[0] < w[1]:
                        a = w[0] - TILE * (t - 1)
                        ins = mm(PS[TILE * s:TILE * s + TILE, bank, w[0] - 512 * half:w[1] - 512 * half],
                                 ident[:, TILE * s:TILE * s + TILE], WT[:, r, J, a:a + w[1] - w[0]], start=False)
                return ins

            def scores(bank, half, J, r):
                pieces = []
                for s in range(4):
                    t = 4 * J + s
                    own = []
                    for kind, lo, hi in (("U", 0, TILE * (t - 1)), ("W", max(0, TILE * (t - 1)), min(N, TILE * (t + 2))),
                                         ("L", TILE * (t + 2), N)):
                        w = span(lo, hi, half)
                        if w:
                            own.append((s, kind, w, not own))
                    pieces.append(own)
                for n in range(3):
                    for own in pieces:
                        if n < len(own):
                            s, kind, w, first = own[n]
                            k = ROWS if kind != "W" else ROW_C
                            ins = mm(
                               PS[TILE * s:TILE * s + TILE, bank, w[0] - 512 * half:w[1] - 512 * half],
                               Ks[0:k, r, 1 if kind == "U" else 0, P * J + TILE * s:P * J + TILE * s + TILE],
                               Qs[0:k, r, w[0]:w[1]], start=first)
                return bias(bank, half, J, r) or ins

            def unit(i, c, u, which):
                h, r = 4 * i + c, c % 4
                ready, read, bank = ((s1_ready, s1_read, 0), (s2_ready, s2_read, 2))[which]
                if which == 0 and u == 0:
                    pe.wait_ge(stack_in[r], 96 * (i + c // 4 + 1))
                    pe.wait_ge(wt_in[r], 64 * (i + c // 4 + 1))
                if which == 1 and u == 0:
                    pe.wait_ge(mrow_ready, h + 1)
                wait(pe, read, SLOTS * h + u - 1)
                J, half = u // 2, u % 2
                scores(bank + u % 2, half, J, r).then_inc(ready, 1)

            def values(i, c, J):
                h, p = 4 * i + c, c % 2
                pe.wait_ge(s2_read, SLOTS * h + 2 * J + 2)
                if J == 0:
                    pe.wait_ge(v_ready, h + 1)
                    wait(pe, o_copied, h - 1)
                own = []
                for q in range(4):
                    mine, t = [], 8 * q
                    while t < 8 * q + 8:
                        v, e = value_variant(t, J), t
                        while e < 8 * q + 8 and value_variant(e, J) == v:
                            e += 1
                        mine.append((q, v, t, e))
                        t = e
                    own.append(mine)
                for n in range(max(map(len, own))):
                    for mine in own:
                        if n < len(mine):
                            q, v, t, e = mine[n]
                            ins = mm(PS[TILE * q:TILE * q + 9, 4 + p, TILE * (t - 8 * q):TILE * (e - 8 * q)],
                                     Vst[:, p, J, v, :], PT[:, TILE + N * J + TILE * t:TILE + N * J + TILE * e],
                                     start=J == 0 and n == 0, stop=J == NJ - 1)
                ins.then_inc(pv_done, 1)

            def misc_free(h, *which):
                for s, v, *per in which:
                    most = HEADS + (s is dq_copied)
                    wait(pe, s, (per[0] if per else 1) * (v if not isinstance(v, int) else min(v, most)))

            def iteration(i, c, peeled):
                h = 4 * i + c
                on = lambda n: (not peeled) or 0 <= c + n < HEADS
                for s in range(SLOTS):
                    if s == 3 and on(0):
                        pe.wait_ge(mparts_ready, h + 1)
                        for I_ in range(NJ):
                            ins = mm(MISC[0:3, I_ * P:(I_ + 1) * P], mparts[:, I_, :], identb[:, :], start=I_ % 4 == 0)
                        ins.then_inc(mrow_psum, 1)
                    if on(1):
                        unit(i, c + 1, s, 0)
                    if s == 0 and on(0):
                        pe.wait_ge(s1_read, SLOTS * h + SLOTS)
                        misc_free(h, (dp_copied, h - 1), (dq_copied, h + 3))
                        for I_ in range(NJ):
                            ins = pe.transpose(MISC[:, I_ * P:(I_ + 1) * P], accm[:, c % 2, I_ * P:(I_ + 1) * P], ident[:, :])
                        ins.then_inc(accT_psum, 1)
                    if s == 14 and on(3):
                        r = (c + 3) % 4
                        pe.wait_ge(stack_in[r], 96 * (i + (c + 3) // 4 + 1))
                        misc_free(h, (mrow_ready, h + 1), (on_ready, h - 1), (aj_copied, h + 3, 2), (dp_copied, h))
                        for a in range(2):
                            ins = mm(MISC[:, 512 * a:512 * a + 512], tab[:, r, 0, :], Qs[:, r, 512 * a:512 * a + 512])
                        ins.then_inc(dq_psum, 1)
                    if s >= LAG and on(0):
                        unit(i, c, s - LAG, 1)
                    if s < LAG and on(-1):
                        unit(i, c - 1, s + SLOTS - LAG, 1)
                    if s == 3 and on(-2):
                        pe.wait_ge(dp_in, 16 * (h - 1))
                        pe.wait_ge(rv_ready, h - 1)
                        for q in range(4):
                            ins = mm(PS[TILE * q:TILE * q + HD, 4 + c % 2, 0:256], RVc[0:DIST, c % 2, :],
                                     dp_s[0:DIST, 256 * q:256 * q + 256], start=False)
                        ins.then_inc(rel_done, 1)
                    if s == 9 and on(-2):
                        misc_free(h, (aj_copied, h + 3, 2), (mrow_ready, h + 1))
                        pe.wait_ge(o_copied, h - 1)
                        for a in range(2):
                            ins = pe.transpose(MISC[:, a * P:a * P + P], Oev[:, c % 2, a * P:a * P + P], ident[:, :])
                        ins.then_inc(fin_psum, 1)
                    if s in (5, 7) and on(2):
                        r, part = (c + 2) % 4, (s - 5) // 2
                        if part == 0:
                            misc_free(h, (mrow_ready, h + 1), (dq_copied, h + 3))
                            pe.wait_ge(dq_in, 16 * (h + 3))
                        else:
                            pe.wait_ge(aj_copied, 2 * h + 5)
                        for a in range(4):
                            J = 4 * part + a
                            ins = mm(PS[:, 7, a * P:(a + 1) * P], Ks[:, r, 0, J * P:(J + 1) * P], tab[:, r, 1, :],
                                     start=a == 0)
                        ins.then_inc(ajk_psum, 1)
                        for a in range(4):
                            J = 4 * part + a
                            ins = pe.transpose(PS[:, 6, a * P:a * P + DIST], dq_s[0:DIST, J * P:(J + 1) * P],
                                               ident[0:DIST, 0:DIST])
                        ins.then_inc(aj_psum, 1)
                    if s == 12 and on(-1):
                        misc_free(h, (aj_copied, h + 3, 2), (on_ready, h - 1))
                        pe.wait_ge(pa_in, 16 * h)
                        for J in range(NJ):
                            ins = pe.transpose(MISC[:, J * P:(J + 1) * P], pa_s[:, J, :], ident[:, :])
                        ins.then_inc(dp_psum, 1)
                    if s % 2 and s >= LAG + 3 and on(0):
                        values(i, c, (s - LAG - 3) // 2)
                    if s % 2 and s < LAG + 3 and on(-1):
                        values(i, c - 1, (s - LAG - 3 + SLOTS) // 2)

            steps = iterations(pe, iteration)
            next(steps)
            hm = 2 + 4 * HALF_LOOPS
            pe.wait_ge(dq_copied, hm + 3)
            with pe.Fori(0, E // 4) as k:
                for p in range(2):
                    e = 2 * k + p
                    pe.wait_ge(ew_in[p], 64 * (k + 1))
                    pe.wait_ge(ex_yc, e)
                    pe.transpose(PS[:, 6, 0:P], exb[:, p, :], ident[:, :]).then_inc(ex_T, 1)
                    pe.wait_ge(ex_Tc, e + 1)
                    for m in range(2):
                        for w in range(2):
                            ins = mm(PS[0:I, 7, (2 * w + m) * CAP:(2 * w + m + 1) * CAP],
                                     ew[:, p, (2 * w + m) * I:(2 * w + m + 1) * I], dp_e[:, p * P + m * CAP:p * P + (m + 1) * CAP],
                                     start=m == 0 and w == 0)
                    ins.then_inc(ex_h, 1)
                    pe.wait_ge(ex_g, e + 1)
                    for m in range(2):
                        ins = mm(PS[0:CAP, 6, (1 + m) * P:(2 + m) * P], dq_e[0:I, p * P + m * CAP:p * P + (m + 1) * CAP],
                                 ew2[0:I, p, m * C:(m + 1) * C], start=m == 0)
                    ins.then_inc(ex_y, 1)
            pe.wait_ge(ex_yc, E // 2)
            for _ in steps:
                pass
            with pe.Fori(0, G) as g:
                pe.wait_ge(on_st, g + 1)
                for q in range(4):
                    ins = pe.transpose(PS[:, 0, q * P:(q + 1) * P], accm[:, 0, q * P:(q + 1) * P], ident[:, :])
                ins.then_inc(pj_T, 1)
                pe.wait_ge(pj_Tc, g + 1)
                pe.wait_ge(pj_add, g)
                for q in range(4):
                    ins = mm(PS[:, 1, q * P:(q + 1) * P], accm[:, 1, q * P:(q + 1) * P], wp[:, :], start=q == 0)
                ins.then_inc(pj_y, 1)

        @block.scalar
        def _(act):
            act.wait_ge(stats_ready, 1)
            act.activation(rstd, rstd, ACT.Sqrt).then_inc(rstd_ready, 1)

            def columns(g, p):
                act.wait_ge(xt_psum, g + 1)
                wait(act, sh_psum, 2 * g - 2)
                act.activation(XT[:, p, :], PS[:, 0, :], ACT.Copy).then_inc(xt_ready, 1)

            def group(g, p, k2):
                act.wait_ge(qk_psum, 2 * g + 1)
                wait(act, stacks_out[p], STORES * k2)
                wait(act, q_cut, g)
                wait(act, c_psum, g)
                act.activation(QF, PS[:, 1, :], ACT.Copy, scale=SC)
                act.activation(QP[p][:, 0, :], PS[:, 1, :], ACT.Copy, scale=SC).then_inc(qf_ready, 1)
                act.wait_ge(qk_psum, 2 * g + 2)
                wait(act, k_cut, g)
                act.activation(KF, PS[:, 2, :], ACT.Copy)
                act.activation(KP[p][:, 0, :], PS[:, 2, :], ACT.Copy).then_inc(kf_ready, 1)
                wait(act, sh_ready, 2 * g)
                for a in range(2):
                    act.wait_ge(sh_psum, 2 * g + a + 1)
                    act.activation(EX[0:I, a, :], PS[0:I, 5 + 2 * a, :], ACT.Exp, scale=-1.0).then_inc(sh_exp, 1)
                if after(g):
                    columns(g + 1, 1 - p)
                act.wait_ge(c_psum, g + 1)
                wait(act, c_cut, g)
                act.activation(CF[0:64, :], PS[0:64, 1, :], ACT.Copy)
                act.activation(CP[p][0:64, 0, :], PS[0:64, 1, :], ACT.Copy).then_inc(cf_ready, 1)

            columns(0, 0)
            groups(act, group)
            act.wait_ge(route_max, 1)
            act.activation(RB[:, :, :].rearrange("p a e -> p (a e)"), RB[:, :, :].rearrange("p a e -> p (a e)"),
                           ACT.Exp).then_inc(route_exp, 1)
            act.wait_ge(wts_ready, 1)
            act.wait_ge(pads_set, 1)

            def exps(i, c, u):
                h = 4 * i + c
                act.wait_ge(s2_ready, SLOTS * h + u + 1)
                J, half = u // 2, u % 2
                if half == 0:
                    wait(act, pv_done, NJ * (h - 1) + J + 1)
                    wait(act, pa_out[J // 4], 64 * h)
                act.activation(PT[:, TILE + N * J + 512 * half:TILE + N * J + 512 * half + 512],
                               PS[:, 2 + u % 2, :], ACT.Exp).then_inc(s2_read, 1)

            def iteration(i, c, peeled):
                h = 4 * i + c
                on = lambda n: (not peeled) or 0 <= c + n < HEADS
                for s in range(SLOTS):
                    if s == 3 and on(0):
                        act.wait_ge(mrow_psum, h + 1)
                        act.wait_ge(s1_ready, SLOTS * h + SLOTS)
                        act.activation(Qs[ROW_M:ROW_M + 3, c % 4, :], MISC[0:3, :], ACT.Copy).then_inc(mrow_ready, 1)
                    if s == 14 and on(3):
                        act.wait_ge(dq_psum, h + 4)
                        wait(act, dq_out, 16 * (h + 3))
                        act.activation(dq_e[:, :], MISC, ACT.Copy).then_inc(dq_copied, 1)
                    if s in (5, 7) and on(2):
                        part = (s - 5) // 2
                        act.wait_ge(ajk_psum, 2 * h + 5 + part)
                        wait(act, aj_out, 16 * (h + 2))
                        act.activation(aj_e[:, 4 * part:4 * part + 4, 0:DIST],
                                       PS[:, 7, :].rearrange("p (a n) -> p a n", n=P)[:, :, 0:DIST],
                                       ACT.Copy).then_inc(ajk_copied, 1)
                    if s >= LAG and on(0):
                        exps(i, c, s - LAG)
                    if s < LAG and on(-1):
                        exps(i, c - 1, s + SLOTS - LAG)
                    if s == 4 and on(-2):
                        act.wait_ge(rel_done, h - 1)
                        act.wait_ge(fin_psum, h - 1)
                        act.activation(Oev[:, c % 2, :], PS[:, 4 + c % 2, 0:256], ACT.Copy).then_inc(o_copied, 1)

            steps = iterations(act, iteration)
            next(steps)
            hm = 2 + 4 * HALF_LOOPS
            act.wait_ge(dp_out, 16 * (hm - 1))
            act.wait_ge(dq_out, 16 * (hm + 3))
            with act.Fori(0, E // 4) as k:
                for p in range(2):
                    e = 2 * k + p
                    act.wait_ge(ex_T, e + 1)
                    act.activation(dp_e[:, p * P:p * P + P], PS[:, 6, 0:P], ACT.Copy).then_inc(ex_Tc, 1)
                    act.wait_ge(ex_h, e + 1)
                    act.activation(dq_e[0:I, 256 + p * P:256 + p * P + P], PS[0:I, 7, 0:P], ACT.Exp, scale=-1.0).then_inc(ex_e, 1)
            for _ in steps:
                pass
            with act.Fori(0, G) as g:
                act.wait_ge(pj_T, g + 1)
                act.wait_ge(pj_y, g)
                act.activation(accm[:, 1, 0:512], PS[:, 0, :], ACT.Copy).then_inc(pj_Tc, 1)

        @block.vector
        def _(dve):
            n = [0]

            def step(ins):
                n[0] += 1
                ins.then_inc(dve_step, 1)
                dve.wait_ge(dve_step, n[0])

            dve.wait_ge(tabs_in, 48)
            step(dve.tensor_scalar(tres[:, 1, :], tres[:, 1, :], SC, None, ALU.mult))
            for k in range(2):
                step(dve.tensor_copy(tprt[:, k, :, :], tres[:, :, :]))
                step(dve.tensor_tensor(tres[:, :, :], tres[:, :, :], tprt[:, k, :, :], ALU.subtract))
            dve.tensor_copy(tprt[:, 2, :, :], tres[:, :, :]).then_inc(tabs_cut, 1)
            dve.wait_ge(w_in, 16 * 13)
            dve.tensor_copy(identb[:, :], ident[:, :])
            dve.tensor_scalar(cqk[:, 1, :], cqk[:, 1, :], SC, None, ALU.mult).then_inc(cqk_scaled, 1)
            dve.wait_ge(tv_psum, 1)
            for a in range(2):
                ins = dve.tensor_copy(TV[:, :, 4 * a:4 * a + 4, :].rearrange("p h v d -> p v h d"),
                                      PS[:, a, :].rearrange("p (v h d) -> p v h d", v=4, h=H))
            ins.then_inc(tv_ready, 1)
            dve.wait_ge(x_in, 64)
            for k in range(NB):
                ins = dve.bn_stats(st6[:, k, :], X[:, k, :])
            ins.then_inc(bn_done, 1)
            dve.wait_ge(bn_done, 1)
            step(dve.tensor_copy(tmpn[:, 0, :], st6[:, :, 1]))
            step(dve.tensor_tensor(mean, tmpn[:, 0, :], st6[:, :, 4], ALU.add))
            step(dve.tensor_tensor(tmpn[:, 0, :], tmpn[:, 0, :], st6[:, :, 4], ALU.subtract))
            step(dve.tensor_tensor(tmpn[:, 1, :], tmpn[:, 0, :], tmpn[:, 0, :], ALU.mult))
            step(dve.tensor_tensor(rstd, st6[:, :, 2], st6[:, :, 5], ALU.add))
            step(dve.tensor_scalar(rstd, rstd, 1.0 / C, None, ALU.mult))
            step(dve.scalar_tensor_tensor(out=rstd, in0=tmpn[:, 1, :], scalar=0.25, in1=rstd, op0=ALU.mult, op1=ALU.add))
            step(dve.tensor_scalar(mean, mean, 0.5, None, ALU.mult))
            step(dve.tensor_scalar(rstd, rstd, 1e-5, None, ALU.add))
            dve.sem_inc(stats_ready, 1)
            dve.wait_ge(rstd_ready, 1)
            step(dve.reciprocal(rstd, rstd))
            base = n[0]

            def rows_of(g):
                wait(dve, xt_psum, g)
                wait(dve, xna_copied, g)
                for q in range(4):
                    ins = dve.tensor_scalar(XN[:, q, :], X[:, bass.ds(g * 4 + q, 1), :].rearrange("p a c -> p (a c)"),
                                            mean[:, bass.ds(g * 4 + q, 1)], rstd[:, bass.ds(g * 4 + q, 1)],
                                            ALU.subtract, ALU.mult)
                ins.then_inc(xn_ready, 1)

            def shared_add(g):
                dve.wait_ge(z_psum, g + 1)
                dve.tensor_tensor(X[:, bass.ds(g * 4, 4), :], X[:, bass.ds(g * 4, 4), :],
                                  PS[:, 0, :].rearrange("p (q c) -> p q c", q=4), ALU.add).then_inc(z_added, 1)

            PER = 9

            def group(g, p, k2):
                k = [0]

                def gstep(ins):
                    k[0] += 1
                    ins.then_inc(dve_step, 1)
                    dve.wait_ge(dve_step, g * PER + (base + k[0]))

                if after(g):
                    rows_of(g + 1)
                dve.wait_ge(xn_ready, g + 1)
                dve.tensor_tensor(X[:, bass.ds(g * 4, 4), :], X[:, bass.ds(g * 4, 4), :],
                                  bp_s[:, :].unsqueeze(1).broadcast_to([P, 4, C]), ALU.add)
                dve.wait_ge(qf_ready, g + 1)
                gstep(dve.tensor_tensor(QR, QF, QP[p][:, 0, :], ALU.subtract))
                gstep(dve.tensor_copy(QP[p][:, 1, :], QR))
                gstep(dve.tensor_tensor(QR, QR, QP[p][:, 1, :], ALU.subtract))
                dve.tensor_copy(QP[p][:, 2, :], QR).then_inc(q_cut, 1)
                dve.wait_ge(vg_psum, g + 1)
                VRf = VR[:, :, :, :, :].rearrange("p b h j d -> p b j h d")
                for a in range(2):
                    src = PS[:, 3 + a, 0:384].rearrange("p (q n) -> p q n", q=2)
                    for q in range(2):
                        dve.tensor_copy(
                            VRf[:, bass.ds(g // 2, 1), bass.ds((g % 2) * 4 + 2 * a + q, 1), :, :].rearrange("p b j h d -> p (b j h) d"),
                            src[:, q, 0:C].rearrange("p (h d) -> p h d", h=H))
                    ins = dve.tensor_copy(LG[:, bass.ds(g * 4 + 2 * a, 2), :], src[:, :, C:C + E])
                ins.then_inc(vg_copied, 1)
                if not isinstance(g, int) or g > 0:
                    shared_add(g - 1)
                for a in range(2):
                    dve.wait_ge(sh_exp, 2 * g + a + 1)
                    gstep(dve.tensor_scalar(EX[0:I, a, :], EX[0:I, a, :], 1.0, None, ALU.add))
                    gstep(dve.reciprocal(EX[0:I, a, :], EX[0:I, a, :]))
                    gstep(dve.tensor_tensor(EX[0:I, a, :], PS[0:I, 5 + 2 * a, :], EX[0:I, a, :], ALU.mult))
                    dve.tensor_tensor(HG[0:I, a, :], PS[0:I, 6 if a == 0 else 2, :], EX[0:I, a, :], ALU.mult).then_inc(sh_ready, 1)
                assert k[0] == PER

            rows_of(0)
            groups(dve, group)
            shared_add(G - 1)
            n[0] = base + PER * G

            dve.wait_ge(zeros_out, ZEROS)
            for p in range(2):
                dve.wait_ge(stacks_out[p], STORES * (G // 2))
            def over_e(a):
                return a.unsqueeze(2).broadcast_to([P, NB, E])

            dve.wait_ge(z_added, G)
            dve.wait_ge(vg_copied, G)
            step(dve.tensor_reduce(rmax, LG, AX.X, ALU.max))
            step(dve.tensor_tensor(RB, LG, over_e(rmax), ALU.subtract))
            dve.sem_inc(route_max, 1)
            dve.wait_ge(route_exp, 1)
            step(dve.tensor_reduce(rsum, RB, AX.X, ALU.add))
            step(dve.reciprocal(rsum, rsum))
            step(dve.tensor_tensor(LG, RB, over_e(rsum), ALU.mult))
            dve.memset(RV66[:, :, E:E + 2], BIG)
            step(dve.tensor_tensor(RV66[:, :, 0:E], LG, gb_s[:, :].unsqueeze(1).broadcast_to([P, NB, E]), ALU.add))
            for blk in range(NB):
                ins = dve.max(top8[:, blk, :], RV66[:, blk, :])
            step(ins)
            for blk in range(NB):
                ins = dve.match_replace(RV66[:, blk, :], top8[:, blk, :], RV66[:, blk, :], -BIG)
            step(ins)
            step(dve.tensor_scalar(maskb, RV66[:, :, 0:E], -BIG, None, ALU.is_equal))
            dve.wait_ge(xna_copied, G)
            step(dve.memset(prevb[:, 0, :], 0.0))
            for blk in range(1, NB):
                ins = dve.tensor_tensor(prevb[:, blk, :], prevb[:, blk - 1, :], maskb[:, blk - 1, :], ALU.add)
                step(ins)
            dve.sem_inc(mask_ready, 1)
            dve.wait_ge(one_set, 1)
            for m in range(NB // 8):
                dve.wait_ge(pos_psum, m + 1)
                pos = PS[:, m, :].rearrange("p (a e) -> p a e", e=E)
                b8 = slice(8 * m, 8 * m + 8)
                step(dve.scalar_tensor_tensor(out=RD[:, b8, :], in0=pos, scalar=float(CAP), in1=maskb[:, b8, :],
                                              op0=ALU.is_lt, op1=ALU.mult))
                step(dve.tensor_tensor(RC[:, b8, :], pos, slot_s[:, :].unsqueeze(1).broadcast_to([P, 8, E]), ALU.add))
                step(dve.tensor_tensor(RC[:, b8, :], RC[:, b8, :], RD[:, b8, :], ALU.mult))
            dve.sem_inc(pos_read, 1)
            for blk in range(NB):
                ins = dve.max(top8[:, blk, :], RC[:, blk, :])
            step(ins)
            step(dve.tensor_scalar(RV66[:, :, 0:8], top8, 0.5, 2.0 * E * CAP, ALU.is_lt, ALU.mult))
            step(dve.tensor_tensor(RV66[:, :, 0:8], RV66[:, :, 0:8], top8, ALU.add))
            step(dve.tensor_scalar(RV66[:, :, 0:8], RV66[:, :, 0:8], -1.0, None, ALU.add))
            dve.tensor_copy(idx[:, :, :], RV66[:, :, 0:8]).then_inc(idx_ready, 1)
            step(dve.tensor_tensor(RD, RD, LG, ALU.mult))
            for k6 in range(TOPK):
                step(dve.tensor_tensor(RB, RC, top8[:, :, k6:k6 + 1].broadcast_to([P, NB, E]), ALU.is_equal))
                step(dve.tensor_tensor(RB, RB, RD, ALU.mult))
                step(dve.tensor_reduce(wts[:, k6, :], RB, AX.X, ALU.add))
            dve.sem_inc(wts_ready, 1)
            dve.memset(PS[:, 4, 0:256], 0.0)
            step(dve.memset(PS[:, 5, 0:256], 0.0))
            dve.memset(aj_e[:, :, DIST:P], 0.0)
            dve.sem_inc(psum_zeroed, 1)
            dve.wait_ge(pads_set, 1)

            def iteration(i, c, peeled):
                h = 4 * i + c
                on = lambda m: (not peeled) or 0 <= c + m < HEADS
                for s in range(SLOTS):
                    if on(1):
                        dve.wait_ge(s1_ready, SLOTS * (h + 1) + s + 1)
                        dst = accm[:, (c + 1) % 2, 512 * (s % 2):512 * (s % 2) + 512]
                        if s < 2:
                            wait(dve, accT_psum, h)
                            dve.tensor_copy(dst, PS[:, s % 2, :]).then_inc(s1_read, 1)
                        else:
                            dve.wait_ge(s1_read, SLOTS * (h + 1) + s - 1)
                            dve.tensor_tensor(dst, PS[:, s % 2, :], dst, ALU.max).then_inc(s1_read, 1)
                    if s == 0 and on(0):
                        dve.wait_ge(accT_psum, h + 1)

                        def hstep(ins, m):
                            ins.then_inc(max_step, 1)
                            dve.wait_ge(max_step, 6 * h + m)
                        hstep(dve.tensor_reduce(mx[:, 0, :], MISC.rearrange("p (a b) -> p a b", a=NJ), AX.X, ALU.max), 1)
                        wait(dve, mrow_psum, h)
                        hstep(dve.tensor_scalar(mx[:, 1, :], mx[:, 0, :], -1.0, None, ALU.mult), 2)
                        hstep(dve.tensor_copy(mparts[:, :, 0], mx[:, 1, :]), 3)
                        hstep(dve.tensor_tensor(mx[:, 2, :], mx[:, 1, :], mparts[:, :, 0], ALU.subtract), 4)
                        hstep(dve.tensor_copy(mparts[:, :, 1], mx[:, 2, :]), 5)
                        hstep(dve.tensor_tensor(mx[:, 3, :], mx[:, 2, :], mparts[:, :, 1], ALU.subtract), 6)
                        dve.tensor_copy(mparts[:, :, 2], mx[:, 3, :]).then_inc(mparts_ready, 1)
                    if s == 4 and on(0):
                        wait(dve, pv_done, NJ * (h - 1))
                        v = VR[:, bass.ds(batch_of(h), 1), bass.ds(h % H, 1), :, :].rearrange("p b h j d -> p (b h j) d")
                        t = TV[:, bass.ds(h % H, 1), :, :].rearrange("p h v d -> p (h v) d")
                        dve.tensor_tensor(Vst[:, c % 2, :, :, 0:HD], v.unsqueeze(2).broadcast_to([P, NJ, 8, HD]),
                                          t.unsqueeze(1).broadcast_to([P, NJ, 8, HD]), ALU.add).then_inc(v_ready, 1)
                        wait(dve, rel_done, h - 1)
                        dve.tensor_copy(RVc[0:DIST, c % 2, :],
                                        RV[0:DIST, bass.ds(h % H, 1), :].rearrange("p a d -> p (a d)")).then_inc(rv_ready, 1)
                    if s == 9 and on(-2):
                        hh = h - 2
                        dve.wait_ge(fin_psum, h)
                        o = MISC[:, 0:256].rearrange("p (a q e) -> p q a e", a=2, q=4)
                        dve.reciprocal(rden[:, :, :], o[:, :, :, HD]).then_inc(rden_ready, 1)
                        dve.wait_ge(rden_ready, h - 1)
                        dst = ON[:, 0:NB, :].rearrange("p (b j) (h d) -> p b h j d", b=B, h=H)[
                            :, bass.ds(batch_of(hh), 1), bass.ds(hh % H, 1), :, :].rearrange("p b h (q a) d -> p (b h q) a d", a=2)
                        dve.tensor_tensor(dst, o[:, :, :, 0:HD], rden[:, :, :].unsqueeze(3).broadcast_to([P, 4, 2, HD]),
                                          ALU.mult).then_inc(on_ready, 1)
                    if s in (5, 7) and on(2):
                        part = (s - 5) // 2
                        dve.wait_ge(aj_psum, 2 * h + 5 + part)
                        dve.wait_ge(ajk_copied, 2 * h + 5 + part)
                        w = aj_e[:, 4 * part:4 * part + 4, 0:DIST]
                        q6 = PS[:, 6, :].rearrange("p (a n) -> p a n", n=P)[:, :, 0:DIST]
                        dve.tensor_tensor(w, q6, w, ALU.add).then_inc(aj_copied, 1)
                    if s == 12 and on(-1):
                        dve.wait_ge(dp_psum, h)
                        wait(dve, dp_out, 16 * (h - 1))
                        dve.tensor_copy(dp_e[:, :], MISC).then_inc(dp_copied, 1)

            steps = iterations(dve, iteration)
            next(steps)
            hm = 2 + 4 * HALF_LOOPS
            dve.wait_ge(aj_out, 16 * (hm + 2))
            with dve.Fori(0, E // 4) as k:
                for p in range(2):
                    e = 2 * k + p
                    g_, t_ = dq_e[0:I, p * P:p * P + P], dq_e[0:I, 256 + p * P:256 + p * P + P]

                    def estep(ins, m):
                        ins.then_inc(ex_step, 1)
                        dve.wait_ge(ex_step, 3 * e + m)
                    dve.wait_ge(ex_e, e + 1)
                    estep(dve.tensor_scalar(t_, t_, 1.0, None, ALU.add), 1)
                    estep(dve.reciprocal(t_, t_), 2)
                    estep(dve.tensor_tensor(t_, PS[0:I, 7, 0:P], t_, ALU.mult), 3)
                    dve.tensor_tensor(g_, PS[0:I, 7, P:2 * P], t_, ALU.mult).then_inc(ex_g, 1)
                    dve.wait_ge(ex_y, e + 1)
                    dve.wait_ge(ex_out, 64 * k)
                    dve.tensor_copy(aj_e[0:CAP, 2 * p:2 * p + 2, :],
                                    PS[0:CAP, 6, P:3 * P].rearrange("p (m c) -> p m c", m=2)).then_inc(ex_yc, 1)
            dve.wait_ge(ex_out, 32 * (E // 2))
            for _ in steps:
                pass
            dve.wait_ge(y_added, 5 * NB + 1)
            dve.wait_ge(on_ready, HEADS)
            with dve.Fori(0, G) as g:
                dve.wait_ge(pj_T, g)
                dve.tensor_copy(accm[:, 0, 0:512].rearrange("p (a c) -> p a c", a=4), ON[:, bass.ds(g * 4, 4), :]).then_inc(on_st, 1)
                dve.wait_ge(pj_y, g + 1)
                dve.tensor_tensor(X[:, bass.ds(g * 4, 4), :], X[:, bass.ds(g * 4, 4), :],
                                  PS[:, 1, :].rearrange("p (a c) -> p a c", a=4), ALU.add).then_inc(pj_add, 1)


def kernel(**inputs):
    import numpy as np
    import concourse.bacc as bacc
    from concourse.bass_utils import run_bass_kernel_spmd

    a = {k.replace("L0_", ""): np.asarray(v) for k, v in inputs.items()}
    H, HD, NBK = a["attn_rpe_q_table"].shape
    C = H * HD
    E, D = a["ffn_gate_w"].shape
    I = a["ffn_w1"].shape[1]
    f32 = np.float32

    def by_distance(table, sign):
        return table[..., np.clip(sign * (np.arange(P) - (DIST // 2)), -31, 31) + 31]

    def rows_by_distance(table, sign):
        return by_distance(table, sign).reshape(C, P)

    def far(table, lower, upper):
        t = np.zeros((H, HD, 2, H), f32)
        for h in range(H):
            t[h, :, 0, h] = table[h, :, lower]
            t[h, :, 1, h] = table[h, :, upper]
        return t.reshape(C, 2 * H)

    wqkv = a["attn_w_qkv"]
    vmask = np.zeros((2, 8, P), f32)
    for v in range(8):
        for s in range(4):
            k = value_kind(v, s)
            if k is not None:
                vmask[k, v, TILE * s:TILE * s + TILE] = 1
    kc = np.zeros((9, 2, 1024), f32)
    kc[0:6, 0] = 1
    kc[0:3, 1] = 1
    kc[6:9, 1] = 1
    kc = kc[:ROW_K - ROW_M]
    arrays = {
        "x": a["attn_x"],
        "wqkvg": np.concatenate([wqkv.T, a["ffn_gate_w"].T], axis=1),
        "w_proj": a["attn_w_proj"].T,
        "b_proj": a["attn_b_proj"].reshape(1, C),
        "rk_far": far(a["attn_rpe_k_table"], 0, NBK - 1),
        "rq_far": far(a["attn_rpe_q_table"], NBK - 1, 0),
        "rk_dist": rows_by_distance(a["attn_rpe_k_table"], -1),
        "rq_dist": rows_by_distance(a["attn_rpe_q_table"], 1),
        "rv_rows": by_distance(a["attn_rpe_v_table"].transpose(0, 2, 1), -1).transpose(2, 0, 1)[:DIST],
        "rv_far": np.stack([a["attn_rpe_v_table"][:, 0].reshape(C), a["attn_rpe_v_table"][:, NBK - 1].reshape(C)]),
        "gate_b": a["ffn_gate_b"].reshape(1, E),
        "w1": a["ffn_w1"].transpose(2, 0, 1),
        "w3": a["ffn_w3"].transpose(2, 0, 1),
        "w2": a["ffn_w2"].transpose(2, 0, 1),
        "ws1": a["ffn_ws1"].T,
        "ws3": a["ffn_ws3"].T,
        "ws2": a["ffn_ws2"].T.reshape(2, I, D),
        "ident_c": np.eye(P, dtype=f32),
        "tri_c": np.triu(np.ones((P, P), f32), 1),
        "kconst_c": kc,
        "vmask_c": vmask.reshape(2, 8 * P),
        "slot_c": (np.arange(E) * 64 + 1).astype(f32).reshape(1, E),
    }
    nc = bacc.Bacc("TRN2", target_bir_lowering=False, num_devices=1)
    args, feed = [], {}
    for name, v in arrays.items():
        v = np.ascontiguousarray(v)
        feed[f"in_{name}"] = v
        args.append(nc.dram_tensor(f"in_{name}", v.shape, mybir.dt.from_np(v.dtype), kind="ExternalInput").ap())
    out = nc.dram_tensor("out_0", a["attn_x"].shape, F32, kind="ExternalOutput").ap()
    program(nc, *args, out)
    r = run_bass_kernel_spmd(nc, [feed], core_ids=[0])
    return r.results[0]["out_0"]
```

```python
from contextlib import ExitStack

import concourse.bass as bass
from concourse import mybir

F32 = mybir.dt.float32
BF16 = mybir.dt.bfloat16
I32 = mybir.dt.int32
ALU = mybir.AluOpType
ACT = mybir.ActivationFunctionType
AX = mybir.AxisListType

P = 128
COMBOS = 6
K_PART = [0, 0, 1, 1, 0, 2]
Q_PART = [0, 1, 0, 1, 2, 0]
TILE = 32
WIN = 3 * TILE
DIST = 4 * TILE - 1
ROW_M = 64
ROW_C = 67
ROW_K = 73
ROWS = 76
DROW = 1024 + 128
SLOTS = 16
LAG = 4
BIG = 1.0e30


def wait(eng, sem, value):
    if not isinstance(value, int) or value > 0:
        eng.wait_ge(sem, value)


def span(lo, hi, half):
    lo, hi = max(lo, 512 * half), min(hi, 512 * half + 512)
    return (lo, hi) if lo < hi else None


def value_variant(ti, J):
    r = ti - 4 * J
    return 1 if r <= -2 else 2 if r == -1 else 4 + r if r <= 3 else 3 if r == 4 else 0


def value_kind(variant, s):
    if variant == 0:
        return 0
    if variant == 1:
        return 1
    r = {2: -1, 3: 4}.get(variant, variant - 4)
    return None if abs(s - r) <= 1 else (0 if s < r else 1)


def program(nc, x, wqkvg, w_proj, b_proj, rk_far, rq_far, rk_dist, rq_dist, rv_rows, rv_far,
            gate_b, w13, w2, ws1, ws3, ws2, ident_c, tri_c, kconst_c, vmask_c, slot_c, out):
    B, N, C = x.shape
    T = B * N
    NB = T // P
    G = T // 512
    H = 16
    HD = C // H
    HEADS = B * H
    NJ = N // P
    E = gate_b.shape[1]
    I = w13.shape[3]
    QUADS = E // 4
    assert (T // 512) % 2 == 0 and QUADS % 2 == 0
    SC = float(HD) ** -0.5
    TOPK, CAP = 6, 64
    HALF_LOOPS = (HEADS - 4) // 8
    LOOPS = (HEADS - 4) // 4
    hm = 2 + 4 * HALF_LOOPS

    ctx = ExitStack()
    with ctx:
        def sb(name, shape, dt=F32):
            return ctx.enter_context(nc.sbuf_tensor(name, shape, dt))

        def sem(name):
            return ctx.enter_context(nc.semaphore(name))

        def dram(name, shape, dt=F32):
            return nc.dram_tensor(name, shape, dt, kind="Internal").ap()

        q_stack = dram("q_stack", [H * HD, COMBOS, T], BF16)
        k_stack = dram("k_stack", [H * HD, COMBOS, T], BF16)
        q_far = dram("q_far", [H, 9, T], BF16)
        k_far = dram("k_far", [H, 6, T], BF16)
        tab_stack = dram("tab_stack", [H * HD, COMBOS, 2, P], BF16)
        dq_d = dram("dq_d", [DIST, DROW])
        aj_d = dram("aj_d", [N, P])
        pa_d = dram("pa_d", [N, P])
        dp_d = dram("dp_d", [DIST, DROW])
        xb_d = dram("xb_d", [E * CAP, C])
        yb_d = dram("yb_d", [E * CAP, C])

        X = sb("X", [P, NB, C])
        XNA = sb("XNA", [P, NB, C])
        VR = sb("VR", [P, B, H, NJ, HD])
        ON = sb("ON", [P, max(NB, 32), C])
        TV = sb("TV", [P, H, 8, HD])
        PT = sb("PT", [P, TILE + NJ * N + TILE])
        accm = sb("accm", [P, 2, N])
        Qs = sb("Qs", [ROWS, 4, N], BF16)
        Ks = sb("Ks", [ROWS, 4, 2, N], BF16)
        Ksf = Ks[:, :, :, :].rearrange("p a b c -> p (a b c)")
        Qsf = Qs[:, :, :].rearrange("p a b -> p (a b)")
        tab = sb("tab", [ROWS, 4, 2, P], BF16)
        WT = sb("WT", [P, 4, NJ, WIN])
        Vst = sb("Vst", [P, 2, NJ, 8, 9])
        dq_e = sb("dq_e", [P, N])
        dq_s = sb("dq_s", [P, N])
        aj_e = sb("aj_e", [P, NJ, P])
        pa_s = sb("pa_s", [P, NJ, P])
        dp_e = sb("dp_e", [P, N])
        dp_s = sb("dp_s", [P, N])
        Oev = sb("Oev", [P, 2, 256])
        mx = sb("mx", [P, 4, NJ])
        mparts = sb("mparts", [P, NJ, 3], BF16)
        rden = sb("rden", [P, 4, 2])
        RVc = sb("RVc", [P, 2, HD])
        ident = sb("ident", [P, P])
        zcol = sb("zcol", [P, 1])
        identb = sb("identb", [P, P], BF16)
        RV = sb("RV", [P, H, HD])
        wp = sb("wp", [P, C])
        yg = sb("yg", [P, TOPK, C])
        idx = sb("idx", [P, NB, 8], I32)
        wts = sb("wts", [P, TOPK, NB])
        ew = sb("ew", [P, 4 * 2 * I])
        ew2 = sb("ew2", [P, 4 * C])
        exb = sb("exb", [P, 2, C])

        def cut(t, at, shape, dt=F32):
            n = 1
            for s in shape[1:]:
                n *= s
            w = n if dt == F32 else n // 2
            a = t[:, at:at + w]
            if dt != F32:
                a = a.bitcast(dt)
            names = " ".join("abcd"[:len(shape) - 1])
            kw = {"abcd"[k]: shape[k + 1] for k in range(len(shape) - 1)}
            return (a.rearrange(f"p ({names}) -> p {names}", **kw) if len(shape) > 2 else a), at + w

        at = 0
        LG, at = cut(PT, at, [P, NB, E])
        RB, at = cut(PT, at, [P, NB, E])
        RC, at = cut(PT, at, [P, NB, E])
        RD, at = cut(PT, at, [P, NB, E])
        ONf = ON[:, :, :].rearrange("p a b -> p (a b)")
        at = 0
        RV66, at = cut(ONf, at, [P, NB, E + 2])
        maskb, at = cut(ONf, at, [P, NB, E], BF16)
        assert at <= NB * C
        accf = accm[:, :, :].rearrange("p a b -> p (a b)")
        prevb, at = cut(accf, 0, [P, NB, E], BF16)
        pas = pa_s[:, :, :].rearrange("p a b -> p (a b)")
        XN, at = cut(accf, 0, [P, 4, C])
        XT, at = cut(accf, at, [P, 2, 512])
        QF, at = cut(accf, at, [P, 512])
        CF, QR = dq_e[:, 0:512], dq_e[:, 512:N]
        KR, CR = dp_e[:, 0:512], dp_e[:, 512:N]
        QP = [cut(dq_s, 0, [P, 3, 512], BF16)[0]]
        KP = [cut(dp_s, 0, [P, 3, 512], BF16)[0]]
        CP = [cut(pas, 0, [P, 3, 512], BF16)[0]]
        fz = 0
        QP1, fz = cut(ONf, fz, [P, 3, 512], BF16)
        KP1, fz = cut(ONf, fz, [P, 3, 512], BF16)
        CP1, fz = cut(ONf, fz, [P, 3, 512], BF16)
        QP.append(QP1)
        KP.append(KP1)
        CP.append(CP1)
        KF, fz = cut(ONf, fz, [P, 512])
        Z, fz = cut(ONf, fz, [P, 1024])
        aje = aj_e[:, :, :].rearrange("p a b -> p (a b)")
        EX, at = cut(aje, 0, [P, 2, 512])
        WTf = WT[:, :, :, :].rearrange("p a b c -> p (a b c)")
        at = 0
        HG, at = cut(WTf, at, [P, 2, 512])
        wq_s, at = cut(WTf, at, [P, 3 * C + E])
        ws1_s, at = cut(WTf, at, [P, 2 * I])
        ws3_s, at = cut(WTf, at, [P, 2 * I])
        ws2_s, at = cut(WTf, at, [P, 2, C])
        bp_s, at = cut(WTf, at, [P, C])
        cqk, at = cut(WTf, at, [P, 2, 2 * H])
        st6, at = cut(WTf, at, [P, NB, 6])
        mean, at = cut(WTf, at, [P, NB])
        rstd, at = cut(WTf, at, [P, NB])
        tmpn, at = cut(WTf, at, [P, 2, NB])
        assert at <= 3072
        ygf = yg[:, :, :].rearrange("p a b -> p (a b)")
        at = 0
        gb_s, at = cut(ygf, at, [P, E])
        slot_s, at = cut(ygf, at, [P, E])
        trib, at = cut(ygf, at, [P, P], BF16)
        oneb, at = cut(ygf, at, [P, P], BF16)
        rmax, at = cut(ygf, at, [P, NB])
        rsum, at = cut(ygf, at, [P, NB])
        top8, at = cut(ygf, at, [P, NB, 8])
        assert at <= TOPK * C
        vm_s = dp_s[0:2, 0:8 * P]
        rvf_s = ew[0:2, 0:C]
        tres = exb
        tprt, _ = cut(ew2[:, :], 0, [P, 3, 2, P], BF16)

        W13 = [t[:, 0:8 * I].rearrange("p (m w i) -> p m w i", w=2, i=I) for t in (ew, ygf)]
        W2 = [t[:, 0:4 * C].rearrange("p (m c) -> p m c", c=C) for t in (ew2, pas)]
        XB = [exb[:, :, :], pas[:, 4 * C:6 * C].rearrange("p (a c) -> p a c", c=C)]
        XBT = [dp_e[:, 256 * p:256 * p + 256] for p in range(2)]
        EH = [dp_e[0:I, 512 + 256 * p:768 + 256 * p] for p in range(2)]
        EG = [dq_e[0:I, 256 * p:256 * p + 256] for p in range(2)]
        EY = [aj_e[0:CAP, 4 * p:4 * p + 4, :] for p in range(2)]

        PS = ctx.enter_context(nc.psum_tensor("PS", [P, 8, 512], F32))
        MISC = PS[:, 6:8, :].rearrange("p a b -> p (a b)")

        w_in, x_in, c_in, tabs_in = sem("w_in"), sem("x_in"), sem("c_in"), sem("tabs_in")
        zero_set, one_set, zeros_out, zcol_set, k_zeroed = (
            sem("zero_set"), sem("one_set"), sem("zeros_out"), sem("zcol_set"), sem("k_zeroed"))
        psum_zeroed, pads_set, kconst_in = sem("psum_zeroed"), sem("pads_set"), sem("kconst_in")
        dve_step, cut_step, tab_step = sem("dve_step"), sem("cut_step"), sem("tab_step")
        bn_done, max_step, rden_ready = sem("bn_done"), sem("max_step"), sem("rden_ready")
        stats_ready, rstd_ready = sem("stats_ready"), sem("rstd_ready")
        xn_ready, xna_copied = sem("xn_ready"), sem("xna_copied")
        xt_psum, xt_ready, qk_psum, qf_ready, kf_ready = (
            sem("xt_psum"), sem("xt_ready"), sem("qk_psum"), sem("qf_ready"), sem("kf_ready"))
        vg_psum, vg_copied = sem("vg_psum"), sem("vg_copied")
        sh_psum, sh_silu, sh_ready, z_psum, z_added = (
            sem("sh_psum"), sem("sh_silu"), sem("sh_ready"), sem("z_psum"), sem("z_added"))
        c_psum, cf_ready, cqk_scaled = sem("c_psum"), sem("cf_ready"), sem("cqk_scaled")
        q_cut, k_cut, c_cut, stacks_out = sem("q_cut"), sem("k_cut"), sem("c_cut"), [sem("stacks_out0"), sem("stacks_out1")]
        tv_psum, tv_ready, tabs_cut, tabs_out = (
            sem("tv_psum"), sem("tv_ready"), sem("tabs_cut"), sem("tabs_out"))
        route_max, route_exp, mask_ready, pos_psum, pos_read, idx_ready, wts_ready = (
            sem("route_max"), sem("route_exp"), sem("mask_ready"), sem("pos_psum"), sem("pos_read"),
            sem("idx_ready"), sem("wts_ready"))
        stack_in = [sem(f"stack_in{r}") for r in range(4)]
        wt_in = [sem(f"wt_in{r}") for r in range(4)]
        s1_ready, s1_read, s2_ready, s2_read = (
            sem("s1_ready"), sem("s1_read"), sem("s2_ready"), sem("s2_read"))
        accT_psum, mparts_ready, mrow_psum, mrow_ready = (
            sem("accT_psum"), sem("mparts_ready"), sem("mrow_psum"), sem("mrow_ready"))
        dq_psum, dq_copied, dq_out, dq_in = sem("dq_psum"), sem("dq_copied"), sem("dq_out"), sem("dq_in")
        aj_psum, aj_copied, aj_out = sem("aj_psum"), sem("aj_copied"), sem("aj_out")
        pa_out = [sem("pa_out0"), sem("pa_out1")]
        pa_in = sem("pa_in")
        dp_psum, dp_copied, dp_out, dp_in = sem("dp_psum"), sem("dp_copied"), sem("dp_out"), sem("dp_in")
        v_ready, pv_done, o_copied, fin_psum, on_ready = (
            sem("v_ready"), sem("pv_done"), sem("o_copied"), sem("fin_psum"), sem("on_ready"))
        scattered, ew_in, ex_T, ex_Tc, ex_h, ex_silu, ex_g, ex_y, ex_yc, ex_out = (
            sem("scattered"), [sem("ew_in0"), sem("ew_in1")], sem("ex_T"), sem("ex_Tc"), sem("ex_h"),
            sem("ex_silu"), sem("ex_g"), sem("ex_y"), sem("ex_yc"), [sem("ex_out0"), sem("ex_out1")])
        w2_in = [sem("w2_in0"), sem("w2_in1")]
        rel_done, rv_ready, ajk_psum, ajk_copied = sem("rel_done"), sem("rv_ready"), sem("ajk_psum"), sem("ajk_copied")
        gathered, y_added = sem("gathered"), sem("y_added")
        pj_T, pj_Tc, pj_y, pj_add, stored = (
            sem("pj_T"), sem("pj_Tc"), sem("pj_y"), sem("pj_add"), sem("stored"))

        def live(h, c):
            return c is None or 0 <= h < HEADS

        def iterations(eng, body):
            for h in range(-3, 2):
                body(0, h, True)
            with eng.Fori(0, HALF_LOOPS) as i:
                for r in range(4):
                    body(i, 2 + r, False)
            yield
            with eng.Fori(HALF_LOOPS, LOOPS) as i:
                for r in range(4):
                    body(i, 2 + r, False)
            for h in range(HEADS - 2, HEADS + 2):
                body(0, h, True)

        def turns(eng, count, body):
            for g in range(2):
                body(g, g % 2, 0)
            with eng.Fori(1, count // 2 - 1) as k:
                for p in range(2):
                    body(2 * k + p, p, k)
            for g in range(count - 2, count):
                body(g, g % 2, g // 2)

        def after(g, count, n=1):
            return not isinstance(g, int) or g + n < count

        def batch_of(h):
            b = h // H
            return b if isinstance(h, int) else nc.s_assert_within(
                b, 0, B - 1, skip_runtime_bounds_check_because="the loops' heads are below HEADS")

        def rows(t, offset, pattern):
            return bass.AP(t.tensor, offset, pattern)

        STORES = 16 * (3 + 3 + 4)
        ZEROS = 16 * (5 + E * CAP // 1024 + 3 * (T // 1024))

        block = ctx.enter_context(nc.Block())

        @block.sync
        def _(sp):
            def parts_out(dst, src, part, sem_):
                for n in range(0, COMBOS, 2):
                    a, b = part[n], part[n + 1]
                    s = src[:, a:a + 1, :].ap
                    view = bass.AP(src.tensor, src[:, a:a + 1, :].offset,
                                   [list(s[0]), [(b - a) * src.ap[1][0], 2], list(s[-1])])
                    sp.dma_start(dst[:, n:n + 2, :], view).then_inc(sem_, 16)

            xv = x.rearrange("b (j p) c -> p (b j) c", p=P)
            for g in range(4):
                n = NB // 4
                sp.dma_start(X[:, n * g:n * g + n, :], xv[:, n * g:n * g + n, :]).then_inc(x_in, 16)
            for dst, src in ((tres[:, 0, :], rk_dist), (tres[:, 1, :], rq_dist), (ident[:, :], ident_c)):
                sp.dma_start(dst, src).then_inc(tabs_in, 16)
            for dst, src in ((wq_s, wqkvg), (ws1_s, ws1), (ws3_s, ws3), (wp[:, :], w_proj),
                             (cqk[:, 0, :], rk_far), (cqk[:, 1, :], rq_far)):
                sp.dma_start(dst, src).then_inc(w_in, 16)
            sp.dma_start(ws2_s[0:I], ws2.rearrange("c i d -> i c d")).then_inc(w_in, 16)
            sp.dma_start(RV[0:DIST, :, :], rv_rows).then_inc(w_in, 16)
            sp.dma_start(bp_s, b_proj.partition_broadcast(P)).then_inc(w_in, 16)
            sp.dma_start(gb_s, gate_b.partition_broadcast(P)).then_inc(w_in, 16)
            sp.dma_start(slot_s, slot_c.partition_broadcast(P)).then_inc(w_in, 16)
            sp.dma_start(vm_s, vmask_c).then_inc(w_in, 16)
            sp.dma_start(rvf_s, rv_far).then_inc(w_in, 16)
            sp.wait_ge(tabs_cut, 1)
            parts_out(tab_stack[:, :, 0, :], tprt[:, :, 0, :], K_PART, tabs_out)
            parts_out(tab_stack[:, :, 1, :], tprt[:, :, 1, :], Q_PART, tabs_out)
            sp.wait_ge(zero_set, 1)
            sp.dma_start(dq_d[:, 0:N], Z[0:DIST, :]).then_inc(zeros_out, 16)
            sp.dma_start(dq_d[:, N:DROW], Z[0:DIST, 0:P]).then_inc(zeros_out, 16)
            sp.dma_start(dp_d[:, 0:N], Z[0:DIST, :]).then_inc(zeros_out, 16)
            sp.dma_start(dp_d[:, N:DROW], Z[0:DIST, 0:P]).then_inc(zeros_out, 16)
            sp.dma_start(pa_d.rearrange("(a p) n -> p a n", p=P), Z[:, :].rearrange("p (a n) -> p a n", n=P)).then_inc(zeros_out, 16)
            for n in range(E * CAP // 1024):
                sp.dma_start(xb_d[n * 1024:(n + 1) * 1024, :].rearrange("(p a) n -> p (a n)", p=P),
                             Z[:, :]).then_inc(zeros_out, 16)
            Zb = Z[0:H, :].bitcast(BF16)
            for n in range(3):
                for m in range(T // 1024):
                    sp.dma_start(q_far[:, n, m * 1024:(m + 1) * 1024], Zb[:, 0:1024]).then_inc(zeros_out, 16)

            def stores(g, p, k2):
                tok = bass.ds(g * 512, 512)
                sp.wait_ge(q_cut, g + 1)
                parts_out(q_stack[:, :, tok], QP[p], Q_PART, stacks_out[p])
                sp.wait_ge(k_cut, g + 1)
                parts_out(k_stack[:, :, tok], KP[p], K_PART, stacks_out[p])
                sp.wait_ge(c_cut, g + 1)
                for m in range(2):
                    sp.dma_start(q_far[:, 3 + 3 * m:6 + 3 * m, tok], CP[p][16 * m:16 * m + 16, :, :]).then_inc(stacks_out[p], 16)
                    sp.dma_start(k_far[:, 3 * m:3 * m + 3, tok], CP[p][32 + 16 * m:48 + 16 * m, :, :]).then_inc(stacks_out[p], 16)

            turns(sp, G, stores)
            sp.wait_ge(zeros_out, ZEROS)
            for p in range(2):
                sp.wait_ge(stacks_out[p], STORES * (G // 2))
            sp.wait_ge(tabs_out, 96)
            sp.wait_ge(pads_set, 1)
            sp.wait_ge(kconst_in, 64)
            sp.wait_ge(idx_ready, 1)
            sp.wait_ge(psum_zeroed, 1)

            def load_stacks(i, c):
                h, r = (4 * i + c) % HEADS, c % 4
                b, hh = batch_of(h), h % H
                tok = bass.ds(b * N, N)
                qs = q_stack.rearrange("(h d) n t -> h (d n) t", h=H)[bass.ds(hh, 1), :, tok].rearrange("a n t -> (a n) t")
                sp.dma_start(Qs[0:48, r, :], qs).then_inc(stack_in[r], 16)
                sp.dma_start(Qs[ROW_M:ROW_M + 9, r, :], q_far[bass.ds(hh, 1), :, tok].rearrange("a n t -> (a n) t")
                             ).then_inc(stack_in[r], 16)
                ks = k_stack.rearrange("(h d) n t -> h (d n) t", h=H)[bass.ds(hh, 1), :, tok].rearrange("a n t -> (a n) t")
                kf = k_far[bass.ds(hh, 1), :, tok].rearrange("a (v n) t -> n (a v) t", v=2)
                for v in range(2):
                    sp.dma_start(Ks[0:48, r, v, :], ks).then_inc(stack_in[r], 16)
                sp.dma_start(Ks[ROW_K:ROWS, r, :, :], kf).then_inc(stack_in[r], 16)
                sp.dma_start(tab[0:48, r, :, :],
                             tab_stack.rearrange("(h d) n v p -> h (d n) v p", h=H)[bass.ds(hh, 1), :, :, :].rearrange(
                                 "a n v p -> (a n) v p")).then_inc(stack_in[r], 16)

            def shear(s, J0, J1, t):
                return rows(t, (P * J0 + TILE * s) * P + TILE - 1,
                            [[P - 1, TILE], [P * P, J1 - J0], [1, WIN]])

            def window_out(c, i, part):
                h = 4 * i + c
                sp.wait_ge(s2_read, SLOTS * h + 8 * part + 8)
                wait(sp, pa_in, 16 * h)
                for s in range(4):
                    src = rows(PT[:, :], 0, PT[TILE * s:TILE * s + TILE, 0:1].ap)
                    base = PT[TILE * s:TILE * s + TILE, TILE * s + 4 * part * (N + P):TILE * s + 4 * part * (N + P) + WIN]
                    src = rows(base, base.offset, [list(base.ap[0]), [N + P, 4], [1, WIN]])
                    sp.dma_start(shear(s, 4 * part, 4 * part + 4, pa_d), src).then_inc(pa_out[part], 16)

            def iteration(i, c, peeled):
                h = 4 * i + c
                on = lambda n: (not peeled) or 0 <= c + n < HEADS
                if on(-1):
                    window_out(c - 1, i, 1)
                if on(3):
                    wait(sp, s2_ready, SLOTS * h)
                    load_stacks(i, c + 3)
                if on(-1):
                    sp.wait_ge(pa_out[0], 64 * h)
                    sp.wait_ge(pa_out[1], 64 * h)
                    wait(sp, dp_psum, h - 1)
                    sp.dma_start(pa_s[:, :, :], pa_d.rearrange("(a p) n -> p a n", p=P)).then_inc(pa_in, 16)
                if on(2):
                    sp.wait_ge(aj_copied, 2 * h + 6)
                    if not peeled or c + 1 >= 0:
                        sp.wait_ge(wt_in[(c + 1) % 4], 64 * (i + (c + 1) // 4 + 1))
                    sp.dma_start(aj_d.rearrange("(a p) n -> p a n", p=P), aj_e[:, :, :]).then_inc(aj_out, 16)
                if on(2):
                    sp.wait_ge(aj_out, 16 * (h + 3))
                    wait(sp, s2_ready, SLOTS * (h - 1))
                    for s in range(4):
                        sp.dma_start(WT[TILE * s:TILE * s + TILE, (c + 2) % 4, :, :],
                                     shear(s, 0, NJ, aj_d)).then_inc(wt_in[(c + 2) % 4], 16)
                if on(0):
                    window_out(c, i, 0)
                if on(-1):
                    sp.wait_ge(dp_copied, h)
                    wait(sp, dp_in, 16 * (h - 1))
                    sp.dma_start(dp_d[:, 64:64 + N], dp_e[0:DIST, :]).then_inc(dp_out, 16)
                if on(3):
                    sp.wait_ge(dq_copied, h + 4)
                    wait(sp, dq_in, 16 * (h + 3))
                    sp.dma_start(dq_d[:, 64:64 + N], dq_e[0:DIST, :]).then_inc(dq_out, 16)
                if on(-1):
                    sp.wait_ge(dp_out, 16 * h)
                    wait(sp, rel_done, h - 1)
                    sp.dma_start(dp_s[0:DIST, :], rows(dp_d, DIST, [[DROW - 1, DIST], [1, N]])).then_inc(dp_in, 16)
                if on(3):
                    sp.wait_ge(dq_out, 16 * (h + 4))
                    wait(sp, aj_psum, 2 * h + 6)
                    sp.dma_start(dq_s[0:DIST, :], rows(dq_d, 1, [[DROW + 1, DIST], [1, N]])).then_inc(dq_in, 16)

            steps = iterations(sp, iteration)
            next(steps)
            sp.wait_ge(scattered, 16 * NB * TOPK)

            sp.wait_ge(dp_psum, hm - 1)

            def load_rows(e, p):
                sp.dma_start(XB[p], xb_d[bass.ds(e * 4 * CAP, 4 * CAP), :].rearrange("(a p) c -> p a c", p=P)).then_inc(ew_in[p], 16)
                sp.dma_start(W13[p].rearrange("p m w i -> p (m w i)"),
                             w13[:, bass.ds(e * 4, 4), :, :].rearrange("p m w i -> p (m w i)")).then_inc(ew_in[p], 16)

            def load_w2(e, p):
                sp.dma_start(W2[p][0:I, :, :], w2[:, bass.ds(e * 4, 4), :]).then_inc(w2_in[p], 16)

            def four(e, p, k):
                if after(e, QUADS, 2):
                    sp.wait_ge(ex_h, e + 1)
                    load_rows(e + 2, p)
                    sp.wait_ge(ex_y, e + 1)
                    load_w2(e + 2, p)
                sp.wait_ge(ex_yc, e + 1)
                sp.dma_start(yb_d[bass.ds(e * 4 * CAP, 4 * CAP), :].rearrange("(m s) c -> s m c", s=CAP), EY[p]
                             ).then_inc(ex_out[p], 16)

            for p in range(2):
                load_rows(p, p)
            for p in range(2):
                load_w2(p, p)
            turns(sp, QUADS, four)
            for _ in steps:
                pass
            sp.wait_ge(stack_in[0], 96 * (HEADS // 4 + 1))
            sp.wait_ge(dq_in, 16 * (HEADS + 1))
            ov = out.rearrange("b (j p) c -> p (b j) c", p=P)
            for g in range(G):
                sp.wait_ge(pj_add, g + 1)
                sp.dma_start(ov[:, g * 4:g * 4 + 4, :], X[:, g * 4:g * 4 + 4, :]).then_inc(stored, 16)
            sp.wait_ge(stored, 16 * G)

        @block.gpsimd
        def _(pool):
            pool.memset(Z, 0.0).then_inc(zero_set, 1)
            pool.dma_start(trib, tri_c).then_inc(c_in, 16)
            pool.memset(oneb, 1.0).then_inc(one_set, 1)
            pool.memset(Ks[:, :, :, :], 0.0).then_inc(k_zeroed, 1)
            pool.wait_ge(k_zeroed, 1)
            for r in range(4):
                pool.dma_start(Ks[ROW_M:ROW_K, r, :, :], kconst_c).then_inc(kconst_in, 16)
            pool.memset(Qs[:, :, :], 1.0)
            pool.memset(tab[:, :, :, :], 0.0)
            for J in range(2):
                pool.memset(Vst[:, J, :, :, :], 1.0)
            pool.memset(zcol[:, :], 0.0).then_inc(zcol_set, 1)
            pool.sem_inc(pads_set, 1)
            pool.wait_ge(zcol_set, 1)
            zero_row = zcol[:, :].broadcast_to([P, 512])
            pool.wait_ge(c_in, 16)

            def group(g, p, k2):
                pool.wait_ge(xn_ready, g + 1)
                pool.tensor_copy(XNA[:, bass.ds(g * 4, 4), :], XN).then_inc(xna_copied, 1)
                for m, (F, R, Pt, rdy, done, np_) in enumerate(
                        ((KF, KR, KP[p], kf_ready, k_cut, P), (CF, CR, CP[p], cf_ready, c_cut, 64))):
                    def gstep(ins, k):
                        ins.then_inc(cut_step, 1)
                        pool.wait_ge(cut_step, g * 6 + (3 * m + k))

                    pool.wait_ge(rdy, g + 1)
                    gstep(pool.tensor_tensor(R[0:np_, :], F[0:np_, :], Pt[0:np_, 0, :], ALU.subtract), 1)
                    gstep(pool.tensor_tensor(Pt[0:np_, 1, :], R[0:np_, :], zero_row[0:np_, :], ALU.add), 2)
                    gstep(pool.tensor_tensor(R[0:np_, :], R[0:np_, :], Pt[0:np_, 1, :], ALU.subtract), 3)
                    pool.tensor_tensor(Pt[0:np_, 2, :], R[0:np_, :], zero_row[0:np_, :], ALU.add).then_inc(done, 1)

            turns(pool, G, group)
            pool.wait_ge(idx_ready, 1)
            pool.wait_ge(xna_copied, G)
            for blk in range(NB):
                for k in range(TOPK):
                    pool.indirect_dma_start(
                        out=xb_d, out_offset=bass.IndirectOffsetOnAxis(ap=idx[:, blk, k:k + 1], axis=0),
                        in_=XNA[:, blk, :], in_offset=None, bounds_check=E * CAP - 1, oob_is_err=False,
                    ).then_inc(scattered, 16)
            for p in range(2):
                pool.wait_ge(ex_out[p], 16 * (QUADS // 2))
            pool.memset(yg[:, :, :], 0.0).then_inc(y_added, 1)
            for blk in range(NB):
                def ystep(m, *a):
                    pool.tensor_tensor(*a).then_inc(y_added, 1)
                    pool.wait_ge(y_added, 5 * blk + m + 1)

                pool.wait_ge(y_added, 5 * blk + 1)
                for k in range(TOPK):
                    pool.indirect_dma_start(
                        out=yg[:, k, :], out_offset=None, in_=yb_d,
                        in_offset=bass.IndirectOffsetOnAxis(ap=idx[:, blk, k:k + 1], axis=0),
                        bounds_check=E * CAP - 1, oob_is_err=False,
                    ).then_inc(gathered, 16)
                pool.wait_ge(gathered, 16 * TOPK * (blk + 1))
                ystep(1, yg[:, :, :], yg[:, :, :], wts[:, :, blk:blk + 1].broadcast_to([P, TOPK, C]), ALU.mult)
                ystep(2, yg[:, 0:3, :], yg[:, 0:3, :], yg[:, 3:6, :], ALU.add)
                ystep(3, yg[:, 0, :], yg[:, 0, :], yg[:, 1, :], ALU.add)
                ystep(4, yg[:, 0, :], yg[:, 0, :], yg[:, 2, :], ALU.add)
                ystep(5, X[:, blk, :], X[:, blk, :], yg[:, 0, :], ALU.add)

        @block.tensor
        def _(pe):
            def mm(o, l, r, start=True, stop=True):
                return pe.matmul(o, l, r, start=start, stop=stop, skip_group_check=True)

            pe.sem_inc(fin_psum, 1)
            pe.wait_ge(w_in, 16 * 13)
            pe.wait_ge(tabs_in, 48)
            for v in range(8):
                ins = mm(PS[:, v // 4, (v % 4) * P:(v % 4 + 1) * P], vm_s[:, v * P:(v + 1) * P], rvf_s,
                         start=v % 4 == 0)
            ins.then_inc(tv_psum, 1)
            pe.wait_ge(tv_ready, 1)
            pe.wait_ge(cqk_scaled, 1)

            def transposes(g):
                pe.wait_ge(xn_ready, g + 1)
                wait(pe, z_added, g - 1)
                for q in range(4):
                    ins = pe.transpose(PS[:, 0, q * P:(q + 1) * P], XN[:, q, :], ident[:, :])
                ins.then_inc(xt_psum, 1)

            def shared_out(g):
                pe.wait_ge(sh_ready, 2 * g + 2)
                for q in range(4):
                    for a in range(2):
                        ins = mm(PS[:, 0, q * P:(q + 1) * P], HG[0:I, a, q * P:(q + 1) * P], ws2_s[0:I, a, :],
                                 start=q == 0 and a == 0, stop=a == 1)
                ins.then_inc(z_psum, 1)

            def group(g, p, k2):
                XTp = XT[:, p, :]
                pe.wait_ge(xt_ready, g + 1)
                wait(pe, cf_ready, g)
                mm(PS[:, 1, :], wq_s[:, 0:C], XTp).then_inc(qk_psum, 1)
                wait(pe, vg_copied, g)
                for q in range(4):
                    ins = mm(PS[:, 3 + q // 2, (q % 2) * 192:(q % 2) * 192 + 192], XT[:, p, q * P:(q + 1) * P],
                             wq_s[:, 2 * C:3 * C + E], start=q % 2 == 0)
                ins.then_inc(vg_psum, 1)
                if not isinstance(g, int) or g > 0:
                    shared_out(g - 1)
                mm(PS[:, 2, :], wq_s[:, C:2 * C], XTp).then_inc(qk_psum, 1)
                mm(PS[0:I, 5, :], ws1_s[:, 0:I], XTp)
                mm(PS[0:I, 6, :], ws3_s[:, 0:I], XTp).then_inc(sh_psum, 1)
                mm(PS[0:I, 7, :], ws1_s[:, I:2 * I], XTp)
                pe.wait_ge(kf_ready, g + 1)
                mm(PS[0:I, 2, :], ws3_s[:, I:2 * I], XTp).then_inc(sh_psum, 1)
                if after(g, G):
                    transposes(g + 1)
                pe.wait_ge(qf_ready, g + 1)
                mm(PS[0:32, 1, :], cqk[:, 0, :], QF)
                mm(PS[32:64, 1, :], cqk[:, 1, :], KF).then_inc(c_psum, 1)

            transposes(0)
            turns(pe, G, group)
            shared_out(G - 1)
            pe.wait_ge(mask_ready, 1)
            pe.wait_ge(z_added, G)
            for m in range(NB // 8):
                mm(PS[:, m, :], trib, maskb[:, 8 * m:8 * m + 8, :].rearrange("p a e -> p (a e)"), stop=False)
                mm(PS[:, m, :], oneb, prevb[:, 8 * m:8 * m + 8, :].rearrange("p a e -> p (a e)"),
                   start=False).then_inc(pos_psum, 1)
            pe.wait_ge(pos_read, 1)
            pe.wait_ge(psum_zeroed, 1)

            def bias(bank, half, J, r):
                ins = None
                for s in range(4):
                    t = 4 * J + s
                    w = span(TILE * (t - 1), TILE * (t + 2), half)
                    w = w and (max(w[0], 0), min(w[1], N))
                    if w and w[0] < w[1]:
                        a = w[0] - TILE * (t - 1)
                        ins = mm(PS[TILE * s:TILE * s + TILE, bank, w[0] - 512 * half:w[1] - 512 * half],
                                 ident[:, TILE * s:TILE * s + TILE], WT[:, r, J, a:a + w[1] - w[0]], start=False)
                return ins

            def scores(bank, half, J, r):
                ins, first = None, True
                lo, hi = P * J - TILE, P * J + P + TILE
                for v, a, b in ((1, 0, lo), (0, hi, N)):
                    w = span(a, b, half)
                    if w:
                        ins = mm(PS[:, bank, w[0] - 512 * half:w[1] - 512 * half], Ks[:, r, v, P * J:P * J + P],
                                 Qs[:, r, w[0]:w[1]], start=first)
                        first = False
                assert not first
                pieces = []
                for s in range(4):
                    t = 4 * J + s
                    own = []
                    for kind, a, b in (("U", max(0, lo), TILE * (t - 1)), ("W", max(0, TILE * (t - 1)), min(N, TILE * (t + 2))),
                                       ("L", TILE * (t + 2), min(N, hi))):
                        w = span(a, b, half)
                        if w:
                            own.append((s, kind, w))
                    pieces.append(own)
                for n in range(3):
                    for own in pieces:
                        if n < len(own):
                            s, kind, w = own[n]
                            k = ROWS if kind != "W" else ROW_C
                            ins = mm(
                               PS[TILE * s:TILE * s + TILE, bank, w[0] - 512 * half:w[1] - 512 * half],
                               Ks[0:k, r, 1 if kind == "U" else 0, P * J + TILE * s:P * J + TILE * s + TILE],
                               Qs[0:k, r, w[0]:w[1]], start=False)
                return bias(bank, half, J, r) or ins

            def unit(i, c, u, which):
                h, r = 4 * i + c, c % 4
                ready, read, bank = ((s1_ready, s1_read, 0), (s2_ready, s2_read, 2))[which]
                if which == 0 and u == 0:
                    pe.wait_ge(stack_in[r], 96 * (i + c // 4 + 1))
                    pe.wait_ge(wt_in[r], 64 * (i + c // 4 + 1))
                if which == 1 and u == 0:
                    pe.wait_ge(mrow_ready, h + 1)
                wait(pe, read, SLOTS * h + u - 1)
                J, half = u // 2, u % 2
                scores(bank + u % 2, half, J, r).then_inc(ready, 1)

            def values(i, c, J):
                h, p = 4 * i + c, c % 2
                pe.wait_ge(s2_read, SLOTS * h + 2 * J + 2)
                if J == 0:
                    pe.wait_ge(v_ready, h + 1)
                    wait(pe, o_copied, h - 1)
                own = []
                for q in range(4):
                    mine, t = [], 8 * q
                    while t < 8 * q + 8:
                        v, e = value_variant(t, J), t
                        while e < 8 * q + 8 and value_variant(e, J) == v:
                            e += 1
                        mine.append((q, v, t, e))
                        t = e
                    own.append(mine)
                for n in range(max(map(len, own))):
                    for mine in own:
                        if n < len(mine):
                            q, v, t, e = mine[n]
                            ins = mm(PS[TILE * q:TILE * q + 9, 4 + p, TILE * (t - 8 * q):TILE * (e - 8 * q)],
                                     Vst[:, p, J, v, :], PT[:, TILE + N * J + TILE * t:TILE + N * J + TILE * e],
                                     start=J == 0 and n == 0, stop=J == NJ - 1)
                ins.then_inc(pv_done, 1)

            def misc_free(h, *which):
                for s, v, *per in which:
                    most = HEADS + (s is dq_copied)
                    wait(pe, s, (per[0] if per else 1) * (v if not isinstance(v, int) else min(v, most)))

            def iteration(i, c, peeled):
                h = 4 * i + c
                on = lambda n: (not peeled) or 0 <= c + n < HEADS
                for s in range(SLOTS):
                    if s == 3 and on(0):
                        pe.wait_ge(mparts_ready, h + 1)
                        for I_ in range(NJ):
                            ins = mm(MISC[0:3, I_ * P:(I_ + 1) * P], mparts[:, I_, :], identb[:, :], start=I_ % 4 == 0)
                        ins.then_inc(mrow_psum, 1)
                    if on(1):
                        unit(i, c + 1, s, 0)
                    if s == 0 and on(0):
                        pe.wait_ge(s1_read, SLOTS * h + SLOTS)
                        misc_free(h, (dp_copied, h - 1), (dq_copied, h + 3))
                        for I_ in range(NJ):
                            ins = pe.transpose(MISC[:, I_ * P:(I_ + 1) * P], accm[:, c % 2, I_ * P:(I_ + 1) * P], ident[:, :])
                        ins.then_inc(accT_psum, 1)
                    if s == 14 and on(3):
                        r = (c + 3) % 4
                        pe.wait_ge(stack_in[r], 96 * (i + (c + 3) // 4 + 1))
                        misc_free(h, (mrow_ready, h + 1), (on_ready, h - 1), (aj_copied, h + 3, 2), (dp_copied, h))
                        for a in range(2):
                            ins = mm(MISC[:, 512 * a:512 * a + 512], tab[:, r, 0, :], Qs[:, r, 512 * a:512 * a + 512])
                        ins.then_inc(dq_psum, 1)
                    if s >= LAG and on(0):
                        unit(i, c, s - LAG, 1)
                    if s < LAG and on(-1):
                        unit(i, c - 1, s + SLOTS - LAG, 1)
                    if s == 3 and on(-2):
                        pe.wait_ge(dp_in, 16 * (h - 1))
                        pe.wait_ge(rv_ready, h - 1)
                        for q in range(4):
                            ins = mm(PS[TILE * q:TILE * q + HD, 4 + c % 2, 0:256], RVc[0:DIST, c % 2, :],
                                     dp_s[0:DIST, 256 * q:256 * q + 256], start=False)
                        ins.then_inc(rel_done, 1)
                    if s == 9 and on(-2):
                        misc_free(h, (aj_copied, h + 3, 2), (mrow_ready, h + 1))
                        pe.wait_ge(o_copied, h - 1)
                        for a in range(2):
                            ins = pe.transpose(MISC[:, a * P:a * P + P], Oev[:, c % 2, a * P:a * P + P], ident[:, :])
                        ins.then_inc(fin_psum, 1)
                    if s in (5, 7) and on(2):
                        r, part = (c + 2) % 4, (s - 5) // 2
                        if part == 0:
                            misc_free(h, (mrow_ready, h + 1), (dq_copied, h + 3))
                            pe.wait_ge(dq_in, 16 * (h + 3))
                        else:
                            pe.wait_ge(aj_copied, 2 * h + 5)
                        for a in range(4):
                            J = 4 * part + a
                            ins = mm(PS[:, 7, a * P:(a + 1) * P], Ks[:, r, 0, J * P:(J + 1) * P], tab[:, r, 1, :],
                                     start=a == 0)
                        ins.then_inc(ajk_psum, 1)
                        for a in range(4):
                            J = 4 * part + a
                            ins = pe.transpose(PS[:, 6, a * P:a * P + DIST], dq_s[0:DIST, J * P:(J + 1) * P],
                                               ident[0:DIST, 0:DIST])
                        ins.then_inc(aj_psum, 1)
                    if s == 12 and on(-1):
                        misc_free(h, (aj_copied, h + 3, 2), (on_ready, h - 1))
                        pe.wait_ge(pa_in, 16 * h)
                        for J in range(NJ):
                            ins = pe.transpose(MISC[:, J * P:(J + 1) * P], pa_s[:, J, :], ident[:, :])
                        ins.then_inc(dp_psum, 1)
                    if s % 2 and s >= LAG + 3 and on(0):
                        values(i, c, (s - LAG - 3) // 2)
                    if s % 2 and s < LAG + 3 and on(-1):
                        values(i, c - 1, (s - LAG - 3 + SLOTS) // 2)

            steps = iterations(pe, iteration)
            next(steps)
            pe.wait_ge(dq_copied, hm + 3)
            pe.wait_ge(s1_read, SLOTS * (hm + 1))
            pe.wait_ge(s2_read, SLOTS * hm - LAG)

            def hidden(e, p, k):
                pe.wait_ge(ew_in[p], 32 * (k + 1))
                for a in range(2):
                    ins = pe.transpose(PS[:, p, a * P:(a + 1) * P], XB[p][:, a, :], ident[:, :])
                ins.then_inc(ex_T, 1)
                pe.wait_ge(ex_Tc, e + 1)
                for m in range(4):
                    for w in range(2):
                        ins = mm(PS[0:I, 2 + p, (4 * w + m) * CAP:(4 * w + m + 1) * CAP], W13[p][:, m, w, :],
                                 XBT[p][:, m * CAP:(m + 1) * CAP], start=m == 0 and w == 0)
                ins.then_inc(ex_h, 1)

            def four(e, p, k):
                if after(e, QUADS):
                    hidden(e + 1, 1 - p, k + p)
                pe.wait_ge(ex_g, e + 1)
                pe.wait_ge(w2_in[p], 16 * (k + 1))
                wait(pe, ex_yc, e - 1)
                for m in range(4):
                    ins = mm(PS[0:CAP, 6 + p, m * C:(m + 1) * C], EG[p][:, m * CAP:(m + 1) * CAP],
                             W2[p][0:I, m, :], start=m == 0)
                ins.then_inc(ex_y, 1)

            hidden(0, 0, 0)
            turns(pe, QUADS, four)
            pe.wait_ge(ex_yc, QUADS)
            for _ in steps:
                pass
            def columns_of(g):
                wait(pe, pj_Tc, g - 1)
                for q in range(4):
                    ins = pe.transpose(PS[:, g % 2, q * P:(q + 1) * P], ON[:, 4 * g + q, :], ident[:, :])
                ins.then_inc(pj_T, 1)

            pe.wait_ge(on_ready, HEADS)
            columns_of(0)
            for g in range(G):
                if g + 1 < G:
                    columns_of(g + 1)
                pe.wait_ge(pj_Tc, g + 1)
                wait(pe, pj_add, g - 1)
                for q in range(4):
                    ins = mm(PS[:, 2 + g % 2, q * P:(q + 1) * P], accm[:, g % 2, q * P:(q + 1) * P], wp[:, :], start=q == 0)
                ins.then_inc(pj_y, 1)

        @block.scalar
        def _(act):
            act.wait_ge(stats_ready, 1)
            act.activation(rstd, rstd, ACT.Sqrt).then_inc(rstd_ready, 1)

            def columns(g, p):
                act.wait_ge(xt_psum, g + 1)
                wait(act, sh_psum, 2 * g - 2)
                act.activation(XT[:, p, :], PS[:, 0, :], ACT.Copy).then_inc(xt_ready, 1)

            def group(g, p, k2):
                act.wait_ge(qk_psum, 2 * g + 1)
                wait(act, stacks_out[p], STORES * k2)
                wait(act, q_cut, g)
                wait(act, c_psum, g)
                act.activation(QF, PS[:, 1, :], ACT.Copy, scale=SC)
                act.activation(QP[p][:, 0, :], PS[:, 1, :], ACT.Copy, scale=SC).then_inc(qf_ready, 1)
                act.wait_ge(qk_psum, 2 * g + 2)
                wait(act, k_cut, g)
                act.activation(KF, PS[:, 2, :], ACT.Copy)
                act.activation(KP[p][:, 0, :], PS[:, 2, :], ACT.Copy).then_inc(kf_ready, 1)
                wait(act, sh_ready, 2 * g)
                for a in range(2):
                    act.wait_ge(sh_psum, 2 * g + a + 1)
                    act.activation(EX[0:I, a, :], PS[0:I, 5 + 2 * a, :], ACT.Silu).then_inc(sh_silu, 1)
                if after(g, G):
                    columns(g + 1, 1 - p)
                act.wait_ge(c_psum, g + 1)
                wait(act, c_cut, g)
                act.activation(CF[0:64, :], PS[0:64, 1, :], ACT.Copy)
                act.activation(CP[p][0:64, 0, :], PS[0:64, 1, :], ACT.Copy).then_inc(cf_ready, 1)

            columns(0, 0)
            turns(act, G, group)
            act.wait_ge(route_max, 1)
            act.activation(RB[:, :, :].rearrange("p a e -> p (a e)"), RB[:, :, :].rearrange("p a e -> p (a e)"),
                           ACT.Exp).then_inc(route_exp, 1)

            def exps(i, c, u):
                h = 4 * i + c
                act.wait_ge(s2_ready, SLOTS * h + u + 1)
                J, half = u // 2, u % 2
                if isinstance(h, int) and h == 0 and u == 0:
                    act.wait_ge(wts_ready, 1)
                if half == 0:
                    wait(act, pv_done, NJ * (h - 1) + J + 1)
                    wait(act, pa_out[J // 4], 64 * h)
                act.activation(PT[:, TILE + N * J + 512 * half:TILE + N * J + 512 * half + 512],
                               PS[:, 2 + u % 2, :], ACT.Exp).then_inc(s2_read, 1)

            def iteration(i, c, peeled):
                h = 4 * i + c
                on = lambda n: (not peeled) or 0 <= c + n < HEADS
                for s in range(SLOTS):
                    if s < 2 and on(1):
                        act.wait_ge(s1_ready, SLOTS * (h + 1) + s + 1)
                        if s == 0:
                            wait(act, s1_read, SLOTS * (h + 1))
                            wait(act, accT_psum, h)
                        act.activation(accm[:, (c + 1) % 2, 512 * s:512 * s + 512], PS[:, s, :], ACT.Copy).then_inc(s1_read, 1)
                    if s == 3 and on(0):
                        act.wait_ge(mrow_psum, h + 1)
                        act.wait_ge(s1_ready, SLOTS * h + SLOTS)
                        act.activation(Qs[ROW_M:ROW_M + 3, c % 4, :], MISC[0:3, :], ACT.Copy).then_inc(mrow_ready, 1)
                    if s == 14 and on(3):
                        act.wait_ge(dq_psum, h + 4)
                        wait(act, dq_out, 16 * (h + 3))
                        act.activation(dq_e[:, :], MISC, ACT.Copy).then_inc(dq_copied, 1)
                    if s in (5, 7) and on(2):
                        part = (s - 5) // 2
                        act.wait_ge(ajk_psum, 2 * h + 5 + part)
                        wait(act, aj_out, 16 * (h + 2))
                        act.activation(aj_e[:, 4 * part:4 * part + 4, 0:DIST],
                                       PS[:, 7, :].rearrange("p (a n) -> p a n", n=P)[:, :, 0:DIST],
                                       ACT.Copy).then_inc(ajk_copied, 1)
                    if s >= LAG and on(0):
                        exps(i, c, s - LAG)
                    if s < LAG and on(-1):
                        exps(i, c - 1, s + SLOTS - LAG)
                    if s == 4 and on(-2):
                        act.wait_ge(rel_done, h - 1)
                        act.wait_ge(fin_psum, h - 1)
                        act.activation(Oev[:, c % 2, :], PS[:, 4 + c % 2, 0:256], ACT.Copy).then_inc(o_copied, 1)

            steps = iterations(act, iteration)
            next(steps)
            act.wait_ge(dp_out, 16 * (hm - 1))
            act.wait_ge(dq_out, 16 * (hm + 3))

            def hidden(e, p, k):
                act.wait_ge(ex_T, e + 1)
                wait(act, ex_h, e - 1)
                act.activation(XBT[p], PS[:, p, 0:256], ACT.Copy).then_inc(ex_Tc, 1)
                act.wait_ge(ex_h, e + 1)
                wait(act, ex_g, e - 1)
                act.activation(EH[p], PS[0:I, 2 + p, 0:256], ACT.Silu).then_inc(ex_silu, 1)

            def four(e, p, k):
                if after(e, QUADS):
                    hidden(e + 1, 1 - p, k + p)
                act.wait_ge(ex_y, e + 1)
                wait(act, ex_out[p], 16 * k)
                act.activation(EY[p], PS[0:CAP, 6 + p, :].rearrange("p (m c) -> p m c", c=C), ACT.Copy).then_inc(ex_yc, 1)

            act.wait_ge(aj_out, 16 * (hm + 2))
            hidden(0, 0, 0)
            turns(act, QUADS, four)
            for p in range(2):
                act.wait_ge(ex_out[p], 16 * (QUADS // 2))
            for _ in steps:
                pass
            for g in range(G):
                act.wait_ge(pj_T, g + 1)
                wait(act, pj_y, g - 1)
                act.activation(accm[:, g % 2, 0:512], PS[:, g % 2, :], ACT.Copy).then_inc(pj_Tc, 1)

        @block.vector
        def _(dve):
            n = [0]

            def step(ins):
                n[0] += 1
                ins.then_inc(dve_step, 1)
                dve.wait_ge(dve_step, n[0])

            dve.wait_ge(tabs_in, 48)
            step(dve.tensor_scalar(tres[:, 1, :], tres[:, 1, :], SC, None, ALU.mult))
            for k in range(2):
                step(dve.tensor_copy(tprt[:, k, :, :], tres[:, :, :]))
                step(dve.tensor_tensor(tres[:, :, :], tres[:, :, :], tprt[:, k, :, :], ALU.subtract))
            dve.tensor_copy(tprt[:, 2, :, :], tres[:, :, :]).then_inc(tabs_cut, 1)
            dve.wait_ge(w_in, 16 * 13)
            dve.tensor_copy(identb[:, :], ident[:, :])
            dve.tensor_scalar(cqk[:, 1, :], cqk[:, 1, :], SC, None, ALU.mult).then_inc(cqk_scaled, 1)
            dve.wait_ge(tv_psum, 1)
            for a in range(2):
                ins = dve.tensor_copy(TV[:, :, 4 * a:4 * a + 4, :].rearrange("p h v d -> p v h d"),
                                      PS[:, a, :].rearrange("p (v h d) -> p v h d", v=4, h=H))
            ins.then_inc(tv_ready, 1)
            dve.wait_ge(x_in, 64)
            for k in range(NB):
                ins = dve.bn_stats(st6[:, k, :], X[:, k, :])
            ins.then_inc(bn_done, 1)
            dve.wait_ge(bn_done, 1)
            step(dve.tensor_copy(tmpn[:, 0, :], st6[:, :, 1]))
            step(dve.tensor_tensor(mean, tmpn[:, 0, :], st6[:, :, 4], ALU.add))
            step(dve.tensor_tensor(tmpn[:, 0, :], tmpn[:, 0, :], st6[:, :, 4], ALU.subtract))
            step(dve.tensor_tensor(tmpn[:, 1, :], tmpn[:, 0, :], tmpn[:, 0, :], ALU.mult))
            step(dve.tensor_tensor(rstd, st6[:, :, 2], st6[:, :, 5], ALU.add))
            step(dve.tensor_scalar(rstd, rstd, 1.0 / C, None, ALU.mult))
            step(dve.scalar_tensor_tensor(out=rstd, in0=tmpn[:, 1, :], scalar=0.25, in1=rstd, op0=ALU.mult, op1=ALU.add))
            step(dve.tensor_scalar(mean, mean, 0.5, None, ALU.mult))
            step(dve.tensor_scalar(rstd, rstd, 1e-5, None, ALU.add))
            dve.sem_inc(stats_ready, 1)
            dve.wait_ge(rstd_ready, 1)
            step(dve.reciprocal(rstd, rstd))
            base = n[0]

            def rows_of(g):
                wait(dve, xt_psum, g)
                wait(dve, xna_copied, g)
                for q in range(4):
                    ins = dve.tensor_scalar(XN[:, q, :], X[:, bass.ds(g * 4 + q, 1), :].rearrange("p a c -> p (a c)"),
                                            mean[:, bass.ds(g * 4 + q, 1)], rstd[:, bass.ds(g * 4 + q, 1)],
                                            ALU.subtract, ALU.mult)
                ins.then_inc(xn_ready, 1)

            def shared_add(g):
                dve.wait_ge(z_psum, g + 1)
                dve.tensor_tensor(X[:, bass.ds(g * 4, 4), :], X[:, bass.ds(g * 4, 4), :],
                                  PS[:, 0, :].rearrange("p (q c) -> p q c", q=4), ALU.add).then_inc(z_added, 1)

            PER = 3

            def group(g, p, k2):
                k = [0]

                def gstep(ins):
                    k[0] += 1
                    ins.then_inc(dve_step, 1)
                    dve.wait_ge(dve_step, g * PER + (base + k[0]))

                if after(g, G):
                    rows_of(g + 1)
                dve.wait_ge(xn_ready, g + 1)
                dve.tensor_tensor(X[:, bass.ds(g * 4, 4), :], X[:, bass.ds(g * 4, 4), :],
                                  bp_s[:, :].unsqueeze(1).broadcast_to([P, 4, C]), ALU.add)
                dve.wait_ge(qf_ready, g + 1)
                gstep(dve.tensor_tensor(QR, QF, QP[p][:, 0, :], ALU.subtract))
                gstep(dve.tensor_copy(QP[p][:, 1, :], QR))
                gstep(dve.tensor_tensor(QR, QR, QP[p][:, 1, :], ALU.subtract))
                dve.tensor_copy(QP[p][:, 2, :], QR).then_inc(q_cut, 1)
                dve.wait_ge(vg_psum, g + 1)
                VRf = VR[:, :, :, :, :].rearrange("p b h j d -> p b j h d")
                for a in range(2):
                    src = PS[:, 3 + a, 0:384].rearrange("p (q n) -> p q n", q=2)
                    for q in range(2):
                        dve.tensor_copy(
                            VRf[:, bass.ds(g // 2, 1), bass.ds((g % 2) * 4 + 2 * a + q, 1), :, :].rearrange("p b j h d -> p (b j h) d"),
                            src[:, q, 0:C].rearrange("p (h d) -> p h d", h=H))
                    ins = dve.tensor_copy(LG[:, bass.ds(g * 4 + 2 * a, 2), :], src[:, :, C:C + E])
                ins.then_inc(vg_copied, 1)
                if not isinstance(g, int) or g > 0:
                    shared_add(g - 1)
                for a in range(2):
                    dve.wait_ge(sh_silu, 2 * g + a + 1)
                    dve.tensor_tensor(HG[0:I, a, :], PS[0:I, 6 if a == 0 else 2, :], EX[0:I, a, :], ALU.mult).then_inc(sh_ready, 1)
                assert k[0] == PER

            rows_of(0)
            turns(dve, G, group)
            shared_add(G - 1)
            n[0] = base + PER * G

            dve.wait_ge(zeros_out, ZEROS)
            for p in range(2):
                dve.wait_ge(stacks_out[p], STORES * (G // 2))
            def over_e(a):
                return a.unsqueeze(2).broadcast_to([P, NB, E])

            dve.wait_ge(z_added, G)
            dve.wait_ge(vg_copied, G)
            step(dve.tensor_reduce(rmax, LG, AX.X, ALU.max))
            step(dve.tensor_tensor(RB, LG, over_e(rmax), ALU.subtract))
            dve.sem_inc(route_max, 1)
            dve.wait_ge(route_exp, 1)
            step(dve.tensor_reduce(rsum, RB, AX.X, ALU.add))
            step(dve.reciprocal(rsum, rsum))
            step(dve.tensor_tensor(LG, RB, over_e(rsum), ALU.mult))
            dve.memset(RV66[:, :, E:E + 2], BIG)
            step(dve.tensor_tensor(RV66[:, :, 0:E], LG, gb_s[:, :].unsqueeze(1).broadcast_to([P, NB, E]), ALU.add))
            for blk in range(NB):
                ins = dve.max(top8[:, blk, :], RV66[:, blk, :])
            step(ins)
            for blk in range(NB):
                ins = dve.match_replace(RV66[:, blk, :], top8[:, blk, :], RV66[:, blk, :], -BIG)
            step(ins)
            step(dve.tensor_scalar(maskb, RV66[:, :, 0:E], -BIG, None, ALU.is_equal))
            dve.wait_ge(xna_copied, G)
            step(dve.memset(prevb[:, 0, :], 0.0))
            for blk in range(1, NB):
                ins = dve.tensor_tensor(prevb[:, blk, :], prevb[:, blk - 1, :], maskb[:, blk - 1, :], ALU.add)
                step(ins)
            dve.sem_inc(mask_ready, 1)
            dve.wait_ge(one_set, 1)
            for m in range(NB // 8):
                dve.wait_ge(pos_psum, m + 1)
                pos = PS[:, m, :].rearrange("p (a e) -> p a e", e=E)
                b8 = slice(8 * m, 8 * m + 8)
                step(dve.scalar_tensor_tensor(out=RD[:, b8, :], in0=pos, scalar=float(CAP), in1=maskb[:, b8, :],
                                              op0=ALU.is_lt, op1=ALU.mult))
                step(dve.tensor_tensor(RC[:, b8, :], pos, slot_s[:, :].unsqueeze(1).broadcast_to([P, 8, E]), ALU.add))
                step(dve.tensor_tensor(RC[:, b8, :], RC[:, b8, :], RD[:, b8, :], ALU.mult))
            dve.sem_inc(pos_read, 1)
            for blk in range(NB):
                ins = dve.max(top8[:, blk, :], RC[:, blk, :])
            step(ins)
            step(dve.tensor_scalar(RV66[:, :, 0:8], top8, 0.5, 2.0 * E * CAP, ALU.is_lt, ALU.mult))
            step(dve.tensor_tensor(RV66[:, :, 0:8], RV66[:, :, 0:8], top8, ALU.add))
            step(dve.tensor_scalar(RV66[:, :, 0:8], RV66[:, :, 0:8], -1.0, None, ALU.add))
            dve.tensor_copy(idx[:, :, :], RV66[:, :, 0:8]).then_inc(idx_ready, 1)
            dve.memset(PS[:, 4, 0:256], 0.0)
            step(dve.memset(PS[:, 5, 0:256], 0.0))
            dve.memset(aj_e[:, :, DIST:P], 0.0)

            def weights(k):
                step(dve.tensor_tensor(RB, RC, top8[:, :, k:k + 1].broadcast_to([P, NB, E]), ALU.is_equal))
                step(dve.tensor_tensor(RB, RB, RD, ALU.mult))
                step(dve.tensor_reduce(wts[:, k, :], RB, AX.X, ALU.add))

            dve.sem_inc(psum_zeroed, 1)

            def iteration(i, c, peeled):
                h = 4 * i + c
                on = lambda m: (not peeled) or 0 <= c + m < HEADS
                if peeled and c == -3:
                    step(dve.tensor_tensor(RD, RD, LG, ALU.mult))
                if peeled and c < 0:
                    for k in range(2 * c + 6, 2 * c + 8):
                        weights(k)
                if peeled and c == -1:
                    dve.memset(PT[:, 0:TILE], 0.0)
                    dve.memset(PT[:, TILE + NJ * N:], 0.0).then_inc(wts_ready, 1)
                for s in range(SLOTS):
                    if on(1) and s >= 2:
                        dve.wait_ge(s1_ready, SLOTS * (h + 1) + s + 1)
                        dst = accm[:, (c + 1) % 2, 512 * (s % 2):512 * (s % 2) + 512]
                        dve.wait_ge(s1_read, SLOTS * (h + 1) + max(2, s - 1))
                        dve.tensor_tensor(dst, PS[:, s % 2, :], dst, ALU.max).then_inc(s1_read, 1)
                    if s == 0 and on(0):
                        dve.wait_ge(accT_psum, h + 1)

                        def hstep(ins, m):
                            ins.then_inc(max_step, 1)
                            dve.wait_ge(max_step, 6 * h + m)
                        hstep(dve.tensor_reduce(mx[:, 0, :], MISC.rearrange("p (a b) -> p a b", a=NJ), AX.X, ALU.max), 1)
                        wait(dve, mrow_psum, h)
                        hstep(dve.tensor_scalar(mx[:, 1, :], mx[:, 0, :], -1.0, None, ALU.mult), 2)
                        hstep(dve.tensor_copy(mparts[:, :, 0], mx[:, 1, :]), 3)
                        hstep(dve.tensor_tensor(mx[:, 2, :], mx[:, 1, :], mparts[:, :, 0], ALU.subtract), 4)
                        hstep(dve.tensor_copy(mparts[:, :, 1], mx[:, 2, :]), 5)
                        hstep(dve.tensor_tensor(mx[:, 3, :], mx[:, 2, :], mparts[:, :, 1], ALU.subtract), 6)
                        dve.tensor_copy(mparts[:, :, 2], mx[:, 3, :]).then_inc(mparts_ready, 1)
                    if s == 4 and on(0):
                        wait(dve, pv_done, NJ * (h - 1))
                        v = VR[:, bass.ds(batch_of(h), 1), bass.ds(h % H, 1), :, :].rearrange("p b h j d -> p (b h j) d")
                        t = TV[:, bass.ds(h % H, 1), :, :].rearrange("p h v d -> p (h v) d")
                        dve.tensor_tensor(Vst[:, c % 2, :, :, 0:HD], v.unsqueeze(2).broadcast_to([P, NJ, 8, HD]),
                                          t.unsqueeze(1).broadcast_to([P, NJ, 8, HD]), ALU.add).then_inc(v_ready, 1)
                        wait(dve, rel_done, h - 1)
                        dve.tensor_copy(RVc[0:DIST, c % 2, :],
                                        RV[0:DIST, bass.ds(h % H, 1), :].rearrange("p a d -> p (a d)")).then_inc(rv_ready, 1)
                    if s == 9 and on(-2):
                        hh = h - 2
                        dve.wait_ge(fin_psum, h)
                        o = MISC[:, 0:256].rearrange("p (a q e) -> p q a e", a=2, q=4)
                        dve.reciprocal(rden[:, :, :], o[:, :, :, HD]).then_inc(rden_ready, 1)
                        dve.wait_ge(rden_ready, h - 1)
                        dst = ON[:, 0:NB, :].rearrange("p (b j) (h d) -> p b h j d", b=B, h=H)[
                            :, bass.ds(batch_of(hh), 1), bass.ds(hh % H, 1), :, :].rearrange("p b h (q a) d -> p (b h q) a d", a=2)
                        dve.tensor_tensor(dst, o[:, :, :, 0:HD], rden[:, :, :].unsqueeze(3).broadcast_to([P, 4, 2, HD]),
                                          ALU.mult).then_inc(on_ready, 1)
                    if s in (5, 7) and on(2):
                        part = (s - 5) // 2
                        dve.wait_ge(aj_psum, 2 * h + 5 + part)
                        dve.wait_ge(ajk_copied, 2 * h + 5 + part)
                        w = aj_e[:, 4 * part:4 * part + 4, 0:DIST]
                        q6 = PS[:, 6, :].rearrange("p (a n) -> p a n", n=P)[:, :, 0:DIST]
                        dve.tensor_tensor(w, q6, w, ALU.add).then_inc(aj_copied, 1)
                    if s == 12 and on(-1):
                        dve.wait_ge(dp_psum, h)
                        wait(dve, dp_out, 16 * (h - 1))
                        dve.tensor_copy(dp_e[:, :], MISC).then_inc(dp_copied, 1)

            steps = iterations(dve, iteration)
            next(steps)
            dve.wait_ge(dq_out, 16 * (hm + 3))

            def silu(e, p, k):
                dve.wait_ge(ex_silu, e + 1)
                wait(dve, ex_y, e - 1)
                dve.tensor_tensor(EG[p], PS[0:I, 2 + p, 256:512], EH[p], ALU.mult).then_inc(ex_g, 1)

            turns(dve, QUADS, silu)
            for _ in steps:
                pass
            dve.wait_ge(y_added, 5 * NB + 1)
            for g in range(G):
                dve.wait_ge(pj_y, g + 1)
                dve.tensor_tensor(X[:, g * 4:g * 4 + 4, :], X[:, g * 4:g * 4 + 4, :],
                                  PS[:, 2 + g % 2, :].rearrange("p (a c) -> p a c", a=4), ALU.add).then_inc(pj_add, 1)


def kernel(**inputs):
    import numpy as np
    import concourse.bacc as bacc
    from concourse.bass_utils import run_bass_kernel_spmd

    a = {k.replace("L0_", ""): np.asarray(v) for k, v in inputs.items()}
    H, HD, NBK = a["attn_rpe_q_table"].shape
    C = H * HD
    E, D = a["ffn_gate_w"].shape
    I = a["ffn_w1"].shape[1]
    f32 = np.float32

    def by_distance(table, sign):
        return table[..., np.clip(sign * (np.arange(P) - (DIST // 2)), -31, 31) + 31]

    def rows_by_distance(table, sign):
        return by_distance(table, sign).reshape(C, P)

    def far(table, lower, upper):
        t = np.zeros((H, HD, 2, H), f32)
        for h in range(H):
            t[h, :, 0, h] = table[h, :, lower]
            t[h, :, 1, h] = table[h, :, upper]
        return t.reshape(C, 2 * H)

    wqkv = a["attn_w_qkv"]
    vmask = np.zeros((2, 8, P), f32)
    for v in range(8):
        for s in range(4):
            k = value_kind(v, s)
            if k is not None:
                vmask[k, v, TILE * s:TILE * s + TILE] = 1
    kc = np.zeros((9, 2, 1024), f32)
    kc[0:6, 0] = 1
    kc[0:3, 1] = 1
    kc[6:9, 1] = 1
    kc = kc[:ROW_K - ROW_M]
    arrays = {
        "x": a["attn_x"],
        "wqkvg": np.concatenate([wqkv.T, a["ffn_gate_w"].T], axis=1),
        "w_proj": a["attn_w_proj"].T,
        "b_proj": a["attn_b_proj"].reshape(1, C),
        "rk_far": far(a["attn_rpe_k_table"], 0, NBK - 1),
        "rq_far": far(a["attn_rpe_q_table"], NBK - 1, 0),
        "rk_dist": rows_by_distance(a["attn_rpe_k_table"], -1),
        "rq_dist": rows_by_distance(a["attn_rpe_q_table"], 1),
        "rv_rows": by_distance(a["attn_rpe_v_table"].transpose(0, 2, 1), -1).transpose(2, 0, 1)[:DIST],
        "rv_far": np.stack([a["attn_rpe_v_table"][:, 0].reshape(C), a["attn_rpe_v_table"][:, NBK - 1].reshape(C)]),
        "gate_b": a["ffn_gate_b"].reshape(1, E),
        "w13": np.stack([a["ffn_w1"].transpose(2, 0, 1), a["ffn_w3"].transpose(2, 0, 1)], axis=2),
        "w2": a["ffn_w2"].transpose(2, 0, 1),
        "ws1": a["ffn_ws1"].T,
        "ws3": a["ffn_ws3"].T,
        "ws2": a["ffn_ws2"].T.reshape(2, I, D),
        "ident_c": np.eye(P, dtype=f32),
        "tri_c": np.triu(np.ones((P, P), f32), 1),
        "kconst_c": kc,
        "vmask_c": vmask.reshape(2, 8 * P),
        "slot_c": (np.arange(E) * 64 + 1).astype(f32).reshape(1, E),
    }
    nc = bacc.Bacc("TRN2", target_bir_lowering=False, num_devices=1)
    args, feed = [], {}
    for name, v in arrays.items():
        v = np.ascontiguousarray(v)
        feed[f"in_{name}"] = v
        args.append(nc.dram_tensor(f"in_{name}", v.shape, mybir.dt.from_np(v.dtype), kind="ExternalInput").ap())
    out = nc.dram_tensor("out_0", a["attn_x"].shape, F32, kind="ExternalOutput").ap()
    program(nc, *args, out)
    r = run_bass_kernel_spmd(nc, [feed], core_ids=[0])
    return r.results[0]["out_0"]
```
